# Optimizing a Trainium2 kernel written in Bass

```python
import numpy as np
import jax
import jax.numpy as jnp

def _softmax(x, axis=-1):
    return jax.nn.softmax(x, axis=axis)

def _gelu(x):
    return jax.nn.gelu(x, approximate=True)

def _silu(x):
    return jax.nn.silu(x)

def _sigmoid(x):
    return jax.nn.sigmoid(x)

def _layernorm(x, axis=-1, eps=1e-05):
    m = jnp.mean(x, axis=axis, keepdims=True)
    v = jnp.var(x, axis=axis, keepdims=True)
    return (x - m) / jnp.sqrt(v + eps)

def _scatter_add(tgt, idx, src, axis=0):
    return tgt.at[idx].add(src)

def _segment_sum(src, seg, n):
    return jax.ops.segment_sum(src, seg, n)
kernel_name = 'mk_xattn_ffn_d2_seqx_r8_a2c2e6'

def setup_inputs(seed: int=0):
    np.random.seed(seed)
    _w = jnp.asarray

    def _rec_inputs():
        import jax
        import jax.numpy as jnp
        _rk = jax.random.key(seed)
        x = 7.22e-05 + 1 * jax.random.normal(jax.random.fold_in(_rk, 1), (4, 256, 128), jnp.float32)
        _lenS = 256 - jax.random.randint(jax.random.fold_in(_rk, 7), (4,), 0, max(1, 256 // 4) + 1, jnp.int32)
        _lenS2 = 256 - jax.random.randint(jax.random.fold_in(_rk, 8), (4,), 0, max(1, 256 // 4) + 1, jnp.int32)
        _ctx_1024P = jax.random.normal(jax.random.fold_in(_rk, 11), (4, 16, 128), jnp.float32)
        _ctx_1024c = jax.random.dirichlet(jax.random.fold_in(_rk, 511), 0.3 * jnp.ones((16,), jnp.float32), (4, 256))
        _ctx_1024t = jnp.einsum('bsk,bkd->bsd', _ctx_1024c, _ctx_1024P)
        _ctx_1024t = _ctx_1024t * jax.lax.rsqrt(jnp.mean(jnp.square(_ctx_1024t)) + 1e-12) * 0.953939
        ctx_1024 = 4.13588e-05 + 0.999923 * (_ctx_1024t + 0.3 * jax.random.normal(jax.random.fold_in(_rk, 611), (4, 256, 128), jnp.float32))
        _validS = jnp.arange(256)[None, :] < _lenS[:, None]
        _validS2 = jnp.arange(256)[None, :] < _lenS2[:, None]
        _causal = jnp.tril(jnp.ones((256, 256), dtype=bool))
        mask_BxSxS2_ik1 = jnp.where(jnp.broadcast_to(_validS2[:, None, :], (4, 256, 256)), 1, 0).astype(jnp.int32)
        return (x, ctx_1024, mask_BxSxS2_ik1)
    x, ctx_1024, mask_BxSxS2_ik1 = _rec_inputs()

    def _L0_xattn_setup():
        import jax, jax.numpy as jnp
        import numpy as np
        B, T, D, H = (4, 256, 128, 512)
        S = 32
        EPS = 1e-05

        def _layer_norm(x, gamma, beta):
            mu = jnp.mean(x, axis=-1, keepdims=True)
            var = jnp.mean(jnp.square(x - mu), axis=-1, keepdims=True)
            return (x - mu) * jax.lax.rsqrt(var + EPS) * gamma + beta

        def _aft_local(emb, wq, bq, wk, bk, wv, bv, wo, bo, pos_bias):
            q = emb @ wq + bq
            k = emb @ wk + bk
            v = emb @ wv + bv
            idx = jnp.arange(T)
            mask = (jnp.abs(idx[:, None] - idx[None, :]) < S).astype(pos_bias.dtype)
            w = pos_bias * mask
            max_k = jnp.max(k, axis=1, keepdims=True)
            max_w = jnp.max(w, axis=1, keepdims=True)
            ek = jnp.exp(k - max_k)
            ew = jnp.exp(w - max_w)
            num = jnp.einsum('tj,bjd->btd', ew, ek * v)
            den = jnp.einsum('tj,bjd->btd', ew, ek)
            y = jax.nn.sigmoid(q) * num / den
            return y @ wo + bo
        key = jax.random.key(seed)
        ks = jax.random.split(key, 16)
        sd = 0.02
        return {'x': jax.random.normal(ks[0], (B, T, D), jnp.float32), 'pos_encod': jax.random.normal(ks[1], (B, T, D), jnp.float32), 'wq': jax.random.normal(ks[2], (D, D), jnp.float32) * sd, 'bq': jnp.zeros((D,), jnp.float32), 'wk': jax.random.normal(ks[3], (D, D), jnp.float32) * sd, 'bk': jnp.zeros((D,), jnp.float32), 'wv': jax.random.normal(ks[4], (D, D), jnp.float32) * sd, 'bv': jnp.zeros((D,), jnp.float32), 'wo': jax.random.normal(ks[5], (D, D), jnp.float32) * sd, 'bo': jnp.zeros((D,), jnp.float32), 'pos_bias': jax.random.normal(ks[6], (T, T), jnp.float32) * sd, 'gamma': jnp.ones((D,), jnp.float32), 'beta': jnp.zeros((D,), jnp.float32), 'w1': jax.random.normal(ks[7], (D, H), jnp.float32) * sd, 'b1': jnp.zeros((H,), jnp.float32), 'w2': jax.random.normal(ks[8], (H, D), jnp.float32) * sd, 'b2': jnp.zeros((D,), jnp.float32)}
    _L0_xattn_all = _L0_xattn_setup()
    _L0_xattn_in = {k: v for k, v in _L0_xattn_all.items() if k in ('wq', 'bq', 'wk', 'bk', 'wv', 'bv', 'wo', 'bo', 'pos_bias', 'gamma', 'beta', 'w1', 'b1', 'w2', 'b2')}
    del _L0_xattn_all

    def _L0_ffn_setup():
        import jax, jax.numpy as jnp
        import numpy as np
        HIDDEN = 128
        INNER = 512

        def _weight_quant(w):
            scale = 1.0 / jnp.clip(jnp.mean(jnp.abs(w)), 1e-05)
            wq = jnp.clip(jnp.round(w * scale), -1.0, 1.0) / scale
            return w + jax.lax.stop_gradient(wq - w)

        def _act_quant(x):
            scale = 127.0 / jnp.clip(jnp.max(jnp.abs(x), axis=-1, keepdims=True), 1e-05)
            xq = jnp.clip(jnp.round(x * scale), -128.0, 127.0) / scale
            return x + jax.lax.stop_gradient(xq - x)

        def _bitlinear(x, w):
            return jnp.einsum('bsi,oi->bso', _act_quant(x), _weight_quant(w))
        key = jax.random.key(seed)
        k0, k1, k2, k3 = jax.random.split(key, 4)
        x = jax.random.normal(k0, (4, 256, HIDDEN), dtype=jnp.float32)
        w_gate = jax.random.normal(k1, (INNER, HIDDEN), dtype=jnp.float32) / np.sqrt(HIDDEN)
        w_up = jax.random.normal(k2, (INNER, HIDDEN), dtype=jnp.float32) / np.sqrt(HIDDEN)
        w_down = jax.random.normal(k3, (HIDDEN, INNER), dtype=jnp.float32) / np.sqrt(INNER)
        return {'x': x, 'w_gate': w_gate, 'w_up': w_up, 'w_down': w_down}
    _L0_ffn_all = _L0_ffn_setup()
    _L0_ffn_in = {k: v for k, v in _L0_ffn_all.items() if k in ('w_gate', 'w_up', 'w_down')}
    del _L0_ffn_all

    def _L1_xattn_setup():
        import jax, jax.numpy as jnp
        import numpy as np
        B, S, D, H = (2, 256, 128, 16)
        DK = D // H

        def _split_heads(x):
            b, s, _ = x.shape
            return x.reshape(b, s, H, DK).transpose(0, 2, 1, 3)
        key = jax.random.key(seed)
        ks = jax.random.split(key, 13)
        scale = 1.0 / np.sqrt(D)
        return {'query': jax.random.normal(ks[0], (B, S, D), jnp.float32), 'key': jax.random.normal(ks[1], (B, S, D), jnp.float32), 'value': jax.random.normal(ks[2], (B, S, D), jnp.float32), 'mask': jax.random.randint(ks[3], (B, S, S), 0, 2, jnp.int32), 'Wq': jax.random.normal(ks[4], (D, D), jnp.float32) * scale, 'bq': jnp.zeros((D,), jnp.float32), 'Wk': jax.random.normal(ks[5], (D, D), jnp.float32) * scale, 'bk': jnp.zeros((D,), jnp.float32), 'Wv': jax.random.normal(ks[6], (D, D), jnp.float32) * scale, 'bv': jnp.zeros((D,), jnp.float32), 'Wo': jax.random.normal(ks[7], (D, D), jnp.float32) * scale, 'bo': jnp.zeros((D,), jnp.float32)}
    _L1_xattn_all = _L1_xattn_setup()
    _L1_xattn_in = {k: v for k, v in _L1_xattn_all.items() if k in ('Wq', 'bq', 'Wk', 'bk', 'Wv', 'bv', 'Wo', 'bo')}
    del _L1_xattn_all

    def _L1_ffn_setup():
        import jax, jax.numpy as jnp
        import numpy as np
        B, T, E, C, H, G = (2, 256, 8, 128, 256, 16)
        key = jax.random.key(seed)
        ks = jax.random.split(key, 7)
        return {'hidden_states': jax.random.normal(ks[0], (B, T, C), jnp.float32), 'w_red': jax.random.normal(ks[1], (C, G), jnp.float32) * 0.02, 'wg': jax.random.normal(ks[2], (E, G), jnp.float32), 'W1': jax.random.normal(ks[3], (E, C, H), jnp.float32) * 0.02, 'b1': jax.random.normal(ks[4], (E, H), jnp.float32) * 0.02, 'W2': jax.random.normal(ks[5], (E, H, C), jnp.float32) * 0.02, 'b2': jax.random.normal(ks[6], (E, C), jnp.float32) * 0.02}
    _L1_ffn_all = _L1_ffn_setup()
    _L1_ffn_in = {k: v for k, v in _L1_ffn_all.items() if k in ('w_red', 'wg', 'W1', 'b1', 'W2', 'b2')}
    del _L1_ffn_all
    return {'x': x, 'ctx_1024': ctx_1024, 'mask_BxSxS2_ik1': mask_BxSxS2_ik1, 'L0_xattn_wq': _L0_xattn_in['wq'], 'L0_xattn_bq': _L0_xattn_in['bq'], 'L0_xattn_wk': _L0_xattn_in['wk'], 'L0_xattn_bk': _L0_xattn_in['bk'], 'L0_xattn_wv': _L0_xattn_in['wv'], 'L0_xattn_bv': _L0_xattn_in['bv'], 'L0_xattn_wo': _L0_xattn_in['wo'], 'L0_xattn_bo': _L0_xattn_in['bo'], 'L0_xattn_pos_bias': _L0_xattn_in['pos_bias'], 'L0_xattn_gamma': _L0_xattn_in['gamma'], 'L0_xattn_beta': _L0_xattn_in['beta'], 'L0_xattn_w1': _L0_xattn_in['w1'], 'L0_xattn_b1': _L0_xattn_in['b1'], 'L0_xattn_w2': _L0_xattn_in['w2'], 'L0_xattn_b2': _L0_xattn_in['b2'], 'L0_ffn_w_gate': _L0_ffn_in['w_gate'], 'L0_ffn_w_up': _L0_ffn_in['w_up'], 'L0_ffn_w_down': _L0_ffn_in['w_down'], 'L1_xattn_Wq': _L1_xattn_in['Wq'], 'L1_xattn_bq': _L1_xattn_in['bq'], 'L1_xattn_Wk': _L1_xattn_in['Wk'], 'L1_xattn_bk': _L1_xattn_in['bk'], 'L1_xattn_Wv': _L1_xattn_in['Wv'], 'L1_xattn_bv': _L1_xattn_in['bv'], 'L1_xattn_Wo': _L1_xattn_in['Wo'], 'L1_xattn_bo': _L1_xattn_in['bo'], 'L1_ffn_w_red': _L1_ffn_in['w_red'], 'L1_ffn_wg': _L1_ffn_in['wg'], 'L1_ffn_W1': _L1_ffn_in['W1'], 'L1_ffn_b1': _L1_ffn_in['b1'], 'L1_ffn_W2': _L1_ffn_in['W2'], 'L1_ffn_b2': _L1_ffn_in['b2']}

def reference(x, ctx_1024, mask_BxSxS2_ik1, L0_xattn_wq, L0_xattn_bq, L0_xattn_wk, L0_xattn_bk, L0_xattn_wv, L0_xattn_bv, L0_xattn_wo, L0_xattn_bo, L0_xattn_pos_bias, L0_xattn_gamma, L0_xattn_beta, L0_xattn_w1, L0_xattn_b1, L0_xattn_w2, L0_xattn_b2, L0_ffn_w_gate, L0_ffn_w_up, L0_ffn_w_down, L1_xattn_Wq, L1_xattn_bq, L1_xattn_Wk, L1_xattn_bk, L1_xattn_Wv, L1_xattn_bv, L1_xattn_Wo, L1_xattn_bo, L1_ffn_w_red, L1_ffn_wg, L1_ffn_W1, L1_ffn_b1, L1_ffn_W2, L1_ffn_b2):
    import jax
    import jax.numpy as jnp

    def _L0_xattn_ref(x, pos_encod, wq, bq, wk, bk, wv, bv, wo, bo, pos_bias, gamma, beta, w1, b1, w2, b2):
        import jax, jax.numpy as jnp
        import numpy as np
        B, T, D, H = (4, 256, 128, 512)
        S = 32
        EPS = 1e-05

        def _layer_norm(x, gamma, beta):
            mu = jnp.mean(x, axis=-1, keepdims=True)
            var = jnp.mean(jnp.square(x - mu), axis=-1, keepdims=True)
            return (x - mu) * jax.lax.rsqrt(var + EPS) * gamma + beta

        def _aft_local(emb, wq, bq, wk, bk, wv, bv, wo, bo, pos_bias):
            q = emb @ wq + bq
            k = emb @ wk + bk
            v = emb @ wv + bv
            idx = jnp.arange(T)
            mask = (jnp.abs(idx[:, None] - idx[None, :]) < S).astype(pos_bias.dtype)
            w = pos_bias * mask
            max_k = jnp.max(k, axis=1, keepdims=True)
            max_w = jnp.max(w, axis=1, keepdims=True)
            ek = jnp.exp(k - max_k)
            ew = jnp.exp(w - max_w)
            num = jnp.einsum('tj,bjd->btd', ew, ek * v)
            den = jnp.einsum('tj,bjd->btd', ew, ek)
            y = jax.nn.sigmoid(q) * num / den
            return y @ wo + bo
        emb = x + pos_encod
        attn = _aft_local(emb, wq, bq, wk, bk, wv, bv, wo, bo, pos_bias)
        a = _layer_norm(attn + emb, gamma, beta)
        ff = jax.nn.relu(a @ w1 + b1) @ w2 + b2
        return _layer_norm(ff + a, gamma, beta)

    def _L0_ffn_ref(x, w_gate, w_up, w_down):
        import jax, jax.numpy as jnp
        import numpy as np
        HIDDEN = 128
        INNER = 512

        def _weight_quant(w):
            scale = 1.0 / jnp.clip(jnp.mean(jnp.abs(w)), 1e-05)
            wq = jnp.clip(jnp.round(w * scale), -1.0, 1.0) / scale
            return w + jax.lax.stop_gradient(wq - w)

        def _act_quant(x):
            scale = 127.0 / jnp.clip(jnp.max(jnp.abs(x), axis=-1, keepdims=True), 1e-05)
            xq = jnp.clip(jnp.round(x * scale), -128.0, 127.0) / scale
            return x + jax.lax.stop_gradient(xq - x)

        def _bitlinear(x, w):
            return jnp.einsum('bsi,oi->bso', _act_quant(x), _weight_quant(w))
        gate = jax.nn.silu(_bitlinear(x, w_gate))
        up = _bitlinear(x, w_up)
        return _bitlinear(gate * up, w_down)

    def _L1_xattn_ref(query, key, value, mask, Wq, bq, Wk, bk, Wv, bv, Wo, bo):
        import jax, jax.numpy as jnp
        import numpy as np
        B, S, D, H = (2, 256, 128, 16)
        DK = D // H

        def _split_heads(x):
            b, s, _ = x.shape
            return x.reshape(b, s, H, DK).transpose(0, 2, 1, 3)
        q = _split_heads(query @ Wq + bq)
        k = _split_heads(key @ Wk + bk)
        v = _split_heads(value @ Wv + bv)
        scores = jnp.einsum('bhqd,bhkd->bhqk', q, k) / jnp.sqrt(jnp.float32(DK))
        scores = jnp.where(mask[:, None, :, :] == 0, jnp.float32(-1000000000.0), scores)
        p_attn = jax.nn.softmax(scores, axis=-1)
        x = jnp.einsum('bhqk,bhkd->bhqd', p_attn, v)
        x = x.transpose(0, 2, 1, 3).reshape(query.shape[0], -1, D)
        return x @ Wo + bo

    def _L1_ffn_ref(hidden_states, w_red, wg, W1, b1, W2, b2):
        import jax, jax.numpy as jnp
        import numpy as np
        B, T, E, C, H, G = (2, 256, 8, 128, 256, 16)
        b, t, c = hidden_states.shape
        x = hidden_states.reshape(-1, c)
        x_red = x @ w_red
        wg_n = wg / jnp.maximum(jnp.linalg.norm(wg, axis=1, keepdims=True), 0.0001)
        logits = x_red @ wg_n.T
        gates = jax.nn.softmax(logits, axis=1)
        scores = jnp.max(gates, axis=1)
        idx = jnp.argmax(gates, axis=1)
        h = jnp.einsum('nc,ech->neh', x, W1) + b1[None]
        h = jnp.take_along_axis(h, idx[:, None, None], axis=1)[:, 0, :]
        h = jax.nn.gelu(h, approximate=False)
        o = jnp.einsum('nh,ehc->nec', h, W2) + b2[None]
        o = jnp.take_along_axis(o, idx[:, None, None], axis=1)[:, 0, :]
        o = o * scores[:, None]
        return o.reshape(b, t, c)
    x = x + _L0_xattn_ref(_layernorm(x, axis=-1), ctx_1024, L0_xattn_wq, L0_xattn_bq, L0_xattn_wk, L0_xattn_bk, L0_xattn_wv, L0_xattn_bv, L0_xattn_wo, L0_xattn_bo, L0_xattn_pos_bias, L0_xattn_gamma, L0_xattn_beta, L0_xattn_w1, L0_xattn_b1, L0_xattn_w2, L0_xattn_b2)
    x = x + _L0_ffn_ref(_layernorm(x, axis=-1), L0_ffn_w_gate, L0_ffn_w_up, L0_ffn_w_down)
    x = x + _L1_xattn_ref(_layernorm(x, axis=-1), ctx_1024, ctx_1024, mask_BxSxS2_ik1, L1_xattn_Wq, L1_xattn_bq, L1_xattn_Wk, L1_xattn_bk, L1_xattn_Wv, L1_xattn_bv, L1_xattn_Wo, L1_xattn_bo)
    x = x + _L1_ffn_ref(_layernorm(x, axis=-1), L1_ffn_w_red, L1_ffn_wg, L1_ffn_W1, L1_ffn_b1, L1_ffn_W2, L1_ffn_b2)
    return x

_drawn_inputs = setup_inputs


def setup_inputs(seed=0):
    import zlib

    import numpy as np

    out = dict(_drawn_inputs(seed))
    spreads = {'L0_xattn_bq': (0.0, 0.8),
     'L0_xattn_bk': (0.0, 0.8),
     'L0_xattn_bv': (0.0, 0.8),
     'L0_xattn_bo': (0.0, 0.1),
     'L0_xattn_gamma': (1.0, 0.2),
     'L0_xattn_beta': (0.0, 0.1),
     'L0_xattn_b1': (0.0, 0.567),
     'L0_xattn_b2': (0.0, 0.1),
     'L1_xattn_bq': (0.0, 0.685),
     'L1_xattn_bk': (0.0, 0.8),
     'L1_xattn_bv': (0.0, 0.1),
     'L1_xattn_bo': (0.0, 0.1)}
    factors = {'L0_xattn_wq': 8.0,
     'L0_xattn_wk': 8.0,
     'L0_xattn_wv': 8.0,
     'L0_xattn_wo': 8.0,
     'L0_xattn_pos_bias': 8.0,
     'L1_ffn_w_red': 8.0,
     'L1_ffn_wg': 8.0,
     'L1_ffn_W1': 8.0,
     'L1_ffn_b1': 8.0,
     'L1_ffn_W2': 8.0,
     'L1_ffn_b2': 8.0}
    for name, (base, spread) in spreads.items():
        noise = np.random.default_rng([zlib.crc32(name.encode()), seed]).standard_normal(out[name].shape)
        drawn = base * np.exp(spread * noise) if base else spread * noise
        out[name] = jnp.asarray(drawn.astype(out[name].dtype))
    for name, factor in factors.items():
        out[name] = (out[name] * factor).astype(out[name].dtype)
    return out
```

```python
from contextlib import ExitStack

import concourse.bass as bass
import numpy as np
from concourse import mybir

F32, F16, BF16 = mybir.dt.float32, mybir.dt.float16, mybir.dt.bfloat16
I32, U32 = mybir.dt.int32, mybir.dt.uint32
ACT = mybir.ActivationFunctionType
ALU = mybir.AluOpType
AX = mybir.AxisListType

P = 128
B, T, D = 4, 256, 128
TILES = T // P
WINDOW = 32
HID = 512
HC = HID // P
NH, DK = 16, 8
PRING = 8
KRING = 4
QUADS = NH // 4
NE, EH, NG = 8, 256, 16
EC = EH // P
EPS = 1e-5
MAGIC = 12582912.0
BIG = 61440.0
PASSES = ((0, 0), (0, 1), (1, 0))

SEGS = [("qkv", 3 * D), ("wo", D), ("w1", HID), ("w2", HID), ("wk", QUADS * P), ("wv", D), ("wq", QUADS * P),
        ("wo1", D), ("m1", NE * EH), ("m2", EC * NE * D)]
SEG = {}
NW = 0
for _name, _n in SEGS:
    SEG[_name] = (NW, NW + _n)
    NW += _n
BSEGS = [("qkv", 3 * D), ("bo", D), ("b1", HID), ("b2", D), ("bq", QUADS * P), ("bk", QUADS * P), ("bv", D), ("bo1", D)]
BSEG = {}
NB = 0
for _name, _n in BSEGS:
    BSEG[_name] = (NB, NB + _n)
    NB += _n
CSEGS = [("ident", P), ("iota", 2 * NE), ("lo_q", 1), ("lo_k", 1), ("lo_2", 1), ("lo_16", 1), ("sel", P),
         ("band", 2 * T), ("cols", 3), ("wredT", P), ("wgT", NE)]
CSEG = {}
NC_ = 0
for _name, _n in CSEGS:
    CSEG[_name] = (NC_, NC_ + _n)
    NC_ += _n

LN_IN, LN_A, LN_OUT, LN_FFN, LN_ATT, LN_MOE = range(6)
NLN = 6
R_IN, R_A, R_FFN, R_ATT, R_MOE = range(5)
T_EMB, T_Y, T_A, T_QUANT, T_QUERY, T_ATTN, T_MOE = range(7)
C_EMB, C_Y, C_A, C_QUERY, C_ATTN, C_MOE = range(6)


def nth(stage, b):
    return stage * B + b + 1


SIGNALS = """
l_x0 l_x1 l_x2 l_x3 l_ctx l_cst l_pos l_gb l_bias l_mbias l_ctxT l_mask l_ffw l_out l_qkv l_wo l_w1 l_w2 l_wk
l_wv l_wq l_wo1 l_m1 l_m2 ones_ready id_ready bias_hi bias_ready mbias_hi mbias_ready zeros_ready w_hi w_lo
w_lo_pool absum means_ready meanc ffscale ffw_r ffw_c ffw_ready kscale pos_masked pos_max ew_done ewT_mm ewT_hi
ewT_ready wgsq router_mm wg_root router_ready mask_ind count_mm colmask resmask flagsum flag_ready ctxT_hi
ctxT_ready kproj ka_hi ka_ready vproj va_ready kz_zero kz_ready emb kT_mm kmax kmaxb kdiag kshift ek ekv eb_hi eb_lo numden rden
ysig y attn_mm aT_32 hid_mm hid_hi hid_ready ff_mm xb nb x1 amax amaxc ainv ascale q1 q1T_ready gscale gu_mm
tanhg g1 g q2 q2T_mm q2T_ready down_mm x2 q_mm qa_hi qa_ready s_mm smax spread shift_mm qb st_mm probs pv oT
oR_mm oden attn wo1_mm x3 logit_mm top8 topix onehot expsum score wsel ohT_mm ohT oh_mm oh xm_hi xm moe_h
gelu gelu_hi gelu_ready moe_o picked picksum y0 y_out turned cols_hi cols_ready ln_moments ln_vareps ln_rstd
ln_stats rows_ready router_step
""".split()


def build_program(nc, x, ctx_rows, ctx_cols, mask, consts, pos, gamma, beta, bias, mbias, ffw, weights, out):
    scope = ExitStack()
    with scope:
        def sb(name, shape, dt=F32):
            return scope.enter_context(nc.sbuf_tensor(name, shape, dt))

        sig = {n: scope.enter_context(nc.semaphore(n)) for n in SIGNALS}
        ps = scope.enter_context(nc.psum_tensor("ps", [P, 8, 512], F32))

        x_in = sb("x_in", [P, B, TILES, D])
        ctx_in = sb("ctx_in", [P, B, TILES, D])
        cst = sb("cst", [P, NC_])
        gamma_b = sb("gamma_b", [P, D])
        beta_b = sb("beta_b", [P, D])
        bias16 = sb("bias16", [2, NB], F16)
        mbias16 = sb("mbias16", [2 * NE, EH + D], F16)
        wf = sb("wf", [P, HID + SEG["m1"][0]])
        stage = sb("stage", [P, NE * EH])
        mask_in = wf[:, 0:B * TILES * T].bitcast(I32).rearrange("p (b t n) -> p b t n", b=B, t=TILES)
        w16 = sb("w16", [P, 2, NW], F16)
        ffw16 = sb("ffw16", [P, 3, HID], F16)
        ident = cst[:, CSEG["ident"][0]:CSEG["ident"][1]]
        id16 = sb("id16", [P, P], F16)
        idbig = sb("idbig", [P, P], BF16)
        sel16 = sb("sel16", [1, P], F16)
        ones32 = sb("ones32", [P, P])
        ones16 = sb("ones16", [P, T], F16)
        halfs = sb("halfs", [P, 2 * NE])
        roots = sb("roots", [P, NE])

        def c(name, rows=P):
            a, b_ = CSEG[name]
            return cst[0:rows, a:b_]

        def wf32(name):
            a, b_ = SEG[name]
            return stage[:, :] if name in ("m1", "m2") else wf[:, HID + a:HID + b_]

        def w(name, part):
            a, b_ = SEG[name]
            return w16[:, part, a:b_]

        def brow(name):
            a, b_ = BSEG[name]
            return bias16[:, a:b_]

        bk_col = c("cols")[:, 0:1]
        gamma_col = c("cols")[:, 1:2]
        beta_col = c("cols")[:, 2:3]

        gate_pt = sb("gate_pt", [P, 12 * TILES * T])
        hid_xm = sb("hid_xm", [P, 2 * B * HC * T], F16)
        eb_oT = sb("eb_oT", [P, B * QUADS * T])
        half_b = sb("half_b", [P, B * QUADS * T], F16)
        half_c = sb("half_c", [P, B * QUADS * T], F16)
        def taken(buf, start, n, rows=P):
            return buf[0:rows, start:start + n]

        at = 0
        bias_in = taken(gate_pt, 0, NB, 2)
        at += NB
        bias_h = taken(gate_pt, at, NB // 2, 2).bitcast(F16)
        at += NB // 2
        mbias_in = taken(gate_pt, at, EH + D, 2 * NE)
        at += EH + D
        mbias_h = taken(gate_pt, at, (EH + D) // 2, 2 * NE).bitcast(F16)
        at += (EH + D) // 2
        junk = taken(gate_pt, at, HID)
        at += HID
        ctxT_in = taken(gate_pt, at, B * T).rearrange("p (b n) -> p b n", b=B)
        at += B * T
        gelu32 = taken(gate_pt, 0, B * EC * T).rearrange("p (b c n) -> p b c n", b=B, c=EC)
        picked = taken(gate_pt, B * EC * T, 2 * NE * D).rearrange("p (k e n) -> p k e n", k=2, e=NE)

        absum = sb("absum", [P, 3])
        mean = sb("mean", [P, 3])
        wscale = sb("wscale", [P, 3])
        kfac = sb("kfac", [P, 3])
        posmax = sb("posmax", [P, TILES])
        ewT = sb("ewT", [P, 2, TILES, T], F16)
        wgsq = sb("wgsq", [NG, NE])
        wnorm = sb("wnorm", [P, 3, NE])
        router = sb("router", [P, NE])
        router16 = sb("router16", [P, 2, NE], F16)
        colrow = sb("colrow", [1, B, T], F16)
        flag_f = sb("flag_f", [1, 1])
        flag_i = sb("flag_i", [1, 1], I32)
        ka = sb("ka", [P, B, QUADS, T], F16)

        stats = sb("stats", [P, NLN, B, TILES, 6])
        moments = sb("moments", [P, NLN, B, TILES, 2])
        vareps = sb("vareps", [P, NLN, B, TILES])
        rstd = sb("rstd", [P, NLN, B, TILES])
        rows = sb("rows", [P, B, TILES, D])
        emb = sb("emb", [P, B, TILES, D])
        colsA = sb("colsA", [P, 2, B, T], F16)
        y_mem = sb("y_mem", [P, B * T])
        posw = y_mem[:, 0:TILES * T].rearrange("p (t n) -> p t n", t=TILES)
        ew = y_mem[:, TILES * T:2 * TILES * T].rearrange("p (t n) -> p t n", t=TILES)
        colsY = y_mem[:, :].bitcast(F16).rearrange("p (a b n) -> p a b n", a=2, b=B)
        ctxT = colsY
        n_mem = sb("n_mem", [P, 2 * B * T])
        ffw_in = n_mem[:, 0:3 * HID].rearrange("p (k n) -> p k n", k=3)
        colsN = n_mem[:, 0:B * T].bitcast(F16).rearrange("p (a b n) -> p a b n", a=2, b=B)
        a32 = n_mem[:, B * T:2 * B * T].rearrange("p (b n) -> p b n", b=B)
        kmx = sb("kmx", [P, B, 2])
        th = sb("th", [P, B, TILES, D])
        half = B * TILES * 2 * D
        eb = eb_oT[:, 0:half].rearrange("p (b t n) -> p b t n", b=B, t=TILES)
        g1 = eb_oT[:, half:2 * half].rearrange("p (b n) -> p b n", b=B)
        oT = eb_oT[:, :].rearrange("p (b q n) -> p b q n", b=B, q=QUADS)
        g = gate_pt[:, 0:B * TILES * HID].rearrange("p (b t n) -> p b t n", b=B, t=TILES)
        thg = gate_pt[:, B * TILES * HID:].rearrange("p (b n) -> p b n", b=B)
        pt = taken(gate_pt, 0, PRING * TILES * T).rearrange("p (k t n) -> p k t n", k=PRING, t=TILES)
        hid16 = hid_xm[:, :].rearrange("p (a b c n) -> p a b c n", a=2, b=B, c=HC)
        va = hid_xm[:, :].bitcast(F32).rearrange("p (b t h k) -> p b t h k", b=B, t=TILES, h=NH)
        eb16 = hid_xm[:, 0:2 * half].rearrange("p (a b t n) -> p a b t n", a=2, b=B, t=TILES)
        qh = eb_oT[:, 0:half].bitcast(F16).rearrange("p (b h n) -> p b h n", b=B, h=QUADS)
        ind = eb_oT[:, half:half + B * T].bitcast(BF16).rearrange("p (b t n) -> p b t n", b=B, t=TILES)
        colmask = eb_oT[:, half + B * T:half + B * T + B * T // 2].bitcast(BF16).rearrange("p (b n) -> p b n", b=B)
        resmask = wf[:, B * TILES * T:B * TILES * T + B * T].bitcast(BF16).rearrange("p (b t n) -> p b t n", b=B, t=TILES)
        gT = half_b[:, :].rearrange("p (b t c n) -> p b t c n", b=B, t=TILES, c=HC)
        kh = half_b[:, :].rearrange("p (b h n) -> p b h n", b=B, h=QUADS)
        oh = half_b[:, :].rearrange("p (a e n) -> p a e n", a=2, e=NE)
        qa = half_c[:, :].rearrange("p (b h n) -> p b h n", b=B, h=QUADS)
        gelu16 = half_c[:, :].rearrange("p (a b c n) -> p a b c n", a=2, b=B, c=EC)
        xm = hid_xm[:, :].rearrange("p (a b e n) -> p a b e n", a=2, b=2, e=NE)
        rden = sb("rden", [P, B, TILES, D])
        y = sb("y", [P, B, TILES, D])
        xb, x1, x2 = x_in, emb, y
        attn, y0, x3, nb, res = th, rden, xb, ctx_in, ctx_in
        flag_junk = a32[0:1, :, :].rearrange("p b n -> p (b n)")
        amax = sb("amax", [P, B, 4, TILES])
        fac = sb("fac", [P, B, 3, TILES])
        qd_mem = sb("qd_mem", [P, B * P])
        kdiag = qd_mem[:, :].rearrange("p (b n) -> p b n", b=B)
        qT = qd_mem[:, :].bitcast(F16).rearrange("p (b n) -> p b n", b=B)
        kz = taken(gate_pt, PRING * TILES * T, KRING * 4 * T // 2).bitcast(F16).rearrange(
            "p (r h n) -> p r h n", r=KRING, h=4)
        mx = sb("mx", [P, B, NH, TILES])
        spread = sb("spread", [P, 2, TILES, P], F16)
        qb = sb("qb", [P, 2, T], F16)
        oden = sb("oden", [P, B, TILES, NH])
        top8 = sb("top8", [P, B, TILES, 8])
        topix = sb("topix", [P, B, TILES, 8], U32)
        ntop = sb("ntop", [P, B, TILES])
        onehot = sb("onehot", [P, B, TILES, 2 * NE], F16)
        ejunk = sb("ejunk", [P, B, TILES, NE])
        esum = sb("esum", [P, B, TILES])
        score = sb("score", [P, B, TILES])
        wsel = sb("wsel", [P, B, TILES, NE])
        ohT = sb("ohT", [2 * NE, B, T], F16)
        picksum = sb("picksum", [P, 2, D])

        def bank(b, k):
            return ps[:, 2 * b + k, :]

        def score_bank(u):
            return ps[:, (0, 1, 7)[u % 3], :]

        def pair(b):
            return ps[:, 2 * b:2 * b + 2, :]

        block = scope.enter_context(nc.Block())

        @block.sync
        def _(sp):
            sp.dma_start(x_in[:, 0], x[0]).then_inc(sig["l_x0"], 16)
            sp.dma_start(cst[:, :], consts).then_inc(sig["l_cst"], 16)
            sp.dma_start(x_in[:, 1], x[1]).then_inc(sig["l_x1"], 16)
            sp.dma_start(ctx_in[:, :, :, :], ctx_rows).then_inc(sig["l_ctx"], 16)
            sp.dma_start(x_in[:, 2], x[2]).then_inc(sig["l_x2"], 16)
            sp.dma_start(x_in[:, 3], x[3]).then_inc(sig["l_x3"], 16)
            for name in ("qkv", "wo"):
                a, z = SEG[name]
                sp.dma_start(wf32(name), weights[:, a:z]).then_inc(sig["l_" + name], 16)
            sp.dma_start(posw[:, :, :], pos).then_inc(sig["l_pos"], 16)
            sp.dma_start(ffw_in[:, :, :], ffw).then_inc(sig["l_ffw"], 16)
            sp.dma_start(ctxT_in, ctx_cols).then_inc(sig["l_ctxT"], 16)
            for name in ("wk", "wv"):
                a, z = SEG[name]
                sp.dma_start(wf32(name), weights[:, a:z]).then_inc(sig["l_" + name], 16)
            for name in ("w1", "w2", "wq", "wo1", "m1"):
                a, z = SEG[name]
                sp.dma_start(wf32(name), weights[:, a:z]).then_inc(sig["l_" + name], 16)
            sp.wait_ge(sig["w_lo"], 5)
            sp.dma_start(mask_in, mask).then_inc(sig["l_mask"], 16)
            sp.wait_ge(sig["w_lo_pool"], 3)
            sp.dma_start(wf32("m2"), weights[:, SEG["m2"][0]:SEG["m2"][1]]).then_inc(sig["l_m2"], 16)
            for b in range(B):
                sp.wait_ge(sig["y_out"], B * (TILES - 1) + b + 1)
                sp.dma_start(out[b], res[:, b]).then_inc(sig["l_out"], 16)
            sp.wait_ge(sig["l_out"], 16 * B)

        @block.gpsimd
        def _(pool):
            nc.gpsimd.memset(ones32[:, :], 1.0)
            nc.gpsimd.memset(ones16[:, :], 1.0)
            nc.gpsimd.memset(halfs[:, :], -0.5)
            nc.gpsimd.memset(roots[:, :], 0.5).then_inc(sig["ones_ready"], 1)
            pool.wait_ge(sig["ones_ready"], 1)

            def rstd_of(ln, b):
                pool.wait_ge(sig["ln_moments"], nth(ln, b))
                nc.gpsimd.tensor_scalar(vareps[:, ln, b, :], moments[:, ln, b, :, 1], EPS, 1.0, ALU.add,
                                        ALU.mult).then_inc(sig["ln_vareps"], 1)
                pool.wait_ge(sig["ln_vareps"], nth(ln, b))
                nc.gpsimd.tensor_tensor(rstd[:, ln, b, :], vareps[:, ln, b, :], halfs[:, 0:TILES],
                                        ALU.pow).then_inc(sig["ln_rstd"], 1)

            for b in range(B):
                rstd_of(LN_IN, b)
            pool.wait_ge(sig["l_ctx"], 16)
            for b in range(B):
                pool.wait_ge(sig["rows_ready"], nth(R_IN, b))
                nc.gpsimd.tensor_tensor(emb[:, b], rows[:, b], ctx_in[:, b], ALU.add).then_inc(sig["emb"], 1)
            pool.wait_ge(sig["l_pos"], 16)
            pool.wait_ge(sig["l_cst"], 16)
            nc.gpsimd.tensor_tensor(posw[:, :, :], posw[:, :, :], c("band").rearrange("p (a n) -> p a n", a=TILES),
                                    ALU.mult).then_inc(sig["pos_masked"], 1)
            pool.wait_ge(sig["l_gb"], 32)
            pool.wait_ge(sig["rows_ready"], nth(R_IN, B - 1))
            for b in range(B):
                for t in range(TILES):
                    ins = nc.gpsimd.tensor_tensor(xb[:, b, t], x_in[:, b, t], beta_b[:, :], ALU.add)
                ins.then_inc(sig["xb"], 1)
            for b in range(B):
                rstd_of(LN_A, b)

            def split_lo(name, n):
                a, z = SEG[name]
                pool.wait_ge(sig["w_hi"], n)
                nc.gpsimd.tensor_tensor(w16[:, 1, a:z], wf32(name), w16[:, 0, a:z], ALU.subtract)\
                    .then_inc(sig["w_lo_pool"], 1)

            split_lo("wq", 7)
            split_lo("wo1", 8)
            for b in range(B):
                rstd_of(LN_OUT, b)
            for b in range(B):
                rstd_of(LN_FFN, b)
            pool.wait_ge(sig["ff_mm"], B)
            nc.gpsimd.memset(va[:, :, :, :, DK:32], 0.0)
            nc.gpsimd.memset(spread[:, :, :, :], 0.0).then_inc(sig["zeros_ready"], 1)
            pool.wait_ge(sig["zeros_ready"], 1)
            nc.gpsimd.memset(va[:, :, :, :, DK:DK + 1], 1.0).then_inc(sig["zeros_ready"], 1)
            split_lo("m1", 9)
            for b in range(B):
                pool.wait_ge(sig["ascale"], nth(1, b))
                for t in range(TILES):
                    ins = nc.gpsimd.tensor_scalar(g[:, b, t], g[:, b, t], amax[:, b, 3, t:t + 1], MAGIC, ALU.mult, ALU.add)
                ins.then_inc(sig["q2"], 1)
            for b in range(B):
                rstd_of(LN_ATT, b)
            pool.wait_ge(sig["router_step"], 1)
            nc.gpsimd.tensor_tensor(wnorm[:, 1], wnorm[:, 0], roots[:, :], ALU.pow).then_inc(sig["wg_root"], 1)
            split_lo("m2", 10)
            nc.gpsimd.memset(kz[:, :, :, :], 0.0).then_inc(sig["kz_zero"], 1)
            pool.wait_ge(sig["kz_zero"], 1)
            for n in range(B * QUADS):
                b, quad = divmod(n, QUADS)
                pool.wait_ge(sig["ka_ready"], b + 1)
                if n >= KRING:
                    pool.wait_ge(sig["st_mm"], 4 * (n - KRING + 1))
                for k in range(4):
                    part = slice(32 * k, 32 * k + 32)
                    ins = nc.gpsimd.tensor_scalar(kz[part, n % KRING, k], ka[part, b, quad], 1.0, 0.0, ALU.mult, ALU.add)
                ins.then_inc(sig["kz_ready"], 1)
            for b in range(B):
                rstd_of(LN_MOE, b)

        @block.scalar
        def _(act):
            nc_act = nc.scalar.activation
            act.dma_start(gamma_b[:, :], gamma.partition_broadcast(P)).then_inc(sig["l_gb"], 16)
            act.dma_start(beta_b[:, :], beta.partition_broadcast(P)).then_inc(sig["l_gb"], 16)
            act.dma_start(bias_in[:, :], bias).then_inc(sig["l_bias"], 16)
            act.dma_start(mbias_in[:, :], mbias).then_inc(sig["l_mbias"], 16)

            def split_hi(name):
                a, z = SEG[name]
                act.wait_ge(sig["l_" + name], 16)
                nc_act(w16[:, 0, a:z], wf32(name), ACT.Copy).then_inc(sig["w_hi"], 1)

            split_hi("qkv")
            act.wait_ge(sig["l_bias"], 16)
            nc_act(bias_h[:, :], bias_in[:, :], ACT.Copy).then_inc(sig["bias_hi"], 1)
            act.wait_ge(sig["l_mbias"], 16)
            nc_act(mbias_h[:, :], mbias_in[:, :], ACT.Copy).then_inc(sig["mbias_hi"], 1)
            for b in range(B):
                act.wait_ge(sig["turned"], nth(T_EMB, b))
                nc_act(colsA[:, 0, b], bank(b, 0)[:, 0:T], ACT.Copy).then_inc(sig["cols_hi"], 1)
            split_hi("wo")
            act.wait_ge(sig["l_ffw"], 16)
            for k in range(3):
                if k:
                    act.wait_ge(sig["absum"], k)
                nc_act(junk[:, :], ffw_in[:, k], ACT.Abs, accum_out=absum[:, k:k + 1]).then_inc(sig["absum"], 1)
            act.wait_ge(sig["pos_max"], 1)
            for t in range(TILES):
                nc_act(ew[:, t], posw[:, t], ACT.Exp, bias=posmax[:, t:t + 1]).then_inc(sig["ew_done"], 1)
            for b in range(B):
                act.wait_ge(sig["kshift"], b + 1)
                qk = bank(b, 0).rearrange("p (t n) -> p t n", t=TILES)
                nc_act(th[:, b], qk[:, :, 0:D], ACT.Tanh, scale=0.5)
                nc_act(eb[:, b, :, D:2 * D], qk[:, :, D:2 * D], ACT.Exp).then_inc(sig["ek"], 1)
            act.wait_ge(sig["ewT_mm"], 1)
            nc_act(ewT[:, 0], bank(3, 1).rearrange("p (a n) -> p a n", a=TILES), ACT.Copy).then_inc(sig["ewT_hi"], 1)
            for b in range(B):
                act.wait_ge(sig["ekv"], b + 1)
                nc_act(eb16[:, 0, b], eb[:, b], ACT.Copy).then_inc(sig["eb_hi"], 1)
            split_hi("w1")
            split_hi("w2")
            for b in range(B):
                act.wait_ge(sig["turned"], nth(T_Y, b))
                nc_act(colsY[:, 0, b], bank(b, 1)[:, 0:T], ACT.Copy).then_inc(sig["cols_hi"], 1)
            split_hi("wk")
            split_hi("wv")
            split_hi("wq")
            split_hi("wo1")
            for b in range(B):
                act.wait_ge(sig["turned"], nth(T_A, b))
                nc_act(colsN[:, 0, b], bank(b, 1)[:, 0:T], ACT.Identity, scale=gamma_col, bias=beta_col)\
                    .then_inc(sig["cols_hi"], 1)
            for b in range(B):
                act.wait_ge(sig["hid_mm"], b + 1)
                nc_act(hid16[:, 0, b], pair(b), ACT.Relu).then_inc(sig["hid_hi"], 1)
            act.wait_ge(sig["l_ctxT"], 16)
            act.wait_ge(sig["attn_mm"], B)
            nc_act(ctxT[:, 0], ctxT_in, ACT.Copy).then_inc(sig["ctxT_hi"], 1)
            split_hi("m1")
            for b in range(B):
                act.wait_ge(sig["turned"], nth(T_QUANT, b))
                nc_act(qT[:, b], bank(b, 1)[:, 0:T], ACT.Copy, bias=-MAGIC).then_inc(sig["q1T_ready"], 1)
            for t in range(TILES):
                for b in range(B):
                    act.wait_ge(sig["gu_mm"], B * t + b + 1)
                    act.wait_ge(sig["gscale"], b + 1)
                    if t:
                        act.wait_ge(sig["g1"], b + 1)
                    nc_act(thg[:, b], bank(b, 0), ACT.Tanh, scale=fac[:, b, 0, t:t + 1]).then_inc(sig["tanhg"], 1)
            split_hi("m2")
            for b in range(B):
                act.wait_ge(sig["q2T_mm"], b + 1)
                nc_act(gT[:, b].rearrange("p t c n -> p (t c n)"), pair(b).rearrange("p a n -> p (a n)"), ACT.Copy,
                       bias=-MAGIC).then_inc(sig["q2T_ready"], 1)
            for b in range(B):
                act.wait_ge(sig["turned"], nth(T_QUERY, b))
                nc_act(colsA[:, 0, b], bank(b, 1)[:, 0:T], ACT.Copy).then_inc(sig["cols_hi"], 1)
            for b in range(B):
                act.wait_ge(sig["q_mm"], b + 1)
                nc_act(qh[:, b].rearrange("p h n -> p (h n)"), pair(b).rearrange("p a n -> p (a n)"), ACT.Copy)\
                    .then_inc(sig["qa_hi"], 1)
            for b in range(B):
                act.wait_ge(sig["kproj"], b + 1)
                nc_act(kh[:, b].rearrange("p h n -> p (h n)"), pair(b).rearrange("p a n -> p (a n)"), ACT.Copy)\
                    .then_inc(sig["ka_hi"], 1)
            act.wait_ge(sig["zeros_ready"], 2)
            for b in range(B):
                act.wait_ge(sig["vproj"], b + 1)
                for t in range(TILES):
                    ins = nc_act(va[:, b, t, :, 0:DK],
                                 bank(b, 0)[:, t * D:(t + 1) * D].rearrange("p (h k) -> p h k", h=NH), ACT.Copy)
                ins.then_inc(sig["va_ready"], 1)
            def out_copy(m):
                act.wait_ge(sig["pv"], 2 * m + 2)
                b, half = divmod(m, 2)
                nc_act(oT[:, b, 2 * half:2 * half + 2].rearrange("p h n -> p (h n)"), ps[:, 4 + m % 2, :], ACT.Copy)\
                    .then_inc(sig["oT"], 1)

            for n in range(B * QUADS):
                for k in range(4):
                    head = 4 * n + k
                    act.wait_ge(sig["st_mm"], head + 1)
                    if head >= PRING:
                        act.wait_ge(sig["pv"], (head - PRING) // 4 + 1)
                    nc_act(pt[:, head % PRING].rearrange("p t n -> p (t n)"), ps[:, 2 + head % 2, :], ACT.Exp,
                           scale=DK ** -0.5).then_inc(sig["probs"], 1)
                if n >= 2 and n % 2 == 0:
                    out_copy(n // 2 - 1)
            out_copy(B * QUADS // 2 - 1)
            for b in range(B):
                act.wait_ge(sig["turned"], nth(T_ATTN, b))
                nc_act(colsY[:, 0, b], bank(b, 0)[:, 0:T], ACT.Copy).then_inc(sig["cols_hi"], 1)
            for b in range(B):
                act.wait_ge(sig["turned"], nth(T_MOE, b))
                nc_act(colsN[:, 0, b], bank(b, 0)[:, 0:T], ACT.Copy).then_inc(sig["cols_hi"], 1)
            for b in range(B):
                act.wait_ge(sig["topix"], b + 1)
                for t in range(TILES):
                    ins = nc_act(ejunk[:, b, t], bank(b, 1)[:, t * NE:(t + 1) * NE], ACT.Exp, bias=ntop[:, b, t:t + 1],
                                 accum_out=esum[:, b, t:t + 1])
                ins.then_inc(sig["expsum"], 1)
            for b in range(B):
                act.wait_ge(sig["ohT_mm"], b + 1)
                nc_act(ohT[:, b], bank(b, 0)[0:2 * NE, 0:T], ACT.Copy).then_inc(sig["ohT"], 1)
            for b in range(B):
                for half in range(2):
                    act.wait_ge(sig["oh_mm"], 2 * b + half + 1)
                    if b >= 2:
                        act.wait_ge(sig["xm"], b - 1)
                    nc_act(oh[:, b % 2, 4 * half:4 * half + 4].rearrange("p e n -> p (e n)"),
                           pair(b).rearrange("p a n -> p (a n)"), ACT.Copy).then_inc(sig["oh"], 1)
            for b in range(B):
                act.wait_ge(sig["moe_h"], b + 1)
                nc_act(gelu32[:, b].rearrange("p c n -> p (c n)"), bank(b, 0), ACT.Gelu).then_inc(sig["gelu"], 1)
                act.wait_ge(sig["gelu"], b + 1)
                nc_act(gelu16[:, 0, b], gelu32[:, b], ACT.Copy).then_inc(sig["gelu_hi"], 1)

        @block.vector
        def _(dve):
            V = nc.vector

            def ln_stats(ln, b, src):
                for t in range(TILES):
                    ins = V.bn_stats(stats[:, ln, b, t], src(t))
                ins.then_inc(sig["ln_stats"], 1)

            def ln_moments(ln, b):
                dve.wait_ge(sig["ln_stats"], nth(ln, b))
                for t in range(TILES):
                    ins = V.bn_aggr(moments[:, ln, b, t], stats[:, ln, b, t])
                ins.then_inc(sig["ln_moments"], 1)

            def ln_rows(ln, b, src):
                dve.wait_ge(sig["ln_rstd"], nth(ln, b))
                for t in range(TILES):
                    ins = V.tensor_scalar(rows[:, b, t], src(t), moments[:, ln, b, t, 0:1], rstd[:, ln, b, t:t + 1],
                                          ALU.subtract, ALU.mult)
                ins.then_inc(sig["rows_ready"], 1)

            def lo_part(dst, src, hi, done):
                V.tensor_tensor(dst, src, hi, ALU.subtract).then_inc(sig[done], 1)

            def split_lo(name, n):
                a, z = SEG[name]
                dve.wait_ge(sig["w_hi"], n)
                lo_part(w16[:, 1, a:z], wf32(name), w16[:, 0, a:z], "w_lo")

            for b in range(B):
                dve.wait_ge(sig[f"l_x{b}"], 16)
                ln_stats(LN_IN, b, lambda t: x_in[:, b, t])
                ln_moments(LN_IN, b)
            dve.wait_ge(sig["l_cst"], 16)
            V.tensor_copy(id16[:, :], ident)
            V.tensor_scalar(idbig[:, :], ident, BIG, None, ALU.mult)
            V.tensor_copy(sel16[:, :], c("sel", 1)).then_inc(sig["id_ready"], 1)
            for b in range(B):
                ln_rows(LN_IN, b, lambda t: x_in[:, b, t])
            split_lo("qkv", 1)
            dve.wait_ge(sig["bias_hi"], 1)
            V.scalar_tensor_tensor(bias16[:, :], bias_h[:, :], c("lo_2", 2), bias_in[:, :], ALU.mult, ALU.add)\
                .then_inc(sig["bias_ready"], 1)
            dve.wait_ge(sig["mbias_hi"], 1)
            V.scalar_tensor_tensor(mbias16[:, :], mbias_h[:, :], c("lo_16", 2 * NE), mbias_in[:, :], ALU.mult, ALU.add)\
                .then_inc(sig["mbias_ready"], 1)
            for b in range(B):
                dve.wait_ge(sig["cols_hi"], nth(C_EMB, b))
                lo_part(colsA[:, 1, b], bank(b, 0)[:, 0:T], colsA[:, 0, b], "cols_ready")
            split_lo("wo", 2)
            dve.wait_ge(sig["pos_masked"], 1)
            V.tensor_reduce(posmax[:, :], posw[:, :, :], AX.X, ALU.max, negate=True).then_inc(sig["pos_max"], 1)
            V.tensor_tensor(wgsq[:, :], c("wgT", NG), c("wgT", NG), ALU.mult).then_inc(sig["wgsq"], 1)
            for b in range(B):
                dve.wait_ge(sig["kT_mm"], b + 1)
                V.tensor_reduce(kmx[:, b, 0:1], bank(b, 1)[:, T:2 * T], AX.X, ALU.max).then_inc(sig["kmax"], 1)
                dve.wait_ge(sig["kmax"], b + 1)
                V.tensor_scalar(kmx[:, b, 1:2], kmx[:, b, 0:1], bk_col, -1.0, ALU.add, ALU.mult)\
                    .then_inc(sig["kmaxb"], 1)
                dve.wait_ge(sig["kmaxb"], b + 1)
                V.tensor_scalar(kdiag[:, b], ident, kmx[:, b, 1:2], None, ALU.mult).then_inc(sig["kdiag"], 1)
            dve.wait_ge(sig["means_ready"], 1)
            V.tensor_scalar(mean[:, :], bank(3, 1)[:, T:T + 3], 1.0 / (HID * D), 1e-5, ALU.mult, ALU.max)\
                .then_inc(sig["meanc"], 1)
            dve.wait_ge(sig["meanc"], 1)
            V.reciprocal(wscale[:, :], mean[:, :]).then_inc(sig["ffscale"], 1)
            V.tensor_scalar(kfac[:, 0:1], mean[:, 0:1], 0.5 / 127.0, None, ALU.mult)
            V.tensor_scalar(kfac[:, 1:2], mean[:, 0:1], mean[:, 1:2], 0.5 / (127.0 * 127.0), ALU.mult, ALU.mult)
            V.tensor_scalar(kfac[:, 2:3], mean[:, 2:3], 1.0 / 127.0, None, ALU.mult).then_inc(sig["kscale"], 1)
            for b in range(B):
                dve.wait_ge(sig["ek"], b + 1)
                V.tensor_tensor(eb[:, b, :, 0:D], eb[:, b, :, D:2 * D],
                                bank(b, 1)[:, 0:2 * D].rearrange("p (t n) -> p t n", t=TILES), ALU.mult)\
                    .then_inc(sig["ekv"], 1)
            dve.wait_ge(sig["ewT_hi"], 1)
            lo_part(ewT[:, 1], bank(3, 1).rearrange("p (a n) -> p a n", a=TILES), ewT[:, 0], "ewT_ready")
            for b in range(B):
                dve.wait_ge(sig["eb_hi"], b + 1)
                lo_part(eb16[:, 1, b], eb[:, b], eb16[:, 0, b], "eb_lo")
            dve.wait_ge(sig["ffscale"], 1)
            for k in range(3):
                V.tensor_scalar(ffw_in[:, k], ffw_in[:, k], wscale[:, k:k + 1], MAGIC, ALU.mult, ALU.add)\
                    .then_inc(sig["ffw_r"], 1)
            for k in range(3):
                dve.wait_ge(sig["ffw_r"], k + 1)
                V.tensor_scalar(ffw_in[:, k], ffw_in[:, k], MAGIC + 1.0, MAGIC - 1.0, ALU.min, ALU.max)\
                    .then_inc(sig["ffw_c"], 1)
            for k in range(3):
                dve.wait_ge(sig["ffw_c"], k + 1)
                V.tensor_scalar(ffw16[:, k], ffw_in[:, k], MAGIC, None, ALU.subtract).then_inc(sig["ffw_ready"], 1)
            for b in range(B):
                nd = bank(b, 0).rearrange("p (t n) -> p t n", t=TILES)
                dve.wait_ge(sig["numden"], b + 1)
                V.reciprocal(rden[:, b], nd[:, :, D:2 * D]).then_inc(sig["rden"], 1)
                V.scalar_tensor_tensor(th[:, b], th[:, b], 1.0, nd[:, :, 0:D], ALU.add, ALU.mult)\
                    .then_inc(sig["ysig"], 1)
                dve.wait_ge(sig["ysig"], b + 1)
                V.scalar_tensor_tensor(y[:, b], th[:, b], 0.5, rden[:, b], ALU.mult, ALU.mult).then_inc(sig["y"], 1)
            split_lo("w1", 3)
            split_lo("w2", 4)
            for b in range(B):
                dve.wait_ge(sig["cols_hi"], nth(C_Y, b))
                lo_part(colsY[:, 1, b], bank(b, 1)[:, 0:T], colsY[:, 0, b], "cols_ready")
            for b in range(B):
                dve.wait_ge(sig["attn_mm"], b + 1)
                ln_stats(LN_A, b, lambda t: bank(b, 0)[:, t * D:(t + 1) * D])
                ln_moments(LN_A, b)
            for b in range(B):
                ln_rows(LN_A, b, lambda t: bank(b, 0)[:, t * D:(t + 1) * D])
            for b in range(B):
                dve.wait_ge(sig["cols_hi"], nth(C_A, b))
                V.tensor_scalar(a32[:, b], bank(b, 1)[:, 0:T], gamma_col, beta_col, ALU.mult, ALU.add)\
                    .then_inc(sig["aT_32"], 1)
            for b in range(B):
                dve.wait_ge(sig["aT_32"], b + 1)
                lo_part(colsN[:, 1, b], a32[:, b], colsN[:, 0, b], "cols_ready")
            for b in range(B):
                dve.wait_ge(sig["hid_hi"], b + 1)
                V.scalar_tensor_tensor(hid16[:, 1, b].rearrange("p c n -> p (c n)"), pair(b).rearrange("p a n -> p (a n)"),
                                       0.0, hid16[:, 0, b].rearrange("p c n -> p (c n)"), ALU.max, ALU.subtract)\
                    .then_inc(sig["hid_ready"], 1)
            split_lo("wk", 5)
            split_lo("wv", 6)
            dve.wait_ge(sig["ctxT_hi"], 1)
            lo_part(ctxT[:, 1], ctxT_in, ctxT[:, 0], "ctxT_ready")
            for b in range(B):
                dve.wait_ge(sig["ff_mm"], b + 1)
                ln_stats(LN_OUT, b, lambda t: bank(b, 0)[:, t * D:(t + 1) * D])
                ln_moments(LN_OUT, b)
            for b in range(B):
                dve.wait_ge(sig["xb"], b + 1)
                dve.wait_ge(sig["ln_moments"], nth(LN_OUT, b))
                for t in range(TILES):
                    ins = V.scalar_tensor_tensor(nb[:, b, t], bank(b, 0)[:, t * D:(t + 1) * D],
                                                 moments[:, LN_OUT, b, t, 0:1], gamma_b[:, :], ALU.subtract, ALU.mult)
                ins.then_inc(sig["nb"], 1)
            for b in range(B):
                dve.wait_ge(sig["nb"], b + 1)
                dve.wait_ge(sig["ln_rstd"], nth(LN_OUT, b))
                for t in range(TILES):
                    ins = V.scalar_tensor_tensor(x1[:, b, t], nb[:, b, t], rstd[:, LN_OUT, b, t:t + 1], xb[:, b, t],
                                                 ALU.mult, ALU.add)
                ins.then_inc(sig["x1"], 1)
            for b in range(B):
                dve.wait_ge(sig["x1"], b + 1)
                ln_stats(LN_FFN, b, lambda t: x1[:, b, t])
                ln_moments(LN_FFN, b)

            def quant_scale(b, src, row):
                V.tensor_reduce(amax[:, b, row, :], src, AX.X, ALU.max, apply_absolute_value=True)\
                    .then_inc(sig["amax"], 1)
                dve.wait_ge(sig["amax"], nth(row // 2, b))
                V.tensor_scalar(amax[:, b, row, :], amax[:, b, row, :], 1e-5, None, ALU.max).then_inc(sig["amaxc"], 1)
                dve.wait_ge(sig["amaxc"], nth(row // 2, b))
                V.reciprocal(amax[:, b, row + 1, :], amax[:, b, row, :]).then_inc(sig["ainv"], 1)
                dve.wait_ge(sig["ainv"], nth(row // 2, b))
                V.tensor_scalar(amax[:, b, row + 1, :], amax[:, b, row + 1, :], 127.0, None, ALU.mult)\
                    .then_inc(sig["ascale"], 1)

            for b in range(B):
                ln_rows(LN_FFN, b, lambda t: x1[:, b, t])
            dve.wait_ge(sig["kscale"], 1)
            for b in range(B):
                dve.wait_ge(sig["rows_ready"], nth(R_FFN, b))
                quant_scale(b, rows[:, b], 0)
                V.tensor_scalar(fac[:, b, 0, :], amax[:, b, 0, :], kfac[:, 0:1], None, ALU.mult)
                for t in range(TILES):
                    ins = V.tensor_scalar(fac[:, b, 1, t:t + 1], amax[:, b, 0, t:t + 1], amax[:, b, 0, t:t + 1],
                                          kfac[:, 1:2], ALU.mult, ALU.mult)
                ins.then_inc(sig["gscale"], 1)
                dve.wait_ge(sig["ascale"], nth(0, b))
                for t in range(TILES):
                    ins = V.tensor_scalar(rows[:, b, t], rows[:, b, t], amax[:, b, 1, t:t + 1], MAGIC, ALU.mult, ALU.add)
                ins.then_inc(sig["q1"], 1)
            for t in range(TILES):
                for b in range(B):
                    k = B * t + b + 1
                    dve.wait_ge(sig["tanhg"], k)
                    V.scalar_tensor_tensor(g1[:, b], thg[:, b], 1.0, bank(b, 0), ALU.add, ALU.mult)\
                        .then_inc(sig["g1"], 1)
                    dve.wait_ge(sig["g1"], k)
                    V.scalar_tensor_tensor(g[:, b, t], g1[:, b], fac[:, b, 1, t:t + 1], bank(b, 1), ALU.mult, ALU.mult)\
                        .then_inc(sig["g"], 1)
            for b in range(B):
                dve.wait_ge(sig["g"], B + b + 1)
                quant_scale(b, g[:, b], 2)
                V.tensor_scalar(fac[:, b, 2, :], amax[:, b, 2, :], kfac[:, 2:3], None, ALU.mult).then_inc(sig["kscale"], 1)
            for b in range(B):
                dve.wait_ge(sig["down_mm"], b + 1)
                dve.wait_ge(sig["kscale"], b + 2)
                for t in range(TILES):
                    ins = V.scalar_tensor_tensor(x2[:, b, t], bank(b, 0)[:, t * D:(t + 1) * D], fac[:, b, 2, t:t + 1],
                                                 x1[:, b, t], ALU.mult, ALU.add)
                ins.then_inc(sig["x2"], 1)
            for b in range(B):
                dve.wait_ge(sig["x2"], b + 1)
                ln_stats(LN_ATT, b, lambda t: x2[:, b, t])
                ln_moments(LN_ATT, b)
            for b in range(B):
                ln_rows(LN_ATT, b, lambda t: x2[:, b, t])
            for b in range(B):
                dve.wait_ge(sig["cols_hi"], nth(C_QUERY, b))
                lo_part(colsA[:, 1, b], bank(b, 1)[:, 0:T], colsA[:, 0, b], "cols_ready")
            dve.wait_ge(sig["l_mask"], 16)
            V.tensor_scalar(ind[:, :, :, :].rearrange("p a t n -> p (a t n)"),
                            mask_in[:, :, :, :].rearrange("p a t n -> p (a t n)"), 0.0, None, ALU.is_equal)\
                .then_inc(sig["mask_ind"], 1)
            for b in range(B):
                dve.wait_ge(sig["qa_hi"], b + 1)
                V.scalar_tensor_tensor(qa[:, b].rearrange("p h n -> p (h n)"), qh[:, b].rearrange("p h n -> p (h n)"),
                                       c("lo_q"), pair(b).rearrange("p a n -> p (a n)"), ALU.mult, ALU.add)\
                    .then_inc(sig["qa_ready"], 1)
            dve.wait_ge(sig["count_mm"], 1)
            cnt = ps[:, 0:2, :].rearrange("p a n -> p (a n)")
            V.tensor_scalar(colmask[:, :, :].rearrange("p a n -> p (a n)"), cnt, T - 0.5, 4 * BIG, ALU.is_ge, ALU.mult)
            V.tensor_scalar(colrow[:, :, :].rearrange("p a n -> p (a n)"), cnt[0:1], T - 0.5, BIG, ALU.is_ge, ALU.mult)\
                .then_inc(sig["colmask"], 1)
            dve.wait_ge(sig["colmask"], 1)
            V.scalar_tensor_tensor(flag_junk[:, :], colmask[0:1].rearrange("p a n -> p (a n)"), -T / (4 * BIG), cnt[0:1],
                                   ALU.mult, ALU.add, accum_out=flag_f[:, :]).then_inc(sig["flagsum"], 1)
            for b in range(B):
                ins = V.scalar_tensor_tensor(resmask[:, b], ind[:, b], -4 * BIG, colmask[:, b].unsqueeze(1).to_broadcast(
                    [P, TILES, T]), ALU.mult, ALU.add)
            ins.then_inc(sig["resmask"], 1)
            dve.wait_ge(sig["flagsum"], 1)
            V.tensor_copy(flag_i[:, :], flag_f[:, :]).then_inc(sig["flag_ready"], 1)
            dve.wait_ge(sig["router_mm"], 1)
            V.tensor_copy(wnorm[:, 0], bank(3, 1)[:, NE:2 * NE]).then_inc(sig["router_step"], 1)
            dve.wait_ge(sig["wg_root"], 1)
            V.tensor_scalar(wnorm[:, 2], wnorm[:, 1], 1e-4, None, ALU.max).then_inc(sig["router_step"], 1)
            dve.wait_ge(sig["router_step"], 2)
            V.reciprocal(wnorm[:, 1], wnorm[:, 2]).then_inc(sig["router_step"], 1)
            dve.wait_ge(sig["router_step"], 3)
            V.tensor_tensor(router[:, :], bank(3, 1)[:, 0:NE], wnorm[:, 1], ALU.mult).then_inc(sig["router_step"], 1)
            dve.wait_ge(sig["router_step"], 4)
            V.tensor_copy(router16[:, 0], router[:, :]).then_inc(sig["router_step"], 1)
            dve.wait_ge(sig["router_step"], 5)
            lo_part(router16[:, 1], router[:, :], router16[:, 0], "router_ready")
            for b in range(B):
                dve.wait_ge(sig["ka_hi"], b + 1)
                V.scalar_tensor_tensor(ka[:, b].rearrange("p h n -> p (h n)"), kh[:, b].rearrange("p h n -> p (h n)"),
                                       c("lo_k"), pair(b).rearrange("p a n -> p (a n)"), ALU.mult, ALU.add)\
                    .then_inc(sig["ka_ready"], 1)

            def head_max(n, i):
                b, quad = divmod(n, QUADS)
                t, pair_of = divmod(i, 2)
                head = 4 * quad + 2 * pair_of
                dve.wait_ge(sig["s_mm"], 4 * n + i + 1)
                V.tensor_reduce(mx[:, b, head:head + 2, t], score_bank(4 * n + i).rearrange("p (h n) -> p h n", h=2),
                                AX.X, ALU.max).then_inc(sig["smax"], 1)

            def shift_rows(n):
                b, quad = divmod(n, QUADS)
                dve.wait_ge(sig["smax"], 4 * n + 4)
                if n >= 2:
                    dve.wait_ge(sig["shift_mm"], n - 1)
                for t in range(TILES):
                    ins = V.tensor_scalar(
                        spread[:, n % 2, t].rearrange("p (g r) -> p g r", g=4)[:, :, 28:32],
                        mx[:, b, 4 * quad:4 * quad + 4, t:t + 1].to_broadcast([P, 4, 4]),
                        -1.0 / (4 * BIG), None, ALU.mult)
                ins.then_inc(sig["spread"], 1)

            def shifted_query(n):
                b, quad = divmod(n, QUADS)
                dve.wait_ge(sig["shift_mm"], n + 1)
                if n >= 2:
                    dve.wait_ge(sig["st_mm"], 4 * (n - 1))
                V.tensor_tensor(qb[:, n % 2], ps[:, 6, 0:T], qa[:, b, quad], ALU.add).then_inc(sig["qb"], 1)

            for n in range(2):
                for k in range(4):
                    head_max(n, k)
                shift_rows(n)
                if n == 0:
                    shifted_query(0)
            for n in range(B * QUADS):
                for k in range(4):
                    if n + 2 < B * QUADS:
                        head_max(n + 2, k)
                    if k == 1 and n + 1 < B * QUADS:
                        shifted_query(n + 1)
                if n + 2 < B * QUADS:
                    shift_rows(n + 2)
            for b in range(B):
                dve.wait_ge(sig["oR_mm"], b + 1)
                for t in range(TILES):
                    heads = bank(b, t).rearrange("p (h r) -> p h r", h=NH)
                    ins = V.reciprocal(oden[:, b, t], heads[:, :, DK])
                ins.then_inc(sig["oden"], 1)
                dve.wait_ge(sig["oden"], b + 1)
                for t in range(TILES):
                    heads = bank(b, t).rearrange("p (h r) -> p h r", h=NH)
                    ins = V.tensor_tensor(attn[:, b, t].rearrange("p (h k) -> p h k", h=NH), heads[:, :, 0:DK],
                                          oden[:, b, t].unsqueeze(2).to_broadcast([P, NH, DK]), ALU.mult)
                ins.then_inc(sig["attn"], 1)
            for b in range(B):
                dve.wait_ge(sig["cols_hi"], nth(C_ATTN, b))
                lo_part(colsY[:, 1, b], bank(b, 0)[:, 0:T], colsY[:, 0, b], "cols_ready")
            for b in range(B):
                dve.wait_ge(sig["wo1_mm"], b + 1)
                V.tensor_tensor(x3[:, b].rearrange("p t n -> p (t n)"), bank(b, 1)[:, 0:T],
                                x2[:, b].rearrange("p t n -> p (t n)"), ALU.add).then_inc(sig["x3"], 1)
                dve.wait_ge(sig["x3"], b + 1)
                ln_stats(LN_MOE, b, lambda t: x3[:, b, t])
                ln_moments(LN_MOE, b)
            for b in range(B):
                ln_rows(LN_MOE, b, lambda t: x3[:, b, t])
            for b in range(B):
                dve.wait_ge(sig["cols_hi"], nth(C_MOE, b))
                lo_part(colsN[:, 1, b], bank(b, 0)[:, 0:T], colsN[:, 0, b], "cols_ready")
            for b in range(B):
                dve.wait_ge(sig["logit_mm"], b + 1)
                logit = bank(b, 1)[:, 0:TILES * NE].rearrange("p (t e) -> p t e", t=TILES)
                for t in range(TILES):
                    ins = V.max(top8[:, b, t], logit[:, t])
                ins.then_inc(sig["top8"], 1)
                dve.wait_ge(sig["top8"], b + 1)
                V.tensor_scalar(ntop[:, b], top8[:, b, :, 0], -1.0, None, ALU.mult)
                for t in range(TILES):
                    ins = V.max_index(topix[:, b, t], top8[:, b, t], logit[:, t])
                ins.then_inc(sig["topix"], 1)
                dve.wait_ge(sig["topix"], b + 1)
                for t in range(TILES):
                    ins = V.tensor_scalar(onehot[:, b, t], c("iota"), topix[:, b, t, 0:1], None, ALU.is_equal)
                ins.then_inc(sig["onehot"], 1)
            for b in range(B):
                dve.wait_ge(sig["expsum"], b + 1)
                V.reciprocal(score[:, b], esum[:, b]).then_inc(sig["score"], 1)
            for b in range(B):
                dve.wait_ge(sig["onehot"], b + 1)
                dve.wait_ge(sig["score"], b + 1)
                for t in range(TILES):
                    ins = V.tensor_scalar(wsel[:, b, t], onehot[:, b, t, 0:NE], score[:, b, t:t + 1], None, ALU.mult)
                ins.then_inc(sig["wsel"], 1)
            for b in range(B):
                dve.wait_ge(sig["oh"], 2 * b + 2)
                if b >= 2:
                    dve.wait_ge(sig["moe_h"], b - 1)
                for part in range(2):
                    V.tensor_tensor(xm[:, part, b % 2], oh[:, b % 2],
                                    colsN[:, part, b].unsqueeze(1).to_broadcast([P, NE, T]), ALU.mult)\
                        .then_inc(sig["xm" if part else "xm_hi"], 1)
            for b in range(B):
                dve.wait_ge(sig["gelu_hi"], b + 1)
                lo_part(gelu16[:, 1, b], gelu32[:, b], gelu16[:, 0, b], "gelu_ready")
                for t in range(TILES):
                    ins = V.scalar_tensor_tensor(y0[:, b, t], bank(b, 1)[:, t * D:(t + 1) * D], score[:, b, t:t + 1],
                                                 x3[:, b, t], ALU.mult, ALU.add)
                ins.then_inc(sig["y0"], 1)
            for t in range(TILES):
                for b in range(B):
                    k = B * t + b
                    dve.wait_ge(sig["moe_o"], k + 1)
                    dve.wait_ge(sig["wsel"], b + 1)
                    if k >= 2:
                        dve.wait_ge(sig["picksum"], k - 1)
                    V.tensor_tensor(picked[:, k % 2], pair(b).rearrange("p a (e n) -> p (a e) n", n=D),
                                    wsel[:, b, t].unsqueeze(2).to_broadcast([P, NE, D]), ALU.mult)\
                        .then_inc(sig["picked"], 1)
                    dve.wait_ge(sig["picked"], k + 1)
                    if k >= 2:
                        dve.wait_ge(sig["y_out"], k - 1)
                    V.tensor_reduce(picksum[:, k % 2], picked[:, k % 2].rearrange("p e n -> p n e"), AX.X, ALU.add)\
                        .then_inc(sig["picksum"], 1)
                    dve.wait_ge(sig["picksum"], k + 1)
                    dve.wait_ge(sig["y0"], b + 1)
                    V.tensor_tensor(res[:, b, t], picksum[:, k % 2], y0[:, b, t], ALU.add).then_inc(sig["y_out"], 1)

        @block.tensor
        def _(pe):
            def mm(dst, lhsT, rhs, start, stop):
                return nc.tensor.matmul(dst, lhsT, rhs, start=start, stop=stop, skip_group_check=True)

            def product(dst, lhsT, rhs, start=True, stop=True):
                for n, (i, j) in enumerate(PASSES):
                    ins = mm(dst, lhsT(i), rhs(j), start and n == 0, stop and n == len(PASSES) - 1)
                return ins

            def transposed(dst, src):
                return nc.tensor.transpose(dst, src, ident)

            def row_bias(dst, name, stop=True):
                return mm(dst, ones16[0:2, 0:P], brow(name), False, stop)

            pe.wait_ge(sig["l_cst"], 16)
            for b in range(B):
                pe.wait_ge(sig["emb"], b + 1)
                for t in range(TILES):
                    ins = transposed(bank(b, 0)[:, t * P:(t + 1) * P], emb[:, b, t])
                ins.then_inc(sig["turned"], 1)
            pe.wait_ge(sig["w_lo"], 1)
            pe.wait_ge(sig["bias_ready"], 1)
            for b in range(B):
                pe.wait_ge(sig["cols_ready"], nth(C_EMB, b))
                product(bank(b, 1)[:, T:2 * T], lambda i: w("qkv", i)[:, D:2 * D], lambda j: colsA[:, j, b])
                for t in range(TILES):
                    tok = slice(t * P, (t + 1) * P)
                    dst = bank(b, 1)[:, t * D:(t + 1) * D]
                    product(dst, lambda i: colsA[:, i, b, tok], lambda j: w("qkv", j)[:, 2 * D:3 * D], stop=False)
                    ins = mm(dst, ones16[0:2, 0:P], brow("qkv")[:, 2 * D:3 * D], False, True)
                ins.then_inc(sig["kT_mm"], 1)
                for t in range(TILES):
                    tok = slice(t * P, (t + 1) * P)
                    dst = bank(b, 0)[:, t * 2 * D:(t + 1) * 2 * D]
                    product(dst, lambda i: colsA[:, i, b, tok], lambda j: w("qkv", j)[:, 0:2 * D], start=t == 0,
                            stop=False)
                    ins = mm(dst, ones16[0:2, 0:P], brow("qkv")[:, 0:2 * D], False, False)
            pe.wait_ge(sig["ones_ready"], 1)
            for b in range(B):
                pe.wait_ge(sig["kdiag"], b + 1)
                for t in range(TILES):
                    ins = mm(bank(b, 0)[:, t * 2 * D + D:(t + 1) * 2 * D], ones32[:, :], kdiag[:, b], False, True)
                ins.then_inc(sig["kshift"], 1)
            pe.wait_ge(sig["absum"], 3)
            mm(bank(3, 1)[:, T:T + 3], ones32[:, :], absum[:, :], True, True).then_inc(sig["means_ready"], 1)
            pe.wait_ge(sig["ew_done"], TILES)
            pe.wait_ge(sig["meanc"], 1)
            pe.wait_ge(sig["ekv"], B)
            for j in range(TILES):
                for t in range(TILES):
                    ins = transposed(bank(3, 1)[:, j * T + t * P:j * T + (t + 1) * P], ew[:, t, j * P:(j + 1) * P])
            ins.then_inc(sig["ewT_mm"], 1)
            pe.wait_ge(sig["ewT_ready"], 1)
            for b in range(B):
                pe.wait_ge(sig["eb_lo"], b + 1)
                for t in range(TILES):
                    tok = slice(t * P, (t + 1) * P)
                    for j in range(TILES):
                        ins = product(bank(b, 0)[:, t * 2 * D:(t + 1) * 2 * D], lambda i: ewT[:, i, j, tok],
                                      lambda k: eb16[:, k, b, j], start=j == 0, stop=j == TILES - 1)
                ins.then_inc(sig["numden"], 1)
            for b in range(B):
                pe.wait_ge(sig["y"], b + 1)
                for t in range(TILES):
                    ins = transposed(bank(b, 1)[:, t * P:(t + 1) * P], y[:, b, t])
                ins.then_inc(sig["turned"], 1)
            pe.wait_ge(sig["w_lo"], 2)
            pe.wait_ge(sig["id_ready"], 1)
            for b in range(B):
                pe.wait_ge(sig["cols_ready"], nth(C_Y, b))
                for t in range(TILES):
                    tok = slice(t * P, (t + 1) * P)
                    dst = bank(b, 0)[:, t * D:(t + 1) * D]
                    product(dst, lambda i: colsY[:, i, b, tok], lambda j: w("wo", j), stop=False)
                    mm(dst, colsA[:, 0, b, tok], id16[:, :], False, False)
                    mm(dst, colsA[:, 1, b, tok], id16[:, :], False, False)
                    ins = row_bias(dst, "bo")
                ins.then_inc(sig["attn_mm"], 1)
            for b in range(B):
                pe.wait_ge(sig["rows_ready"], nth(R_A, b))
                for t in range(TILES):
                    ins = transposed(bank(b, 1)[:, t * P:(t + 1) * P], rows[:, b, t])
                ins.then_inc(sig["turned"], 1)
            pe.wait_ge(sig["w_lo"], 3)
            for b in range(B):
                pe.wait_ge(sig["cols_ready"], nth(C_A, b))
                for k in range(HC):
                    dst = bank(b, k // 2)[:, (k % 2) * T:(k % 2 + 1) * T]
                    product(dst, lambda i: w("w1", i)[:, k * P:(k + 1) * P], lambda j: colsN[:, j, b], stop=False)
                    ins = mm(dst, brow("b1")[:, k * P:(k + 1) * P], ones16[0:2, :], False, True)
                ins.then_inc(sig["hid_mm"], 1)
            pe.wait_ge(sig["w_lo"], 4)
            for b in range(B):
                pe.wait_ge(sig["hid_ready"], b + 1)
                for t in range(TILES):
                    tok = slice(t * P, (t + 1) * P)
                    dst = bank(b, 0)[:, t * D:(t + 1) * D]
                    for k in range(HC):
                        product(dst, lambda i: hid16[:, i, b, k, tok], lambda j: w("w2", j)[:, k * D:(k + 1) * D],
                                start=k == 0, stop=False)
                    mm(dst, colsN[:, 0, b, tok], id16[:, :], False, False)
                    mm(dst, colsN[:, 1, b, tok], id16[:, :], False, False)
                    ins = row_bias(dst, "b2")
                ins.then_inc(sig["ff_mm"], 1)
            for b in range(B):
                pe.wait_ge(sig["q1"], b + 1)
                for t in range(TILES):
                    ins = transposed(bank(b, 1)[:, t * P:(t + 1) * P], rows[:, b, t])
                ins.then_inc(sig["turned"], 1)
            pe.wait_ge(sig["ffw_ready"], 3)
            for t in range(TILES):
                for b in range(B):
                    tok = slice(t * P, (t + 1) * P)
                    pe.wait_ge(sig["q1T_ready"], b + 1)
                    if t:
                        pe.wait_ge(sig["g"], b + 1)
                    mm(bank(b, 0), qT[:, b, tok], ffw16[:, 0], True, True)
                    mm(bank(b, 1), qT[:, b, tok], ffw16[:, 1], True, True).then_inc(sig["gu_mm"], 1)
            for b in range(B):
                pe.wait_ge(sig["q2"], b + 1)
                for t in range(TILES):
                    for k in range(HC):
                        ins = transposed(bank(b, t)[:, k * P:(k + 1) * P], g[:, b, t, k * P:(k + 1) * P])
                ins.then_inc(sig["q2T_mm"], 1)
            for b in range(B):
                pe.wait_ge(sig["q2T_ready"], b + 1)
                for t in range(TILES):
                    for k in range(HC):
                        ins = mm(bank(b, 0)[:, t * D:(t + 1) * D], gT[:, b, t, k], ffw16[:, 2, k * D:(k + 1) * D],
                                 k == 0, k == HC - 1)
                ins.then_inc(sig["down_mm"], 1)
            for b in range(B):
                pe.wait_ge(sig["rows_ready"], nth(R_ATT, b))
                for t in range(TILES):
                    ins = transposed(bank(b, 1)[:, t * P:(t + 1) * P], rows[:, b, t])
                ins.then_inc(sig["turned"], 1)
            pe.wait_ge(sig["w_lo_pool"], 1)
            for b in range(B):
                pe.wait_ge(sig["cols_ready"], nth(C_QUERY, b))
                for k in range(QUADS):
                    dst = bank(b, k // 2)[:, (k % 2) * T:(k % 2 + 1) * T]
                    product(dst, lambda i: w("wq", i)[:, k * P:(k + 1) * P], lambda j: colsA[:, j, b], stop=False)
                    ins = mm(dst, brow("bq")[:, k * P:(k + 1) * P], ones16[0:2, :], False, True)
                ins.then_inc(sig["q_mm"], 1)
            pe.wait_ge(sig["qa_ready"], 4)
            pe.wait_ge(sig["mask_ind"], 1)
            for b in range(B):
                for t in range(TILES):
                    ins = mm(ps[:, b // 2, (b % 2) * T:(b % 2 + 1) * T], ones16[:, 0:P], ind[:, b, t], t == 0, t == TILES - 1)
            ins.then_inc(sig["count_mm"], 1)
            pe.wait_ge(sig["wgsq"], 1)
            mm(bank(3, 1)[:, 0:NE], c("wredT", NG), c("wgT", NG), True, True)
            mm(bank(3, 1)[:, NE:2 * NE], ones32[0:NG, :], wgsq[:, :], True, True).then_inc(sig["router_mm"], 1)
            pe.wait_ge(sig["ctxT_ready"], 1)
            pe.wait_ge(sig["w_lo"], 6)
            pe.wait_ge(sig["flagsum"], 1)
            for b in range(B):
                if b == 3:
                    pe.wait_ge(sig["router_step"], 4)
                for k in range(QUADS):
                    dst = bank(b, k // 2)[:, (k % 2) * T:(k % 2 + 1) * T]
                    product(dst, lambda i: w("wk", i)[:, k * P:(k + 1) * P], lambda j: ctxT[:, j, b], stop=False)
                    mm(dst, brow("bk")[:, k * P:(k + 1) * P], ones16[0:2, :], False, False)
                    ins = mm(dst, sel16[:, :], colrow[:, b], False, True)
                ins.then_inc(sig["kproj"], 1)
            for b in range(B):
                pe.wait_ge(sig["ka_ready"], b + 1)
                for t in range(TILES):
                    tok = slice(t * P, (t + 1) * P)
                    dst = bank(b, 0)[:, t * D:(t + 1) * D]
                    product(dst, lambda i: ctxT[:, i, b, tok], lambda j: w("wv", j), stop=False)
                    ins = row_bias(dst, "bv")
                ins.then_inc(sig["vproj"], 1)
            pe.wait_ge(sig["va_ready"], 4)

            def scores(n, i, masked):
                b, quad = divmod(n, QUADS)
                t, pair_of = divmod(i, 2)
                if i == 0:
                    pe.wait_ge(sig["kz_ready"], n + 1)
                if 4 * n + i >= 3:
                    pe.wait_ge(sig["smax"], 4 * n + i - 2)
                dst = score_bank(4 * n + i)
                ins = mm(dst, qa[:, b, quad, t * P:(t + 1) * P],
                         kz[:, n % KRING, 2 * pair_of:2 * pair_of + 2].rearrange("p h n -> p (h n)"), True, not masked)
                if masked:
                    for h in range(2):
                        ins = mm(dst[:, h * T:(h + 1) * T], idbig[:, :], resmask[:, b, t], False, h == 1)
                ins.then_inc(sig["s_mm"], 1)

            def shift(n):
                pe.wait_ge(sig["spread"], n + 1)
                if n >= 1:
                    pe.wait_ge(sig["qb"], n)
                for t in range(TILES):
                    ins = mm(ps[:, 6, t * P:(t + 1) * P], spread[:, n % 2, t], id16[:, :], True, True)
                ins.then_inc(sig["shift_mm"], 1)

            def shifted_scores(n, k, masked):
                b, quad = divmod(n, QUADS)
                head = 4 * n + k
                if k == 0:
                    pe.wait_ge(sig["qb"], n + 1)
                if head >= 2:
                    pe.wait_ge(sig["probs"], head - 1)
                for t in range(TILES):
                    tok = slice(t * P, (t + 1) * P)
                    dst = ps[:, 2 + head % 2, t * T:(t + 1) * T]
                    ins = mm(dst, kz[:, n % KRING, k, tok], qb[:, n % 2], True, not masked)
                    if masked:
                        for q in range(TILES):
                            ins = mm(ps[:, 2 + head % 2, t * T + q * P:t * T + (q + 1) * P],
                                     resmask[:, b, q, tok], idbig[:, :], False, q == TILES - 1)
                ins.then_inc(sig["st_mm"], 1)

            def weighted_values(n, t):
                b, quad = divmod(n, QUADS)
                m = n // 2
                if t == 0:
                    pe.wait_ge(sig["probs"], 4 * n + 4)
                    if m >= 2 and n % 2 == 0:
                        pe.wait_ge(sig["oT"], m - 1)
                for k in range(4):
                    ins = mm(ps[32 * k:32 * k + 32, 4 + m % 2, (n % 2) * T:(n % 2 + 1) * T],
                             va[:, b, t, 4 * quad + k], pt[:, (4 * n + k) % PRING, t], t == 0, t == TILES - 1)
                if t == TILES - 1:
                    ins.then_inc(sig["pv"], 1)

            def attention(masked):
                for n in range(2):
                    for k in range(4):
                        scores(n, k, masked)
                    if n == 0:
                        shift(0)
                for n in range(B * QUADS):
                    for k in range(4):
                        shifted_scores(n, k, masked)
                        if n + 2 < B * QUADS:
                            scores(n + 2, k, masked)
                        if k == 1 and n + 1 < B * QUADS:
                            shift(n + 1)
                        if k < TILES and n >= 1:
                            weighted_values(n - 1, k)
                for t in range(TILES):
                    weighted_values(B * QUADS - 1, t)

            pe.wait_ge(sig["flag_ready"], 1)
            pe.wait_ge(sig["resmask"], 1)
            general = pe.value_load(flag_i[0:1, 0:1], min_val=0, max_val=B * T * T)
            with pe.If(general > 0):
                attention(True)
            with pe.Else():
                attention(False)

            for b in range(B):
                pe.wait_ge(sig["oT"], 2 * B)
                pe.wait_ge(sig["qb"], B * QUADS)
                for t in range(TILES):
                    for k in range(QUADS):
                        ins = transposed(bank(b, t)[:, k * P:(k + 1) * P], oT[:, b, k, t * P:(t + 1) * P])
                ins.then_inc(sig["oR_mm"], 1)
            for b in range(B):
                pe.wait_ge(sig["attn"], b + 1)
                for t in range(TILES):
                    ins = transposed(bank(b, 0)[:, t * P:(t + 1) * P], attn[:, b, t])
                ins.then_inc(sig["turned"], 1)
            pe.wait_ge(sig["w_lo_pool"], 2)
            for b in range(B):
                pe.wait_ge(sig["cols_ready"], nth(C_ATTN, b))
                for t in range(TILES):
                    tok = slice(t * P, (t + 1) * P)
                    dst = bank(b, 1)[:, t * D:(t + 1) * D]
                    product(dst, lambda i: colsY[:, i, b, tok], lambda j: w("wo1", j), stop=False)
                    ins = row_bias(dst, "bo1")
                ins.then_inc(sig["wo1_mm"], 1)
            for b in range(B):
                pe.wait_ge(sig["rows_ready"], nth(R_MOE, b))
                for t in range(TILES):
                    ins = transposed(bank(b, 0)[:, t * P:(t + 1) * P], rows[:, b, t])
                ins.then_inc(sig["turned"], 1)
            pe.wait_ge(sig["router_ready"], 1)
            for b in range(B):
                pe.wait_ge(sig["cols_ready"], nth(C_MOE, b))
                for t in range(TILES):
                    tok = slice(t * P, (t + 1) * P)
                    ins = product(bank(b, 1)[:, t * NE:(t + 1) * NE], lambda i: colsN[:, i, b, tok],
                                  lambda j: router16[:, j])
                ins.then_inc(sig["logit_mm"], 1)
            for b in range(B):
                pe.wait_ge(sig["onehot"], b + 1)
                for t in range(TILES):
                    ins = mm(bank(b, 0)[0:2 * NE, t * P:(t + 1) * P], onehot[:, b, t], id16[:, :], True, True)
                ins.then_inc(sig["ohT_mm"], 1)
            for b in range(B):
                for half in range(2):
                    if half == 0:
                        pe.wait_ge(sig["ohT"], b + 1)
                        pe.wait_ge(sig["expsum"], b + 1)
                    else:
                        pe.wait_ge(sig["oh"], 2 * b + 1)
                    for e in range(4):
                        for t in range(TILES):
                            ins = mm(bank(b, e // 2)[:, (e % 2) * T + t * P:(e % 2) * T + (t + 1) * P],
                                     onehot[:, b, t, 4 * half + e:4 * half + e + 1].to_broadcast([P, P]),
                                     id16[:, :], True, True)
                    ins.then_inc(sig["oh_mm"], 1)
            pe.wait_ge(sig["w_lo_pool"], 3)
            pe.wait_ge(sig["mbias_ready"], 1)
            for b in range(B):
                pe.wait_ge(sig["xm"], b + 1)
                for t in range(TILES):
                    mm(bank(b, 1)[:, t * D:(t + 1) * D], ohT[:, b, t * P:(t + 1) * P], mbias16[:, EH:EH + D], True, True)
                for k in range(EC):
                    dst = bank(b, 0)[:, k * T:(k + 1) * T]
                    for e in range(NE):
                        product(dst, lambda i: w("m1", i)[:, e * EH + k * P:e * EH + (k + 1) * P],
                                lambda j: xm[:, j, b % 2, e], start=e == 0, stop=False)
                    ins = mm(dst, mbias16[:, k * P:(k + 1) * P], ohT[:, b], False, True)
                ins.then_inc(sig["moe_h"], 1)
            pe.wait_ge(sig["w_lo_pool"], 4)
            for t in range(TILES):
                for b in range(B):
                    tok = slice(t * P, (t + 1) * P)
                    pe.wait_ge(sig["gelu_ready"], b + 1)
                    pe.wait_ge(sig["y0"], b + 1)
                    if t:
                        pe.wait_ge(sig["picked"], b + 1)
                    for half in range(2):
                        for k in range(EC):
                            col = k * NE * D + half * 4 * D
                            ins = product(bank(b, half), lambda i: gelu16[:, i, b, k, tok],
                                          lambda j: w("m2", j)[:, col:col + 4 * D], start=k == 0, stop=k == EC - 1)
                    ins.then_inc(sig["moe_o"], 1)


def kernel(x, ctx_1024, mask_BxSxS2_ik1, L0_xattn_wq, L0_xattn_bq, L0_xattn_wk, L0_xattn_bk, L0_xattn_wv, L0_xattn_bv,
           L0_xattn_wo, L0_xattn_bo, L0_xattn_pos_bias, L0_xattn_gamma, L0_xattn_beta, L0_xattn_w1, L0_xattn_b1,
           L0_xattn_w2, L0_xattn_b2, L0_ffn_w_gate, L0_ffn_w_up, L0_ffn_w_down, L1_xattn_Wq, L1_xattn_bq, L1_xattn_Wk,
           L1_xattn_bk, L1_xattn_Wv, L1_xattn_bv, L1_xattn_Wo, L1_xattn_bo, L1_ffn_w_red, L1_ffn_wg, L1_ffn_W1,
           L1_ffn_b1, L1_ffn_W2, L1_ffn_b2):
    import concourse.bacc as bacc
    from concourse.bass_utils import run_bass_kernel_spmd

    def heads32(m):
        m = m.reshape(m.shape[0], QUADS, 4, 1, DK)
        wide = np.zeros((m.shape[0], QUADS, 4, 4, DK), np.float32)
        wide[:, :, :, 0:3] = m
        return wide.reshape(m.shape[0], QUADS * P)

    x_rows = np.ascontiguousarray(np.asarray(x).reshape(B, TILES, P, D).transpose(0, 2, 1, 3))
    ctx = np.asarray(ctx_1024)
    ctx_rows = np.ascontiguousarray(ctx.reshape(B, TILES, P, D).transpose(2, 0, 1, 3))
    ctx_cols = np.ascontiguousarray(ctx.transpose(2, 0, 1))
    mask = np.ascontiguousarray(np.asarray(mask_BxSxS2_ik1).reshape(B, TILES, P, T).transpose(2, 0, 1, 3))
    pos = np.ascontiguousarray(np.asarray(L0_xattn_pos_bias).reshape(TILES, P, T).transpose(1, 0, 2))

    consts = np.zeros((P, NC_), np.float32)
    row = np.arange(P)
    consts[:, CSEG["ident"][0]:CSEG["ident"][1]] = np.eye(P)
    consts[:, CSEG["iota"][0]:CSEG["iota"][1]] = np.tile(np.arange(NE), 2)
    consts[:, CSEG["lo_q"][0]] = np.where((row % 32) // DK == 2, -1.0, 0.0)
    consts[:, CSEG["lo_k"][0]] = np.where((row % 32) // DK == 1, -1.0, 0.0)
    consts[:, CSEG["lo_2"][0]] = np.where(row == 1, -1.0, 0.0)
    consts[:, CSEG["lo_16"][0]] = np.where((row >= NE) & (row < 2 * NE), -1.0, 0.0)
    consts[0, CSEG["sel"][0]:CSEG["sel"][1]] = (row % 32 >= 24) & (row % 32 < 28)
    i, j = np.arange(T).reshape(TILES, P).T[:, :, None], np.arange(T)[None, None, :]
    consts[:, CSEG["band"][0]:CSEG["band"][1]] = (np.abs(i - j) < WINDOW).reshape(P, TILES * T)
    consts[:, CSEG["cols"][0]:CSEG["cols"][1]] = np.stack([np.asarray(L0_xattn_bk), np.asarray(L0_xattn_gamma), np.asarray(L0_xattn_beta)], 1)
    consts[0:NG, CSEG["wredT"][0]:CSEG["wredT"][1]] = np.asarray(L1_ffn_w_red).T
    consts[0:NG, CSEG["wgT"][0]:CSEG["wgT"][1]] = np.asarray(L1_ffn_wg).T

    def mask_rows(m, rows, value):
        m = m.reshape(1, QUADS, 4, 32).copy()
        m[:, :, :, rows] = value
        return m.reshape(1, QUADS * P)

    bias = np.concatenate([
        np.asarray(L0_xattn_bq)[None], np.asarray(L0_xattn_bk)[None], np.asarray(L0_xattn_bv)[None],
        np.asarray(L0_xattn_bo)[None], np.asarray(L0_xattn_b1)[None], np.asarray(L0_xattn_b2)[None],
        mask_rows(heads32(np.asarray(L1_xattn_bq)[None]), slice(24, 28), -BIG),
        mask_rows(heads32(np.asarray(L1_xattn_bk)[None]), slice(28, 32), BIG),
        np.asarray(L1_xattn_bv)[None], np.asarray(L1_xattn_bo)[None]], 1)
    bias = np.ascontiguousarray(np.repeat(bias, 2, 0))
    mb = np.concatenate([np.asarray(L1_ffn_b1), np.asarray(L1_ffn_b2)], 1)
    mbias = np.ascontiguousarray(np.concatenate([mb, mb], 0))
    ffw = np.ascontiguousarray(np.stack([
        np.asarray(L0_ffn_w_gate).T, np.asarray(L0_ffn_w_up).T,
        np.asarray(L0_ffn_w_down).T.reshape(HC, P, D).transpose(1, 0, 2).reshape(P, HC * D)], 1))
    weights = np.ascontiguousarray(np.concatenate([
        np.asarray(L0_xattn_wq), np.asarray(L0_xattn_wk), np.asarray(L0_xattn_wv), np.asarray(L0_xattn_wo),
        np.asarray(L0_xattn_w1), np.asarray(L0_xattn_w2).reshape(HC, P, D).transpose(1, 0, 2).reshape(P, HC * D),
        heads32(np.asarray(L1_xattn_Wk)), np.asarray(L1_xattn_Wv), heads32(np.asarray(L1_xattn_Wq)), np.asarray(L1_xattn_Wo),
        np.asarray(L1_ffn_W1).transpose(1, 0, 2).reshape(P, NE * EH),
        np.asarray(L1_ffn_W2).reshape(NE, EC, P, D).transpose(2, 1, 0, 3).reshape(P, EC * NE * D)], 1))

    arrays = {"x": x_rows, "ctx_rows": ctx_rows, "ctx_cols": ctx_cols, "mask": mask, "consts": consts, "pos": pos,
              "gamma": np.ascontiguousarray(np.asarray(L0_xattn_gamma)),
              "beta": np.ascontiguousarray(np.asarray(L0_xattn_beta)),
              "bias": bias, "mbias": mbias, "ffw": ffw, "weights": weights}
    nc = bacc.Bacc("TRN2", target_bir_lowering=False, num_devices=1)
    args = [nc.dram_tensor(f"{n}_dram", a.shape, mybir.dt.from_np(a.dtype), kind="ExternalInput").ap()
            for n, a in arrays.items()]
    out = nc.dram_tensor("out_dram", (B, P, TILES, D), F32, kind="ExternalOutput").ap()
    build_program(nc, *args, out)
    r = run_bass_kernel_spmd(nc, [{f"{n}_dram": a for n, a in arrays.items()}], core_ids=[0])
    got = r.results[0]["out_dram"]
    return np.ascontiguousarray(got.transpose(0, 2, 1, 3).reshape(B, T, D))
```

```python
from contextlib import ExitStack

import concourse.bass as bass
import numpy as np
from concourse import mybir

F32, F16, BF16 = mybir.dt.float32, mybir.dt.float16, mybir.dt.bfloat16
I32, U32 = mybir.dt.int32, mybir.dt.uint32
ACT = mybir.ActivationFunctionType
ALU = mybir.AluOpType
AX = mybir.AxisListType

P = 128
B, T, D = 4, 256, 128
TILES = T // P
WINDOW = 32
HID = 512
HC = HID // P
NH, DK = 16, 8
PRING = 8
KRING = 4
QUADS = NH // 4
NE, EH, NG = 8, 256, 16
EC = EH // P
EPS = 1e-5
MAGIC = 12582912.0
BIG = 61440.0
GU_ORDER = [(pair + i, t) for pair in range(0, B, 2) for t in range(TILES) for i in range(2)]
OUT_PAIRS = (0, 1, 0, 1, 2, 3, 0, 1)
PASSES = ((0, 0), (0, 1), (1, 0))

SEGS = [("qkv", 3 * D), ("wo", D), ("w1", HID), ("w2", HID), ("wk", QUADS * P), ("wv", D), ("wq", QUADS * P),
        ("wo1", D), ("m1", NE * EH), ("m2", EC * NE * D)]
SEG = {}
NW = 0
for _name, _n in SEGS:
    SEG[_name] = (NW, NW + _n)
    NW += _n
BSEGS = [("qkv", 3 * D), ("bo", D), ("b1", HID), ("b2", D), ("bq", QUADS * P), ("bk", QUADS * P), ("bv", D), ("bo1", D)]
BSEG = {}
NB = 0
for _name, _n in BSEGS:
    BSEG[_name] = (NB, NB + _n)
    NB += _n
BPARTS = (BSEG["qkv"], (BSEG["qkv"][1], NB))
CSEGS = [("ident", P), ("iota", 2 * NE), ("lo_q", 1), ("lo_k", 1), ("lo_2", 1), ("lo_16", 1), ("sel", P),
         ("band", 2 * T), ("cols", 3), ("wredT", P), ("wgT", NE)]
CSEG = {}
NC_ = 0
for _name, _n in CSEGS:
    CSEG[_name] = (NC_, NC_ + _n)
    NC_ += _n

LN_IN, LN_A, LN_OUT, LN_FFN, LN_ATT, LN_MOE = range(6)
NLN = 6
R_IN, R_ATT, R_MOE = range(3)
NMR_TURN = {LN_A: 0, LN_FFN: 1}
T_EMB, T_Y, T_A, T_QUANT, T_QUERY, T_ATTN, T_MOE = range(7)
C_EMB, C_Y, C_A, C_QUERY, C_ATTN, C_MOE = range(6)


def nth(stage, b):
    return stage * B + b + 1


SIGNALS = """
l_x0 l_x1 l_x2 l_x3 l_ctx l_cst l_pos l_gb l_bias l_mbias l_ctxT l_mask l_ffw l_out l_qkv l_wo l_w1 l_w2 l_wk
l_wv l_wq l_wo1 l_m1 l_m2 ones_ready id_ready bias_hi bias_ready bias_neg bias_rest mbias_hi mbias_ready zeros_ready w_hi w_lo
w_lo_pool absum means_ready meanc ffscale ffw_r ffw_c ffw_ready kscale pos_masked pos_max ew_done ewT_mm ewT_hi
ewT_ready wgsq   router_ready mask_ind count_mm colmask resmask flagsum flag_ready ctxT_hi
ctxT_ready kproj ka_hi ka_ready vproj va_ready kz_zero kz_ready emb kT_mm kmax kmaxb kdiag kshift ek ekv eb_hi eb_lo numden 
ysig y attn_mm  hid_mm hid_hi hid_ready ff_mm xb nb x1 amax amaxc  ascale q1 q1T_ready gscale gu_mm
silu g q2 q2_act q2T_mm q2T_ready down_mm x2 q_mm qa_hi qa_ready s_mm smax spread shift_mm qb st_mm probs pv oT
oR_mm oden attn wo1_mm x3 logit_mm top8 topix onehot expsum score wsel ohT_mm ohT oh_mm oh xm_hi xm moe_h
gelu gelu_hi gelu_ready moe_o picked picksum y0 y_out turned cols_hi cols_ready ln_moments ln_vareps ln_rstd
ln_stats rows_ready rows_act ln_nmr router_step flagstep
""".split()


def build_program(nc, x, ctx_rows, ctx_cols, mask, consts, pos, gamma, beta, bias, mbias, ffw, weights, out):
    scope = ExitStack()
    with scope:
        def sb(name, shape, dt=F32):
            return scope.enter_context(nc.sbuf_tensor(name, shape, dt))

        sig = {n: scope.enter_context(nc.semaphore(n)) for n in SIGNALS}
        ps = scope.enter_context(nc.psum_tensor("ps", [P, 8, 512], F32))

        x_in = sb("x_in", [P, B, TILES, D])
        ctx_in = sb("ctx_in", [P, B, TILES, D])
        cst = sb("cst", [P, NC_])
        gamma_b = sb("gamma_b", [P, D])
        beta_b = sb("beta_b", [P, D])
        bias16 = sb("bias16", [2, NB], F16)
        mbias16 = sb("mbias16", [2 * NE, EH + D], F16)
        wf = sb("wf", [P, HID + SEG["m1"][0]])
        stage = sb("stage", [P, NE * EH])
        mask_in = wf[:, 0:B * TILES * T].bitcast(I32).rearrange("p (b t n) -> p b t n", b=B, t=TILES)
        w16 = sb("w16", [P, 2, NW], F16)
        ffw16 = sb("ffw16", [P, 3, HID], F16)
        ident = cst[:, CSEG["ident"][0]:CSEG["ident"][1]]
        id16 = sb("id16", [P, P], F16)
        idbig = sb("idbig", [P, P], BF16)
        sel16 = sb("sel16", [1, P], F16)
        ones32 = sb("ones32", [P, P])
        ones16 = sb("ones16", [P, T], F16)
        all_masked = sb("all_masked", [P, 2])
        mask_sums = sb("mask_sums", [P, 4])
        silu_junk = sb("silu_junk", [P, 1])
        halfs = sb("halfs", [P, 2 * NE])
        roots = sb("roots", [P, NE])
        minus_ones = sb("minus_ones", [P, NE])

        def c(name, rows=P):
            a, b_ = CSEG[name]
            return cst[0:rows, a:b_]

        def wf32(name):
            a, b_ = SEG[name]
            return stage[:, :] if name in ("m1", "m2") else wf[:, HID + a:HID + b_]

        def w(name, part):
            a, b_ = SEG[name]
            return w16[:, part, a:b_]

        def brow(name):
            a, b_ = BSEG[name]
            return bias16[:, a:b_]

        bk_col = c("cols")[:, 0:1]
        gamma_col = c("cols")[:, 1:2]
        beta_col = c("cols")[:, 2:3]

        gate_pt = sb("gate_pt", [P, 12 * TILES * T])
        hid_xm = sb("hid_xm", [P, 2 * B * HC * T], F16)
        eb_oT = sb("eb_oT", [P, B * QUADS * T])
        half_b = sb("half_b", [P, B * QUADS * T], F16)
        half_c = sb("half_c", [P, B * QUADS * T], F16)
        def taken(buf, start, n, rows=P):
            return buf[0:rows, start:start + n]

        at = 0
        bias_in = taken(gate_pt, 0, NB, 2)
        at += NB
        bias_h = taken(gate_pt, at, NB // 2, 2).bitcast(F16)
        at += NB // 2
        mbias_in = taken(gate_pt, at, EH + D, 2 * NE)
        at += EH + D
        mbias_h = taken(gate_pt, at, (EH + D) // 2, 2 * NE).bitcast(F16)
        at += (EH + D) // 2
        junk = taken(gate_pt, at, HID)
        at += HID
        ctxT_in = taken(gate_pt, at, B * T).rearrange("p (b n) -> p b n", b=B)
        at += B * T
        gelu32 = taken(gate_pt, 0, B * EC * T).rearrange("p (b c n) -> p b c n", b=B, c=EC)
        picked = taken(gate_pt, B * EC * T, 2 * NE * D).rearrange("p (k e n) -> p k e n", k=2, e=NE)

        absum = sb("absum", [P, 3])
        mean = sb("mean", [P, 3])
        wscale = sb("wscale", [P, 3])
        posmax = sb("posmax", [P, TILES])
        ewT = sb("ewT", [P, 2, TILES, T], F16)
        wgsq = sb("wgsq", [NG, NE])
        wnorm = sb("wnorm", [P, 5, NE])
        router = sb("router", [P, NE])
        router16 = sb("router16", [P, 2, NE], F16)
        colrow = sb("colrow", [1, B, T], F16)
        flag_f = sb("flag_f", [1, 3])
        flag_i = sb("flag_i", [1, 1], I32)
        ka = sb("ka", [P, B, QUADS, T], F16)

        stats = sb("stats", [P, NLN, B, TILES, 6])
        moments = sb("moments", [P, NLN, B, TILES, 2])
        vareps = sb("vareps", [P, NLN, B, TILES])
        rstd = sb("rstd", [P, NLN, B, TILES])
        nmean = sb("nmean", [P, NLN, B, TILES])
        nmr = sb("nmr", [P, NLN, B, TILES])
        rows = sb("rows", [P, B, TILES, D])
        emb = sb("emb", [P, B, TILES, D])
        colsA = sb("colsA", [P, 2, B, T], F16)
        y_mem = sb("y_mem", [P, B * T])
        posw = y_mem[:, 0:TILES * T].rearrange("p (t n) -> p t n", t=TILES)
        ew = y_mem[:, TILES * T:2 * TILES * T].rearrange("p (t n) -> p t n", t=TILES)
        colsY = y_mem[:, :].bitcast(F16).rearrange("p (a b n) -> p a b n", a=2, b=B)
        ctxT = colsY
        n_mem = sb("n_mem", [P, 2 * B * T])
        ffw_in = n_mem[:, 0:3 * HID].rearrange("p (k n) -> p k n", k=3)
        colsN = n_mem[:, 0:B * T].bitcast(F16).rearrange("p (a b n) -> p a b n", a=2, b=B)
        a32_mem = n_mem[:, B * T:2 * B * T]
        a32 = a32_mem.rearrange("p (b n) -> p b n", b=B)
        kmx = sb("kmx", [P, B, 2])
        th = sb("th", [P, B, TILES, D])
        half = B * TILES * 2 * D
        eb = eb_oT[:, 0:half].rearrange("p (b t n) -> p b t n", b=B, t=TILES)
        oT = eb_oT[:, :].rearrange("p (b q n) -> p b q n", b=B, q=QUADS)
        g = gate_pt[:, 0:B * TILES * HID].rearrange("p (b t n) -> p b t n", b=B, t=TILES)
        silu = gate_pt[:, B * TILES * HID:].rearrange("p (b n) -> p b n", b=B)
        pt = taken(gate_pt, 0, PRING * TILES * T).rearrange("p (k t n) -> p k t n", k=PRING, t=TILES)
        hid16 = hid_xm[:, :].rearrange("p (a b c n) -> p a b c n", a=2, b=B, c=HC)
        va = hid_xm[:, :].bitcast(F32).rearrange("p (b t h k) -> p b t h k", b=B, t=TILES, h=NH)
        eb16 = hid_xm[:, 0:2 * half].rearrange("p (a b t n) -> p a b t n", a=2, b=B, t=TILES)
        qh = eb_oT[:, 0:half].bitcast(F16).rearrange("p (b h n) -> p b h n", b=B, h=QUADS)
        resmask = wf[:, B * TILES * T:B * TILES * T + B * T].bitcast(BF16).rearrange("p (b t n) -> p b t n", b=B, t=TILES)
        gT = half_b[:, :].rearrange("p (b t c n) -> p b t c n", b=B, t=TILES, c=HC)
        kh = a32_mem[:, :].bitcast(F16).rearrange("p (b h n) -> p b h n", b=B, h=2)
        oh = half_b[:, :].rearrange("p (a e n) -> p a e n", a=2, e=NE)
        qa = half_c[:, :].rearrange("p (b h n) -> p b h n", b=B, h=QUADS)
        gelu16 = half_c[:, :].rearrange("p (a b c n) -> p a b c n", a=2, b=B, c=EC)
        xm = hid_xm[:, :].rearrange("p (a b e n) -> p a b e n", a=2, b=2, e=NE)
        rden = sb("rden", [P, B, TILES, D])
        y = sb("y", [P, B, TILES, D])
        xb, x1, x2 = x_in, emb, y
        attn, y0, x3, nb, res = th, rden, xb, ctx_in, ctx_in
        ind = rden[:, :, :, :].rearrange("p b t n -> p (b t n)").bitcast(BF16).rearrange("p (b t n) -> p b t n", b=B, t=TILES)
        cnt = th[:, :, :, :].rearrange("p b t n -> p (b t n)")
        colmask = colsA[:, 0]
        colmask = colmask.rearrange("p b n -> p (b n)").bitcast(BF16).rearrange("p (b n) -> p b n", b=B)
        amax = sb("amax", [P, B, 4, TILES])
        fac = sb("fac", [P, B, 3, TILES])
        qd_mem = sb("qd_mem", [P, B * P])
        kdiag = qd_mem[:, :].rearrange("p (b n) -> p b n", b=B)
        qT = qd_mem[:, :].bitcast(F16).rearrange("p (b n) -> p b n", b=B)
        kz = taken(gate_pt, PRING * TILES * T, KRING * 4 * T // 2).bitcast(F16).rearrange(
            "p (r h n) -> p r h n", r=KRING, h=4)
        mx = sb("mx", [P, B, NH, TILES])
        spread = sb("spread", [P, 2, TILES, P], F16)
        qb = sb("qb", [P, 2, T], F16)
        oden = sb("oden", [P, B, TILES, NH])
        top8 = sb("top8", [P, B, TILES, 8])
        topix = sb("topix", [P, B, TILES, 8], U32)
        ntop = sb("ntop", [P, B, TILES])
        onehot = sb("onehot", [P, B, TILES, 2 * NE], F16)
        ejunk = sb("ejunk", [P, B, TILES, NE])
        esum = sb("esum", [P, B, TILES])
        score = sb("score", [P, B, TILES])
        wsel = sb("wsel", [P, B, TILES, NE])
        ohT = sb("ohT", [2 * NE, B, T], F16)
        picksum = sb("picksum", [P, 2, D])

        def bank(b, k):
            return ps[:, 2 * b + k, :]

        def score_bank(u):
            return ps[:, (0, 1, 7)[u % 3], :]

        def pair(b):
            return ps[:, 2 * b:2 * b + 2, :]

        block = scope.enter_context(nc.Block())

        @block.sync
        def _(sp):
            for b in range(B):
                sp.dma_start(x_in[:, b], x[b]).then_inc(sig[f"l_x{b}"], 16)
            sp.dma_start(cst[:, :], consts).then_inc(sig["l_cst"], 16)
            for name in ("qkv", "wo"):
                a, z = SEG[name]
                sp.dma_start(wf32(name), weights[:, a:z]).then_inc(sig["l_" + name], 16)
            sp.dma_start(posw[:, :, :], pos).then_inc(sig["l_pos"], 16)
            sp.dma_start(ffw_in[:, :, :], ffw).then_inc(sig["l_ffw"], 16)
            sp.dma_start(ctxT_in, ctx_cols).then_inc(sig["l_ctxT"], 16)
            for name in ("wk", "wv"):
                a, z = SEG[name]
                sp.dma_start(wf32(name), weights[:, a:z]).then_inc(sig["l_" + name], 16)
            for name in ("w1", "w2", "wq", "wo1", "m1"):
                a, z = SEG[name]
                sp.dma_start(wf32(name), weights[:, a:z]).then_inc(sig["l_" + name], 16)
            sp.wait_ge(sig["w_lo"], 2)
            sp.wait_ge(sig["w_lo_pool"], 2)
            sp.dma_start(mask_in, mask).then_inc(sig["l_mask"], 16)
            sp.wait_ge(sig["w_lo_pool"], 7)
            sp.dma_start(wf32("m2"), weights[:, SEG["m2"][0]:SEG["m2"][1]]).then_inc(sig["l_m2"], 16)
            for b in range(B):
                sp.wait_ge(sig["y_out"], TILES * (b + 1))
                sp.dma_start(out[b], res[:, b]).then_inc(sig["l_out"], 16)
            sp.wait_ge(sig["l_out"], 16 * B)

        @block.gpsimd
        def _(pool):
            nc.gpsimd.memset(ones32[:, :], 1.0)
            nc.gpsimd.memset(ones16[:, :], 1.0)
            nc.gpsimd.memset(halfs[:, :], -0.5)
            nc.gpsimd.memset(minus_ones[:, :], -1.0)
            nc.gpsimd.memset(all_masked[:, 0:1], -(T - 1) * BIG)
            nc.gpsimd.memset(all_masked[:, 1:2], -(T - 1) * 4 * BIG)
            nc.gpsimd.memset(roots[:, :], 0.5).then_inc(sig["ones_ready"], 1)
            pool.wait_ge(sig["ones_ready"], 1)

            def rstd_of(ln, b):
                pool.wait_ge(sig["ln_moments"], nth(ln, b))
                if ln in NMR_TURN:
                    nc.gpsimd.tensor_scalar(nmean[:, ln, b, :], moments[:, ln, b, :, 0], -1.0, 0.0, ALU.mult, ALU.add)
                nc.gpsimd.tensor_scalar(vareps[:, ln, b, :], moments[:, ln, b, :, 1], EPS, 1.0, ALU.add,
                                        ALU.mult).then_inc(sig["ln_vareps"], 1)
                pool.wait_ge(sig["ln_vareps"], nth(ln, b))
                nc.gpsimd.tensor_tensor(rstd[:, ln, b, :], vareps[:, ln, b, :], halfs[:, 0:TILES],
                                        ALU.pow).then_inc(sig["ln_rstd"], 1)

            def rows_shift(ln, b):
                pool.wait_ge(sig["ln_rstd"], nth(ln, b))
                nc.gpsimd.tensor_tensor(nmr[:, ln, b, :], nmean[:, ln, b, :], rstd[:, ln, b, :], ALU.mult)\
                    .then_inc(sig["ln_nmr"], 1)

            def split_lo(name, n):
                a, z = SEG[name]
                pool.wait_ge(sig["w_hi"], n)
                nc.gpsimd.tensor_tensor(w16[:, 1, a:z], wf32(name), w16[:, 0, a:z], ALU.subtract)\
                    .then_inc(sig["w_lo_pool"], 1)

            for b in range(B):
                rstd_of(LN_IN, b)
            pool.wait_ge(sig["l_ctx"], 16)
            for b in range(B):
                pool.wait_ge(sig["rows_ready"], nth(R_IN, b))
                nc.gpsimd.tensor_tensor(emb[:, b], rows[:, b], ctx_in[:, b], ALU.add).then_inc(sig["emb"], 1)
            pool.wait_ge(sig["l_pos"], 16)
            pool.wait_ge(sig["l_cst"], 16)
            nc.gpsimd.tensor_tensor(posw[:, :, :], posw[:, :, :], c("band").rearrange("p (a n) -> p a n", a=TILES),
                                    ALU.mult).then_inc(sig["pos_masked"], 1)
            nc.gpsimd.tensor_tensor(wgsq[:, :], c("wgT", NG), c("wgT", NG), ALU.mult).then_inc(sig["wgsq"], 1)
            pool.wait_ge(sig["l_gb"], 32)
            pool.wait_ge(sig["rows_ready"], nth(R_IN, B - 1))
            for b in range(B):
                for t in range(TILES):
                    ins = nc.gpsimd.tensor_tensor(xb[:, b, t], x_in[:, b, t], beta_b[:, :], ALU.add)
                ins.then_inc(sig["xb"], 1)
            cols = slice(*BPARTS[1])
            pool.wait_ge(sig["bias_hi"], 2)
            nc.gpsimd.tensor_scalar(bias16[:, cols], bias_h[:, cols], c("lo_2", 2), 0.0, ALU.mult, ALU.add)\
                .then_inc(sig["bias_neg"], 1)
            pool.wait_ge(sig["bias_neg"], 1)
            nc.gpsimd.tensor_tensor(bias16[:, cols], bias16[:, cols], bias_in[:, cols], ALU.add).then_inc(sig["bias_rest"], 1)
            pool.wait_ge(sig["meanc"], 1)
            nc.gpsimd.tensor_tensor(wnorm[:, 2], wnorm[:, 1], roots[:, :], ALU.pow).then_inc(sig["router_step"], 1)
            pool.wait_ge(sig["router_step"], 1)
            nc.gpsimd.tensor_scalar(wnorm[:, 3], wnorm[:, 2], 1e-4, 1.0, ALU.max, ALU.mult).then_inc(sig["router_step"], 1)
            pool.wait_ge(sig["router_step"], 2)
            nc.gpsimd.tensor_tensor(wnorm[:, 4], wnorm[:, 3], minus_ones[:, :], ALU.pow).then_inc(sig["router_step"], 1)
            pool.wait_ge(sig["router_step"], 3)
            nc.gpsimd.tensor_tensor(router[:, :], wnorm[:, 0], wnorm[:, 4], ALU.mult).then_inc(sig["router_step"], 1)
            pool.wait_ge(sig["router_step"], 4)
            nc.gpsimd.tensor_scalar(router16[:, 0], router[:, :], 1.0, 0.0, ALU.mult, ALU.add).then_inc(sig["router_step"], 1)
            pool.wait_ge(sig["router_step"], 5)
            nc.gpsimd.tensor_tensor(router16[:, 1], router[:, :], router16[:, 0], ALU.subtract)\
                .then_inc(sig["router_ready"], 1)
            split_lo("w1", 3)
            split_lo("w2", 4)
            split_lo("wk", 5)
            split_lo("wv", 6)
            split_lo("wq", 7)
            split_lo("wo1", 8)
            for b in range(B):
                pool.wait_ge(sig["ysig"], b + 1)
                nc.gpsimd.tensor_tensor(y[:, b], th[:, b], rden[:, b], ALU.mult).then_inc(sig["y"], 1)
            for b in range(B):
                rstd_of(LN_A, b)
                rows_shift(LN_A, b)
            pool.wait_ge(sig["ctxT_hi"], 1)
            nc.gpsimd.tensor_tensor(ctxT[:, 1], ctxT_in, ctxT[:, 0], ALU.subtract).then_inc(sig["ctxT_ready"], 1)
            for b in range(B):
                rstd_of(LN_OUT, b)
            for b in range(B):
                rstd_of(LN_FFN, b)
                rows_shift(LN_FFN, b)
            pool.wait_ge(sig["colmask"], 1)
            nc.gpsimd.tensor_scalar(resmask[:, :, :, :].rearrange("p a t n -> p (a t n)"),
                                    ind[:, :, :, :].rearrange("p a t n -> p (a t n)"), -4 * BIG, 0.0, ALU.mult, ALU.add)\
                .then_inc(sig["resmask"], 1)
            pool.wait_ge(sig["resmask"], 1)
            for b in range(B):
                ins = nc.gpsimd.tensor_tensor(resmask[:, b], resmask[:, b], colmask[:, b].unsqueeze(1).to_broadcast(
                    [P, TILES, T]), ALU.add)
            ins.then_inc(sig["resmask"], 1)
            nc.gpsimd.memset(spread[:, :, :, :], 0.0)
            pool.wait_ge(sig["ff_mm"], B)
            nc.gpsimd.memset(va[:, :, :, :, DK:32], 0.0).then_inc(sig["zeros_ready"], 1)
            pool.wait_ge(sig["zeros_ready"], 1)
            nc.gpsimd.memset(va[:, :, :, :, DK:DK + 1], 1.0).then_inc(sig["zeros_ready"], 1)
            split_lo("m1", 9)
            for b in range(B):
                pool.wait_ge(sig["ascale"], nth(1, b))
                nc.gpsimd.tensor_scalar(g[:, b, 0], g[:, b, 0], amax[:, b, 3, 0:1], MAGIC, ALU.mult, ALU.add)\
                    .then_inc(sig["q2"], 1)
            for b in range(B):
                rstd_of(LN_ATT, b)
            nc.gpsimd.memset(kz[:, :, :, :], 0.0).then_inc(sig["kz_zero"], 1)
            pool.wait_ge(sig["kz_zero"], 1)
            for n in range(B * QUADS):
                b, quad = divmod(n, QUADS)
                pool.wait_ge(sig["ka_ready"], B + b + 1)
                if n >= KRING:
                    pool.wait_ge(sig["st_mm"], 4 * (n - KRING + 1))
                for k in range(4):
                    part = slice(32 * k, 32 * k + 32)
                    ins = nc.gpsimd.tensor_scalar(kz[part, n % KRING, k], ka[part, b, quad], 1.0, 0.0, ALU.mult, ALU.add)
                ins.then_inc(sig["kz_ready"], 1)
                if n == 6:
                    pool.wait_ge(sig["kz_ready"], n + 1)
                    split_lo("m2", 10)
                    pool.wait_ge(sig["w_lo_pool"], 8)
            for b in range(B):
                rstd_of(LN_MOE, b)

        @block.scalar
        def _(act):
            nc_act = nc.scalar.activation
            act.dma_start(ctx_in[:, :, :, :], ctx_rows).then_inc(sig["l_ctx"], 16)
            act.dma_start(gamma_b[:, :], gamma.partition_broadcast(P)).then_inc(sig["l_gb"], 16)
            act.dma_start(beta_b[:, :], beta.partition_broadcast(P)).then_inc(sig["l_gb"], 16)
            act.dma_start(bias_in[:, :], bias).then_inc(sig["l_bias"], 16)
            act.dma_start(mbias_in[:, :], mbias).then_inc(sig["l_mbias"], 16)

            def split_hi(name):
                a, z = SEG[name]
                act.wait_ge(sig["l_" + name], 16)
                nc_act(w16[:, 0, a:z], wf32(name), ACT.Copy).then_inc(sig["w_hi"], 1)

            split_hi("qkv")
            act.wait_ge(sig["l_bias"], 16)

            def bias_hi(k):
                cols = slice(*BPARTS[k])
                nc_act(bias_h[:, cols], bias_in[:, cols], ACT.Copy).then_inc(sig["bias_hi"], 1)

            bias_hi(0)
            for b in range(B):
                act.wait_ge(sig["turned"], nth(T_EMB, b))
                nc_act(colsA[:, 0, b], bank(b, 0)[:, 0:T], ACT.Copy).then_inc(sig["cols_hi"], 1)
            act.wait_ge(sig["pos_max"], 1)
            for t in range(TILES):
                nc_act(ew[:, t], posw[:, t], ACT.Exp, bias=posmax[:, t:t + 1]).then_inc(sig["ew_done"], 1)
            bias_hi(1)
            act.wait_ge(sig["ewT_mm"], 1)
            nc_act(ewT[:, 0], bank(3, 1).rearrange("p (a n) -> p a n", a=TILES), ACT.Copy).then_inc(sig["ewT_hi"], 1)
            split_hi("wo")
            act.wait_ge(sig["l_ffw"], 16)
            for k in range(3):
                if k:
                    act.wait_ge(sig["absum"], k)
                nc_act(junk[:, :], ffw_in[:, k], ACT.Abs, accum_out=absum[:, k:k + 1]).then_inc(sig["absum"], 1)
            for b in range(B):
                act.wait_ge(sig["kshift"], b + 1)
                qk = bank(b, 0).rearrange("p (t n) -> p t n", t=TILES)
                nc_act(th[:, b], qk[:, :, 0:D], ACT.Tanh, scale=0.5)
                nc_act(eb[:, b, :, D:2 * D], qk[:, :, D:2 * D], ACT.Exp).then_inc(sig["ek"], 1)
            for b in range(B):
                act.wait_ge(sig["ekv"], b + 1)
                nc_act(eb16[:, 0, b], eb[:, b], ACT.Copy).then_inc(sig["eb_hi"], 1)
            act.wait_ge(sig["l_mbias"], 16)
            nc_act(mbias_h[:, :], mbias_in[:, :], ACT.Copy).then_inc(sig["mbias_hi"], 1)
            for name in ("w1", "w2", "wk", "wv", "wq", "wo1"):
                split_hi(name)
            for b in range(B):
                act.wait_ge(sig["turned"], nth(T_Y, b))
                nc_act(colsY[:, 0, b], bank(b, 1)[:, 0:T], ACT.Copy).then_inc(sig["cols_hi"], 1)

            def act_rows(ln, b, src):
                act.wait_ge(sig["ln_nmr"], NMR_TURN[ln] * B + b + 1)
                for t in range(TILES):
                    ins = nc_act(rows[:, b, t], src(t), ACT.Identity, scale=rstd[:, ln, b, t:t + 1],
                                 bias=nmr[:, ln, b, t:t + 1])
                ins.then_inc(sig["rows_act"], 1)

            for b in range(B):
                act_rows(LN_A, b, lambda t: bank(b, 0)[:, t * D:(t + 1) * D])
            act.wait_ge(sig["ffw_ready"], 3)
            for b in range(B):
                act.wait_ge(sig["turned"], nth(T_A, b))
                nc_act(a32[:, b], bank(b, 1)[:, 0:T], ACT.Identity, scale=gamma_col, bias=beta_col)
                nc_act(colsN[:, 0, b], bank(b, 1)[:, 0:T], ACT.Identity, scale=gamma_col, bias=beta_col)\
                    .then_inc(sig["cols_hi"], 1)
            act.wait_ge(sig["l_ctxT"], 16)
            nc_act(ctxT[:, 0], ctxT_in, ACT.Copy).then_inc(sig["ctxT_hi"], 1)
            for b in range(B):
                act.wait_ge(sig["hid_mm"], b + 1)
                nc_act(hid16[:, 0, b], pair(b), ACT.Relu).then_inc(sig["hid_hi"], 1)
            act.wait_ge(sig["count_mm"], 1)
            act.wait_ge(sig["ones_ready"], 1)
            for a in range(2):
                cols = slice(2 * a, 2 * a + 2)
                nc_act(colrow[:, cols].rearrange("p b n -> p (b n)"), bank(a, 1)[0:1], ACT.Relu, scale=BIG,
                       bias=all_masked[0:1, 0:1])
                nc_act(colmask[:, cols].rearrange("p b n -> p (b n)"), bank(a, 1), ACT.Relu, scale=4 * BIG,
                       bias=all_masked[:, 1:2], accum_out=mask_sums[:, 2 * a:2 * a + 1])
                ins = nc_act(cnt[:, a * 2 * T:(a + 1) * 2 * T], bank(a, 1), ACT.Copy, accum_out=mask_sums[:, 2 * a + 1:2 * a + 2])
            ins.then_inc(sig["colmask"], 1)
            split_hi("m1")
            nc_act(silu_junk[:, :], all_masked[:, 0:1], ACT.Silu)

            def key_hi(b, half_no):
                act.wait_ge(sig["kproj"], half_no * B + b + 1)
                nc_act(kh[:, b].rearrange("p h n -> p (h n)"), bank(b, 1), ACT.Copy).then_inc(sig["ka_hi"], 1)

            for b in range(B):
                act.wait_ge(sig["vproj"], b + 1)
                for t in range(TILES):
                    ins = nc_act(va[:, b, t, :, 0:DK],
                                 bank(b, 1)[:, t * D:(t + 1) * D].rearrange("p (h k) -> p h k", h=NH), ACT.Copy)
                ins.then_inc(sig["va_ready"], 1)
            for b in range(B):
                key_hi(b, 0)
                act_rows(LN_FFN, b, lambda t: x1[:, b, t])
            for b in range(B):
                act.wait_ge(sig["ascale"], nth(0, b))
                for t in range(TILES):
                    ins = nc_act(rows[:, b, t], rows[:, b, t], ACT.Copy, scale=amax[:, b, 1, t:t + 1], bias=MAGIC)
                ins.then_inc(sig["q1"], 1)
            for b in range(B):
                act.wait_ge(sig["turned"], nth(T_QUANT, b))
                nc_act(qT[:, b], bank(b, 1)[:, 0:T], ACT.Copy, bias=-MAGIC).then_inc(sig["q1T_ready"], 1)

            def round_gated(b):
                act.wait_ge(sig["ascale"], nth(1, b))
                nc_act(g[:, b, 1], g[:, b, 1], ACT.Copy, scale=amax[:, b, 3, 1:2], bias=MAGIC).then_inc(sig["q2_act"], 1)

            for u, (b, t) in enumerate(GU_ORDER):
                act.wait_ge(sig["gu_mm"], u + 1)
                act.wait_ge(sig["gscale"], b + 1)
                if t:
                    act.wait_ge(sig["g"], u - 1)
                nc_act(silu[:, b], bank(b, 0), ACT.Silu, scale=fac[:, b, 0, t:t + 1]).then_inc(sig["silu"], 1)
                if (b, t) in ((2, 1), (3, 1)):
                    round_gated(b - 2)
            for b in range(2, B):
                round_gated(b)
            for b in range(B):
                act.wait_ge(sig["q2T_mm"], b + 1)
                nc_act(gT[:, b].rearrange("p t c n -> p (t c n)"), pair(b).rearrange("p a n -> p (a n)"), ACT.Copy,
                       bias=-MAGIC).then_inc(sig["q2T_ready"], 1)
            for b in range(B):
                key_hi(b, 1)
            act.wait_ge(sig["resmask"], 2)
            for b in range(B):
                act.wait_ge(sig["turned"], nth(T_QUERY, b))
                nc_act(colsA[:, 0, b], bank(b, 0)[:, 0:T], ACT.Copy).then_inc(sig["cols_hi"], 1)
            for b in range(B):
                act.wait_ge(sig["q_mm"], b + 1)
                nc_act(qh[:, b].rearrange("p h n -> p (h n)"), pair(b).rearrange("p a n -> p (a n)"), ACT.Copy)\
                    .then_inc(sig["qa_hi"], 1)
            split_hi("m2")
            def out_copy(m):
                act.wait_ge(sig["pv"], 2 * m + 2)
                b, half = divmod(m, 2)
                nc_act(oT[:, b, 2 * half:2 * half + 2].rearrange("p h n -> p (h n)"), ps[:, 4 + m % 2, :], ACT.Copy)\
                    .then_inc(sig["oT"], 1)

            for n in range(B * QUADS):
                for k in range(4):
                    head = 4 * n + k
                    act.wait_ge(sig["st_mm"], head + 1)
                    if head >= PRING:
                        act.wait_ge(sig["pv"], (head - PRING) // 4 + 1)
                    nc_act(pt[:, head % PRING].rearrange("p t n -> p (t n)"), ps[:, 2 + head % 2, :], ACT.Exp,
                           scale=DK ** -0.5).then_inc(sig["probs"], 1)
                if n >= 2 and n % 2 == 0:
                    out_copy(n // 2 - 1)
            out_copy(B * QUADS // 2 - 1)
            for b in range(B):
                act.wait_ge(sig["turned"], nth(T_ATTN, b))
                nc_act(colsY[:, 0, b], bank(b, 0)[:, 0:T], ACT.Copy).then_inc(sig["cols_hi"], 1)
            for b in range(B):
                act.wait_ge(sig["turned"], nth(T_MOE, b))
                nc_act(colsN[:, 0, b], bank(b, 0)[:, 0:T], ACT.Copy).then_inc(sig["cols_hi"], 1)
            def gate_sum(b):
                act.wait_ge(sig["topix"], b + 1)
                for t in range(TILES):
                    ins = nc_act(ejunk[:, b, t], bank(b, 1)[:, t * NE:(t + 1) * NE], ACT.Exp, bias=ntop[:, b, t:t + 1],
                                 accum_out=esum[:, b, t:t + 1])
                ins.then_inc(sig["expsum"], 1)
                act.wait_ge(sig["ohT_mm"], b + 1)
                nc_act(ohT[:, b], bank(b, 0)[0:2 * NE, 0:T], ACT.Copy).then_inc(sig["ohT"], 1)

            def onehot_copy(b):
                for half in range(2):
                    act.wait_ge(sig["oh_mm"], 2 * b + half + 1)
                    if b >= 2:
                        act.wait_ge(sig["xm"], b - 1)
                    nc_act(oh[:, b % 2, 4 * half:4 * half + 4].rearrange("p e n -> p (e n)"),
                           pair(b).rearrange("p a n -> p (a n)"), ACT.Copy).then_inc(sig["oh"], 1)

            gate_sum(0)
            gate_sum(1)
            onehot_copy(0)
            gate_sum(2)
            onehot_copy(1)
            gate_sum(3)
            for b in range(B):
                if b + 2 < B:
                    onehot_copy(b + 2)
                act.wait_ge(sig["moe_h"], b + 1)
                nc_act(gelu32[:, b].rearrange("p c n -> p (c n)"), bank(b, 0), ACT.Gelu).then_inc(sig["gelu"], 1)
                act.wait_ge(sig["gelu"], b + 1)
                nc_act(gelu16[:, 0, b], gelu32[:, b], ACT.Copy).then_inc(sig["gelu_hi"], 1)

        @block.vector
        def _(dve):
            V = nc.vector

            def ln_stats(ln, b, src):
                for t in range(TILES):
                    ins = V.bn_stats(stats[:, ln, b, t], src(t))
                ins.then_inc(sig["ln_stats"], 1)

            def ln_moments(ln, b):
                dve.wait_ge(sig["ln_stats"], nth(ln, b))
                for t in range(TILES):
                    ins = V.bn_aggr(moments[:, ln, b, t], stats[:, ln, b, t])
                ins.then_inc(sig["ln_moments"], 1)

            def ln_rows(ln, b, src):
                dve.wait_ge(sig["ln_rstd"], nth(ln, b))
                for t in range(TILES):
                    ins = V.tensor_scalar(rows[:, b, t], src(t), moments[:, ln, b, t, 0:1], rstd[:, ln, b, t:t + 1],
                                          ALU.subtract, ALU.mult)
                ins.then_inc(sig["rows_ready"], 1)

            def lo_part(dst, src, hi, done):
                V.tensor_tensor(dst, src, hi, ALU.subtract).then_inc(sig[done], 1)

            def split_lo(name, n):
                a, z = SEG[name]
                dve.wait_ge(sig["w_hi"], n)
                lo_part(w16[:, 1, a:z], wf32(name), w16[:, 0, a:z], "w_lo")

            for b in range(B):
                dve.wait_ge(sig[f"l_x{b}"], 16)
                ln_stats(LN_IN, b, lambda t: x_in[:, b, t])
                ln_moments(LN_IN, b)
            dve.wait_ge(sig["l_cst"], 16)
            V.tensor_copy(id16[:, :], ident)
            V.tensor_scalar(idbig[:, :], ident, BIG, None, ALU.mult)
            V.tensor_copy(sel16[:, :], c("sel", 1)).then_inc(sig["id_ready"], 1)
            for b in range(B):
                ln_rows(LN_IN, b, lambda t: x_in[:, b, t])
            split_lo("qkv", 1)
            cols = slice(*BPARTS[0])
            dve.wait_ge(sig["bias_hi"], 1)
            V.scalar_tensor_tensor(bias16[:, cols], bias_h[:, cols], c("lo_2", 2), bias_in[:, cols], ALU.mult, ALU.add)\
                .then_inc(sig["bias_ready"], 1)
            for b in range(B):
                dve.wait_ge(sig["cols_hi"], nth(C_EMB, b))
                lo_part(colsA[:, 1, b], bank(b, 0)[:, 0:T], colsA[:, 0, b], "cols_ready")
            dve.wait_ge(sig["pos_masked"], 1)
            V.tensor_reduce(posmax[:, :], posw[:, :, :], AX.X, ALU.max, negate=True).then_inc(sig["pos_max"], 1)
            for b in range(B):
                if b == 2:
                    dve.wait_ge(sig["ewT_hi"], 1)
                    lo_part(ewT[:, 1], bank(3, 1).rearrange("p (a n) -> p a n", a=TILES), ewT[:, 0], "ewT_ready")
                dve.wait_ge(sig["kT_mm"], b + 1)
                V.tensor_reduce(kmx[:, b, 0:1], bank(b, 1)[:, T:2 * T], AX.X, ALU.max).then_inc(sig["kmax"], 1)
                dve.wait_ge(sig["kmax"], b + 1)
                V.tensor_scalar(kmx[:, b, 1:2], kmx[:, b, 0:1], bk_col, -1.0, ALU.add, ALU.mult)\
                    .then_inc(sig["kmaxb"], 1)
                dve.wait_ge(sig["kmaxb"], b + 1)
                V.tensor_scalar(kdiag[:, b], ident, kmx[:, b, 1:2], None, ALU.mult).then_inc(sig["kdiag"], 1)
            split_lo("wo", 2)
            dve.wait_ge(sig["means_ready"], 1)
            V.tensor_copy(wnorm[:, 0:2], bank(3, 1)[:, T + NE:T + 3 * NE].rearrange("p (a n) -> p a n", a=2))
            V.tensor_scalar(mean[:, :], bank(3, 1)[:, T:T + 3], 1.0 / (HID * D), 1e-5, ALU.mult, ALU.max)\
                .then_inc(sig["meanc"], 1)
            dve.wait_ge(sig["meanc"], 1)
            V.reciprocal(wscale[:, :], mean[:, :]).then_inc(sig["ffscale"], 1)
            for b in range(B):
                dve.wait_ge(sig["ek"], b + 1)
                V.scalar_tensor_tensor(eb[:, b, :, 0:D], eb[:, b, :, D:2 * D], 0.5,
                                       bank(b, 1)[:, 0:2 * D].rearrange("p (t n) -> p t n", t=TILES), ALU.mult, ALU.mult)\
                    .then_inc(sig["ekv"], 1)
            for b in range(B):
                dve.wait_ge(sig["eb_hi"], b + 1)
                lo_part(eb16[:, 1, b], eb[:, b], eb16[:, 0, b], "eb_lo")
            for b in range(B):
                nd = bank(b, 0).rearrange("p (t n) -> p t n", t=TILES)
                dve.wait_ge(sig["numden"], b + 1)
                V.reciprocal(rden[:, b], nd[:, :, D:2 * D])
                V.scalar_tensor_tensor(th[:, b], th[:, b], 1.0, nd[:, :, 0:D], ALU.add, ALU.mult)\
                    .then_inc(sig["ysig"], 1)
            for b in range(B):
                dve.wait_ge(sig["cols_hi"], nth(C_Y, b))
                lo_part(colsY[:, 1, b], bank(b, 1)[:, 0:T], colsY[:, 0, b], "cols_ready")
            for b in range(B):
                dve.wait_ge(sig["attn_mm"], b + 1)
                ln_stats(LN_A, b, lambda t: bank(b, 0)[:, t * D:(t + 1) * D])
                ln_moments(LN_A, b)
            dve.wait_ge(sig["ffscale"], 1)
            for k in range(3):
                V.tensor_scalar(ffw_in[:, k], ffw_in[:, k], wscale[:, k:k + 1], MAGIC, ALU.mult, ALU.add)\
                    .then_inc(sig["ffw_r"], 1)
            for k in range(3):
                dve.wait_ge(sig["ffw_r"], k + 1)
                V.tensor_scalar(ffw_in[:, k], ffw_in[:, k], MAGIC + 1.0, MAGIC - 1.0, ALU.min, ALU.max)\
                    .then_inc(sig["ffw_c"], 1)
            for k in range(3):
                dve.wait_ge(sig["ffw_c"], k + 1)
                V.tensor_scalar(ffw16[:, k], ffw_in[:, k], MAGIC, None, ALU.subtract).then_inc(sig["ffw_ready"], 1)
            for b in range(B):
                dve.wait_ge(sig["cols_hi"], nth(C_A, b))
                lo_part(colsN[:, 1, b], a32[:, b], colsN[:, 0, b], "cols_ready")
            dve.wait_ge(sig["mbias_hi"], 1)
            V.scalar_tensor_tensor(mbias16[:, :], mbias_h[:, :], c("lo_16", 2 * NE), mbias_in[:, :], ALU.mult, ALU.add)\
                .then_inc(sig["mbias_ready"], 1)
            dve.wait_ge(sig["y"], B)
            dve.wait_ge(sig["l_mask"], 16)
            V.tensor_scalar(ind[:, :, :, :].rearrange("p a t n -> p (a t n)"), mask_in.rearrange("p a t n -> p (a t n)"),
                            0.0, None, ALU.is_equal).then_inc(sig["mask_ind"], 1)
            for b in range(B):
                dve.wait_ge(sig["hid_hi"], b + 1)
                V.scalar_tensor_tensor(hid16[:, 1, b].rearrange("p c n -> p (c n)"), pair(b).rearrange("p a n -> p (a n)"),
                                       0.0, hid16[:, 0, b].rearrange("p c n -> p (c n)"), ALU.max, ALU.subtract)\
                    .then_inc(sig["hid_ready"], 1)
            for b in range(B):
                dve.wait_ge(sig["ff_mm"], b + 1)
                ln_stats(LN_OUT, b, lambda t: bank(b, 0)[:, t * D:(t + 1) * D])
                ln_moments(LN_OUT, b)
            for b in range(B):
                dve.wait_ge(sig["xb"], b + 1)
                dve.wait_ge(sig["ln_moments"], nth(LN_OUT, b))
                for t in range(TILES):
                    ins = V.scalar_tensor_tensor(nb[:, b, t], bank(b, 0)[:, t * D:(t + 1) * D],
                                                 moments[:, LN_OUT, b, t, 0:1], gamma_b[:, :], ALU.subtract, ALU.mult)
                ins.then_inc(sig["nb"], 1)
            for b in range(B):
                dve.wait_ge(sig["nb"], b + 1)
                dve.wait_ge(sig["ln_rstd"], nth(LN_OUT, b))
                for t in range(TILES):
                    ins = V.scalar_tensor_tensor(x1[:, b, t], nb[:, b, t], rstd[:, LN_OUT, b, t:t + 1], xb[:, b, t],
                                                 ALU.mult, ALU.add)
                ins.then_inc(sig["x1"], 1)
                if b:
                    dve.wait_ge(sig["x1"], b)
                    ln_stats(LN_FFN, b - 1, lambda t: x1[:, b - 1, t])
                if b > 1:
                    ln_moments(LN_FFN, b - 2)
            dve.wait_ge(sig["x1"], B)
            ln_stats(LN_FFN, B - 1, lambda t: x1[:, B - 1, t])
            ln_moments(LN_FFN, B - 2)
            ln_moments(LN_FFN, B - 1)

            def key_lo(b, half_no):
                dve.wait_ge(sig["ka_hi"], half_no * B + b + 1)
                V.scalar_tensor_tensor(ka[:, b, 2 * half_no:2 * half_no + 2].rearrange("p h n -> p (h n)"),
                                       kh[:, b].rearrange("p h n -> p (h n)"), c("lo_k"), bank(b, 1), ALU.mult, ALU.add)\
                    .then_inc(sig["ka_ready"], 1)

            def quant_scale(b, row):
                dve.wait_ge(sig["amax"], B + 1 + GU_ORDER.index((b, 1)) if row else b + 1)
                V.tensor_scalar(amax[:, b, row, :], amax[:, b, row, :], 1e-5, 1.0 / 127.0, ALU.max, ALU.mult)\
                    .then_inc(sig["amaxc"], 1)
                dve.wait_ge(sig["amaxc"], nth(row // 2, b))
                V.reciprocal(amax[:, b, row + 1, :], amax[:, b, row, :]).then_inc(sig["ascale"], 1)

            for b in range(B):
                key_lo(b, 0)
                dve.wait_ge(sig["rows_act"], nth(NMR_TURN[LN_FFN], b))
                V.tensor_reduce(amax[:, b, 0, :], rows[:, b], AX.X, ALU.max, apply_absolute_value=True)\
                    .then_inc(sig["amax"], 1)
                if b:
                    quant_scale(b - 1, 0)
            quant_scale(B - 1, 0)
            for b in range(B):
                V.tensor_scalar(fac[:, b, 0, :], amax[:, b, 0, :], mean[:, 0:1], None, ALU.mult)
                V.tensor_scalar(fac[:, b, 1, :], amax[:, b, 0, :], mean[:, 1:2], None, ALU.mult).then_inc(sig["gscale"], 1)
            dve.wait_ge(sig["colmask"], 1)
            V.tensor_tensor(flag_f[:, 0:2], mask_sums[0:1, 0:2], mask_sums[0:1, 2:4], ALU.add).then_inc(sig["flagsum"], 1)
            dve.wait_ge(sig["flagsum"], 1)
            V.scalar_tensor_tensor(flag_f[:, 2:3], flag_f[:, 0:1], -T / (4 * BIG), flag_f[:, 1:2], ALU.mult, ALU.add)\
                .then_inc(sig["flagstep"], 1)
            dve.wait_ge(sig["flagstep"], 1)
            V.tensor_copy(flag_i[:, :], flag_f[:, 2:3]).then_inc(sig["flag_ready"], 1)
            def gate_max(u):
                b, t = GU_ORDER[u]
                dve.wait_ge(sig["g"], u + 1)
                V.tensor_reduce(amax[:, b, 2, t:t + 1], g[:, b, t], AX.X, ALU.max, apply_absolute_value=True)\
                    .then_inc(sig["amax"], 1)

            dve.wait_ge(sig["gscale"], B)
            for u, (b, t) in enumerate(GU_ORDER):
                dve.wait_ge(sig["silu"], u + 1)
                V.scalar_tensor_tensor(g[:, b, t], silu[:, b], fac[:, b, 1, t:t + 1], bank(b, 1), ALU.mult, ALU.mult)\
                    .then_inc(sig["g"], 1)
                if u:
                    gate_max(u - 1)
                if u == 4:
                    quant_scale(0, 2)
                if u == 5:
                    quant_scale(1, 2)
            gate_max(len(GU_ORDER) - 1)
            for b in range(2, B):
                quant_scale(b, 2)
            for b in range(B):
                V.tensor_scalar(fac[:, b, 2, :], amax[:, b, 2, :], mean[:, 2:3], None, ALU.mult).then_inc(sig["kscale"], 1)
            for b in range(B):
                dve.wait_ge(sig["down_mm"], b + 1)
                dve.wait_ge(sig["kscale"], b + 1)
                for t in range(TILES):
                    ins = V.scalar_tensor_tensor(x2[:, b, t], bank(b, 0)[:, t * D:(t + 1) * D], fac[:, b, 2, t:t + 1],
                                                 x1[:, b, t], ALU.mult, ALU.add)
                ins.then_inc(sig["x2"], 1)
                if b:
                    dve.wait_ge(sig["x2"], b)
                    ln_stats(LN_ATT, b - 1, lambda t: x2[:, b - 1, t])
                if b > 1:
                    ln_moments(LN_ATT, b - 2)
            dve.wait_ge(sig["x2"], B)
            ln_stats(LN_ATT, B - 1, lambda t: x2[:, B - 1, t])
            ln_moments(LN_ATT, B - 2)
            ln_moments(LN_ATT, B - 1)
            for b in range(B):
                ln_rows(LN_ATT, b, lambda t: x2[:, b, t])
            for b in range(B):
                key_lo(b, 1)
                dve.wait_ge(sig["cols_hi"], nth(C_QUERY, b))
                lo_part(colsA[:, 1, b], bank(b, 0)[:, 0:T], colsA[:, 0, b], "cols_ready")
            for b in range(B):
                dve.wait_ge(sig["qa_hi"], b + 1)
                V.scalar_tensor_tensor(qa[:, b].rearrange("p h n -> p (h n)"), qh[:, b].rearrange("p h n -> p (h n)"),
                                       c("lo_q"), pair(b).rearrange("p a n -> p (a n)"), ALU.mult, ALU.add)\
                    .then_inc(sig["qa_ready"], 1)

            def head_max(n, i):
                b, quad = divmod(n, QUADS)
                t, pair_of = divmod(i, 2)
                head = 4 * quad + 2 * pair_of
                dve.wait_ge(sig["s_mm"], 4 * n + i + 1)
                V.tensor_reduce(mx[:, b, head:head + 2, t], score_bank(4 * n + i).rearrange("p (h n) -> p h n", h=2),
                                AX.X, ALU.max).then_inc(sig["smax"], 1)

            def shift_rows(n):
                b, quad = divmod(n, QUADS)
                dve.wait_ge(sig["smax"], 4 * n + 4)
                if n >= 2:
                    dve.wait_ge(sig["shift_mm"], n - 1)
                for t in range(TILES):
                    ins = V.tensor_scalar(
                        spread[:, n % 2, t].rearrange("p (g r) -> p g r", g=4)[:, :, 28:32],
                        mx[:, b, 4 * quad:4 * quad + 4, t:t + 1].to_broadcast([P, 4, 4]),
                        -1.0 / (4 * BIG), None, ALU.mult)
                ins.then_inc(sig["spread"], 1)

            def shifted_query(n):
                b, quad = divmod(n, QUADS)
                dve.wait_ge(sig["shift_mm"], n + 1)
                if n >= 2:
                    dve.wait_ge(sig["st_mm"], 4 * (n - 1))
                V.tensor_tensor(qb[:, n % 2], ps[:, 6, 0:T], qa[:, b, quad], ALU.add).then_inc(sig["qb"], 1)

            for n in range(2):
                for k in range(4):
                    head_max(n, k)
                    if n == 1 and k == 0:
                        shifted_query(0)
                shift_rows(n)
            for n in range(B * QUADS):
                for k in range(4):
                    if n + 2 < B * QUADS:
                        head_max(n + 2, k)
                    if k == 1 and n + 1 < B * QUADS:
                        shifted_query(n + 1)
                if n + 2 < B * QUADS:
                    shift_rows(n + 2)
            for b in range(B):
                dve.wait_ge(sig["oR_mm"], b + 1)
                for t in range(TILES):
                    heads = bank(b, t).rearrange("p (h r) -> p h r", h=NH)
                    ins = V.reciprocal(oden[:, b, t], heads[:, :, DK])
                ins.then_inc(sig["oden"], 1)
                dve.wait_ge(sig["oden"], b + 1)
                for t in range(TILES):
                    heads = bank(b, t).rearrange("p (h r) -> p h r", h=NH)
                    ins = V.tensor_tensor(attn[:, b, t].rearrange("p (h k) -> p h k", h=NH), heads[:, :, 0:DK],
                                          oden[:, b, t].unsqueeze(2).to_broadcast([P, NH, DK]), ALU.mult)
                ins.then_inc(sig["attn"], 1)
            for b in range(B):
                dve.wait_ge(sig["cols_hi"], nth(C_ATTN, b))
                lo_part(colsY[:, 1, b], bank(b, 0)[:, 0:T], colsY[:, 0, b], "cols_ready")
            for b in range(B):
                dve.wait_ge(sig["wo1_mm"], b + 1)
                V.tensor_tensor(x3[:, b].rearrange("p t n -> p (t n)"), bank(b, 1)[:, 0:T],
                                x2[:, b].rearrange("p t n -> p (t n)"), ALU.add).then_inc(sig["x3"], 1)
                dve.wait_ge(sig["x3"], b + 1)
                ln_stats(LN_MOE, b, lambda t: x3[:, b, t])
                ln_moments(LN_MOE, b)
            for b in range(B):
                ln_rows(LN_MOE, b, lambda t: x3[:, b, t])
            for b in range(B):
                dve.wait_ge(sig["cols_hi"], nth(C_MOE, b))
                lo_part(colsN[:, 1, b], bank(b, 0)[:, 0:T], colsN[:, 0, b], "cols_ready")
            for b in range(B):
                dve.wait_ge(sig["logit_mm"], b + 1)
                logit = bank(b, 1)[:, 0:TILES * NE].rearrange("p (t e) -> p t e", t=TILES)
                for t in range(TILES):
                    ins = V.max(top8[:, b, t], logit[:, t])
                ins.then_inc(sig["top8"], 1)
                dve.wait_ge(sig["top8"], b + 1)
                V.tensor_scalar(ntop[:, b], top8[:, b, :, 0], -1.0, None, ALU.mult)
                for t in range(TILES):
                    ins = V.max_index(topix[:, b, t], top8[:, b, t], logit[:, t])
                ins.then_inc(sig["topix"], 1)
                dve.wait_ge(sig["topix"], b + 1)
                for t in range(TILES):
                    ins = V.tensor_scalar(onehot[:, b, t], c("iota"), topix[:, b, t, 0:1], None, ALU.is_equal)
                ins.then_inc(sig["onehot"], 1)
            def masked_tokens(b):
                dve.wait_ge(sig["oh"], 2 * b + 2)
                if b >= 2:
                    dve.wait_ge(sig["moe_h"], b - 1)
                for part in range(2):
                    V.tensor_tensor(xm[:, part, b % 2], oh[:, b % 2],
                                    colsN[:, part, b].unsqueeze(1).to_broadcast([P, NE, T]), ALU.mult)\
                        .then_inc(sig["xm" if part else "xm_hi"], 1)

            def gelu_lo(b):
                dve.wait_ge(sig["gelu_hi"], b + 1)
                lo_part(gelu16[:, 1, b], gelu32[:, b], gelu16[:, 0, b], "gelu_ready")
                for t in range(TILES):
                    ins = V.scalar_tensor_tensor(y0[:, b, t], bank(b, 1)[:, t * D:(t + 1) * D], score[:, b, t:t + 1],
                                                 x3[:, b, t], ALU.mult, ALU.add)
                ins.then_inc(sig["y0"], 1)

            def pick(u):
                b, t = divmod(u, TILES)
                pair_of = OUT_PAIRS[u]
                dve.wait_ge(sig["moe_o"], u + 1)
                dve.wait_ge(sig["wsel"], b + 1)
                if u >= 2:
                    dve.wait_ge(sig["picksum"], u - 1)
                V.tensor_tensor(picked[:, u % 2], pair(pair_of).rearrange("p a (e n) -> p (a e) n", n=D),
                                wsel[:, b, t].unsqueeze(2).to_broadcast([P, NE, D]), ALU.mult)\
                    .then_inc(sig["picked"], 1)
                dve.wait_ge(sig["picked"], u + 1)
                if u >= 2:
                    dve.wait_ge(sig["y_out"], u - 1)
                V.tensor_reduce(picksum[:, u % 2], picked[:, u % 2].rearrange("p e n -> p n e"), AX.X, ALU.add)\
                    .then_inc(sig["picksum"], 1)
                dve.wait_ge(sig["picksum"], u + 1)
                dve.wait_ge(sig["y0"], b + 1)
                V.tensor_tensor(res[:, b, t], picksum[:, u % 2], y0[:, b, t], ALU.add).then_inc(sig["y_out"], 1)

            masked_tokens(0)
            masked_tokens(1)
            for b in range(B):
                dve.wait_ge(sig["expsum"], b + 1)
                V.reciprocal(score[:, b], esum[:, b]).then_inc(sig["score"], 1)
            for b in range(B):
                dve.wait_ge(sig["onehot"], b + 1)
                dve.wait_ge(sig["score"], b + 1)
                for t in range(TILES):
                    ins = V.tensor_scalar(wsel[:, b, t], onehot[:, b, t, 0:NE], score[:, b, t:t + 1], None, ALU.mult)
                ins.then_inc(sig["wsel"], 1)
            for b in range(B):
                if b + 2 < B:
                    masked_tokens(b + 2)
                gelu_lo(b)
                if b:
                    pick(2 * b - 2)
                    pick(2 * b - 1)
            pick(2 * B - 2)
            pick(2 * B - 1)

        @block.tensor
        def _(pe):
            def mm(dst, lhsT, rhs, start, stop):
                return nc.tensor.matmul(dst, lhsT, rhs, start=start, stop=stop, skip_group_check=True)

            def product(dst, lhsT, rhs, start=True, stop=True):
                for n, (i, j) in enumerate(PASSES):
                    ins = mm(dst, lhsT(i), rhs(j), start and n == 0, stop and n == len(PASSES) - 1)
                return ins

            def transposed(dst, src):
                return nc.tensor.transpose(dst, src, ident)

            def row_bias(dst, name, stop=True):
                return mm(dst, ones16[0:2, 0:P], brow(name), False, stop)

            pe.wait_ge(sig["l_cst"], 16)
            for b in range(B):
                pe.wait_ge(sig["emb"], b + 1)
                for t in range(TILES):
                    ins = transposed(bank(b, 0)[:, t * P:(t + 1) * P], emb[:, b, t])
                ins.then_inc(sig["turned"], 1)
            pe.wait_ge(sig["w_lo"], 1)
            pe.wait_ge(sig["bias_ready"], 1)
            for b in range(B):
                if b == B - 2:
                    pe.wait_ge(sig["ew_done"], TILES)
                    for j in range(TILES):
                        for t in range(TILES):
                            ins = transposed(bank(3, 1)[:, j * T + t * P:j * T + (t + 1) * P], ew[:, t, j * P:(j + 1) * P])
                    ins.then_inc(sig["ewT_mm"], 1)
                if b == B - 1:
                    pe.wait_ge(sig["ewT_ready"], 1)
                pe.wait_ge(sig["cols_ready"], nth(C_EMB, b))
                product(bank(b, 1)[:, T:2 * T], lambda i: w("qkv", i)[:, D:2 * D], lambda j: colsA[:, j, b])
                for t in range(TILES):
                    tok = slice(t * P, (t + 1) * P)
                    dst = bank(b, 1)[:, t * D:(t + 1) * D]
                    product(dst, lambda i: colsA[:, i, b, tok], lambda j: w("qkv", j)[:, 2 * D:3 * D], stop=False)
                    ins = mm(dst, ones16[0:2, 0:P], brow("qkv")[:, 2 * D:3 * D], False, True)
                ins.then_inc(sig["kT_mm"], 1)
                for t in range(TILES):
                    tok = slice(t * P, (t + 1) * P)
                    dst = bank(b, 0)[:, t * 2 * D:(t + 1) * 2 * D]
                    product(dst, lambda i: colsA[:, i, b, tok], lambda j: w("qkv", j)[:, 0:2 * D], start=t == 0,
                            stop=False)
                    ins = mm(dst, ones16[0:2, 0:P], brow("qkv")[:, 0:2 * D], False, False)
            pe.wait_ge(sig["ones_ready"], 1)
            for b in range(B):
                pe.wait_ge(sig["kdiag"], b + 1)
                for t in range(TILES):
                    ins = mm(bank(b, 0)[:, t * 2 * D + D:(t + 1) * 2 * D], ones32[:, :], kdiag[:, b], False, True)
                ins.then_inc(sig["kshift"], 1)
            pe.wait_ge(sig["absum"], 3)
            pe.wait_ge(sig["wgsq"], 1)
            mm(bank(3, 1)[:, T + NE:T + 2 * NE], c("wredT", NG), c("wgT", NG), True, True)
            mm(bank(3, 1)[:, T + 2 * NE:T + 3 * NE], ones32[0:NG, :], wgsq[:, :], True, True)
            mm(bank(3, 1)[:, T:T + 3], ones32[:, :], absum[:, :], True, True).then_inc(sig["means_ready"], 1)
            pe.wait_ge(sig["ewT_ready"], 1)
            for b in range(B):
                pe.wait_ge(sig["eb_lo"], b + 1)
                for t in range(TILES):
                    tok = slice(t * P, (t + 1) * P)
                    for j in range(TILES):
                        ins = product(bank(b, 0)[:, t * 2 * D:(t + 1) * 2 * D], lambda i: ewT[:, i, j, tok],
                                      lambda k: eb16[:, k, b, j], start=j == 0, stop=j == TILES - 1)
                ins.then_inc(sig["numden"], 1)
            for b in range(B):
                pe.wait_ge(sig["y"], b + 1)
                for t in range(TILES):
                    ins = transposed(bank(b, 1)[:, t * P:(t + 1) * P], y[:, b, t])
                ins.then_inc(sig["turned"], 1)
            pe.wait_ge(sig["bias_rest"], 1)
            pe.wait_ge(sig["w_lo"], 2)
            pe.wait_ge(sig["id_ready"], 1)
            for b in range(B):
                pe.wait_ge(sig["cols_ready"], nth(C_Y, b))
                for t in range(TILES):
                    tok = slice(t * P, (t + 1) * P)
                    dst = bank(b, 0)[:, t * D:(t + 1) * D]
                    product(dst, lambda i: colsY[:, i, b, tok], lambda j: w("wo", j), stop=False)
                    mm(dst, colsA[:, 0, b, tok], id16[:, :], False, False)
                    mm(dst, colsA[:, 1, b, tok], id16[:, :], False, False)
                    ins = row_bias(dst, "bo")
                ins.then_inc(sig["attn_mm"], 1)
            for b in range(B):
                pe.wait_ge(sig["rows_act"], nth(NMR_TURN[LN_A], b))
                for t in range(TILES):
                    ins = transposed(bank(b, 1)[:, t * P:(t + 1) * P], rows[:, b, t])
                ins.then_inc(sig["turned"], 1)
            pe.wait_ge(sig["w_lo_pool"], 1)
            for b in range(B):
                pe.wait_ge(sig["cols_ready"], nth(C_A, b))
                for k in range(HC):
                    dst = bank(b, k // 2)[:, (k % 2) * T:(k % 2 + 1) * T]
                    product(dst, lambda i: w("w1", i)[:, k * P:(k + 1) * P], lambda j: colsN[:, j, b], stop=False)
                    ins = mm(dst, brow("b1")[:, k * P:(k + 1) * P], ones16[0:2, :], False, True)
                ins.then_inc(sig["hid_mm"], 1)
            pe.wait_ge(sig["w_lo_pool"], 2)
            for b in range(B):
                pe.wait_ge(sig["hid_ready"], b + 1)
                for t in range(TILES):
                    tok = slice(t * P, (t + 1) * P)
                    dst = bank(b, 0)[:, t * D:(t + 1) * D]
                    for k in range(HC):
                        product(dst, lambda i: hid16[:, i, b, k, tok], lambda j: w("w2", j)[:, k * D:(k + 1) * D],
                                start=k == 0, stop=False)
                    mm(dst, colsN[:, 0, b, tok], id16[:, :], False, False)
                    mm(dst, colsN[:, 1, b, tok], id16[:, :], False, False)
                    ins = row_bias(dst, "b2")
                ins.then_inc(sig["ff_mm"], 1)
                if b == 1:
                    pe.wait_ge(sig["mask_ind"], 1)
                    for a in range(B):
                        for t in range(TILES):
                            ins = mm(bank(a // 2, 1)[:, (a % 2) * T:(a % 2 + 1) * T], ones16[:, 0:P], ind[:, a, t], t == 0,
                                     t == TILES - 1)
                    ins.then_inc(sig["count_mm"], 1)

            def keys(b, half_no):
                for i in range(2):
                    k = 2 * half_no + i
                    dst = bank(b, 1)[:, i * T:(i + 1) * T]
                    product(dst, lambda i: w("wk", i)[:, k * P:(k + 1) * P], lambda j: ctxT[:, j, b], stop=False)
                    mm(dst, brow("bk")[:, k * P:(k + 1) * P], ones16[0:2, :], False, False)
                    ins = mm(dst, sel16[:, :], colrow[:, b], False, True)
                ins.then_inc(sig["kproj"], 1)

            pe.wait_ge(sig["ctxT_ready"], 1)
            pe.wait_ge(sig["w_lo_pool"], 4)
            pe.wait_ge(sig["colmask"], 1)
            for b in range(B):
                for t in range(TILES):
                    tok = slice(t * P, (t + 1) * P)
                    dst = bank(b, 1)[:, t * D:(t + 1) * D]
                    product(dst, lambda i: ctxT[:, i, b, tok], lambda j: w("wv", j), stop=False)
                    ins = row_bias(dst, "bv")
                ins.then_inc(sig["vproj"], 1)
            for b in range(B):
                pe.wait_ge(sig["va_ready"], b + 1)
                keys(b, 0)
            for b in range(B):
                pe.wait_ge(sig["q1"], b + 1)
                pe.wait_ge(sig["ka_ready"], b + 1)
                for t in range(TILES):
                    ins = transposed(bank(b, 1)[:, t * P:(t + 1) * P], rows[:, b, t])
                ins.then_inc(sig["turned"], 1)
            pe.wait_ge(sig["ffw_ready"], 3)
            for u, (b, t) in enumerate(GU_ORDER):
                tok = slice(t * P, (t + 1) * P)
                if t:
                    pe.wait_ge(sig["g"], u - 1)
                else:
                    pe.wait_ge(sig["q1T_ready"], b + 1)
                mm(bank(b, 0), qT[:, b, tok], ffw16[:, 0], True, True)
                mm(bank(b, 1), qT[:, b, tok], ffw16[:, 1], True, True).then_inc(sig["gu_mm"], 1)
            for b in range(B):
                pe.wait_ge(sig["q2"], b + 1)
                pe.wait_ge(sig["q2_act"], b + 1)
                for t in range(TILES):
                    for k in range(HC):
                        ins = transposed(bank(b, t)[:, k * P:(k + 1) * P], g[:, b, t, k * P:(k + 1) * P])
                ins.then_inc(sig["q2T_mm"], 1)
            for b in range(B):
                pe.wait_ge(sig["q2T_ready"], b + 1)
                for t in range(TILES):
                    for k in range(HC):
                        ins = mm(bank(b, 0)[:, t * D:(t + 1) * D], gT[:, b, t, k], ffw16[:, 2, k * D:(k + 1) * D],
                                 k == 0, k == HC - 1)
                ins.then_inc(sig["down_mm"], 1)
            for b in range(B):
                keys(b, 1)
            for b in range(B):
                pe.wait_ge(sig["rows_ready"], nth(R_ATT, b))
                for t in range(TILES):
                    ins = transposed(bank(b, 0)[:, t * P:(t + 1) * P], rows[:, b, t])
                ins.then_inc(sig["turned"], 1)
            pe.wait_ge(sig["w_lo_pool"], 5)
            for b in range(B):
                pe.wait_ge(sig["cols_ready"], nth(C_QUERY, b))
                for k in range(QUADS):
                    dst = bank(b, k // 2)[:, (k % 2) * T:(k % 2 + 1) * T]
                    product(dst, lambda i: w("wq", i)[:, k * P:(k + 1) * P], lambda j: colsA[:, j, b], stop=False)
                    ins = mm(dst, brow("bq")[:, k * P:(k + 1) * P], ones16[0:2, :], False, True)
                ins.then_inc(sig["q_mm"], 1)
            pe.wait_ge(sig["qa_ready"], B)
            pe.wait_ge(sig["zeros_ready"], 2)

            def scores(n, i, masked):
                b, quad = divmod(n, QUADS)
                t, pair_of = divmod(i, 2)
                if i == 0:
                    pe.wait_ge(sig["kz_ready"], n + 1)
                if 4 * n + i >= 3:
                    pe.wait_ge(sig["smax"], 4 * n + i - 2)
                dst = score_bank(4 * n + i)
                ins = mm(dst, qa[:, b, quad, t * P:(t + 1) * P],
                         kz[:, n % KRING, 2 * pair_of:2 * pair_of + 2].rearrange("p h n -> p (h n)"), True, not masked)
                if masked:
                    for h in range(2):
                        ins = mm(dst[:, h * T:(h + 1) * T], idbig[:, :], resmask[:, b, t], False, h == 1)
                ins.then_inc(sig["s_mm"], 1)

            def shift(n):
                pe.wait_ge(sig["spread"], n + 1)
                if n >= 1:
                    pe.wait_ge(sig["qb"], n)
                for t in range(TILES):
                    ins = mm(ps[:, 6, t * P:(t + 1) * P], spread[:, n % 2, t], id16[:, :], True, True)
                ins.then_inc(sig["shift_mm"], 1)

            def shifted_scores(n, k, masked):
                b, quad = divmod(n, QUADS)
                head = 4 * n + k
                if k == 0:
                    pe.wait_ge(sig["qb"], n + 1)
                if head >= 2:
                    pe.wait_ge(sig["probs"], head - 1)
                for t in range(TILES):
                    tok = slice(t * P, (t + 1) * P)
                    dst = ps[:, 2 + head % 2, t * T:(t + 1) * T]
                    ins = mm(dst, kz[:, n % KRING, k, tok], qb[:, n % 2], True, not masked)
                    if masked:
                        for q in range(TILES):
                            ins = mm(ps[:, 2 + head % 2, t * T + q * P:t * T + (q + 1) * P],
                                     resmask[:, b, q, tok], idbig[:, :], False, q == TILES - 1)
                ins.then_inc(sig["st_mm"], 1)

            def weighted_values(n, t):
                b, quad = divmod(n, QUADS)
                m = n // 2
                if t == 0:
                    pe.wait_ge(sig["probs"], 4 * n + 4)
                    if m >= 2 and n % 2 == 0:
                        pe.wait_ge(sig["oT"], m - 1)
                for k in range(4):
                    ins = mm(ps[32 * k:32 * k + 32, 4 + m % 2, (n % 2) * T:(n % 2 + 1) * T],
                             va[:, b, t, 4 * quad + k], pt[:, (4 * n + k) % PRING, t], t == 0, t == TILES - 1)
                if t == TILES - 1:
                    ins.then_inc(sig["pv"], 1)

            def attention(masked):
                for n in range(2):
                    for k in range(4):
                        scores(n, k, masked)
                    if n == 0:
                        shift(0)
                for n in range(B * QUADS):
                    for k in range(4):
                        shifted_scores(n, k, masked)
                        if n + 2 < B * QUADS:
                            scores(n + 2, k, masked)
                        if k == 1 and n + 1 < B * QUADS:
                            shift(n + 1)
                        if k < TILES and n >= 1:
                            weighted_values(n - 1, k)
                for t in range(TILES):
                    weighted_values(B * QUADS - 1, t)

            pe.wait_ge(sig["flag_ready"], 1)
            pe.wait_ge(sig["resmask"], 2)
            general = pe.value_load(flag_i[0:1, 0:1], min_val=0, max_val=B * T * T)
            with pe.If(general > 0):
                attention(True)
            with pe.Else():
                attention(False)

            for b in range(B):
                pe.wait_ge(sig["oT"], 2 * B)
                pe.wait_ge(sig["qb"], B * QUADS)
                for t in range(TILES):
                    for k in range(QUADS):
                        ins = transposed(bank(b, t)[:, k * P:(k + 1) * P], oT[:, b, k, t * P:(t + 1) * P])
                ins.then_inc(sig["oR_mm"], 1)
            for b in range(B):
                pe.wait_ge(sig["attn"], b + 1)
                for t in range(TILES):
                    ins = transposed(bank(b, 0)[:, t * P:(t + 1) * P], attn[:, b, t])
                ins.then_inc(sig["turned"], 1)
            pe.wait_ge(sig["w_lo_pool"], 6)
            for b in range(B):
                pe.wait_ge(sig["cols_ready"], nth(C_ATTN, b))
                for t in range(TILES):
                    tok = slice(t * P, (t + 1) * P)
                    dst = bank(b, 1)[:, t * D:(t + 1) * D]
                    product(dst, lambda i: colsY[:, i, b, tok], lambda j: w("wo1", j), stop=False)
                    ins = row_bias(dst, "bo1")
                ins.then_inc(sig["wo1_mm"], 1)
            for b in range(B):
                pe.wait_ge(sig["rows_ready"], nth(R_MOE, b))
                for t in range(TILES):
                    ins = transposed(bank(b, 0)[:, t * P:(t + 1) * P], rows[:, b, t])
                ins.then_inc(sig["turned"], 1)
            pe.wait_ge(sig["router_ready"], 1)
            for b in range(B):
                pe.wait_ge(sig["cols_ready"], nth(C_MOE, b))
                for t in range(TILES):
                    tok = slice(t * P, (t + 1) * P)
                    ins = product(bank(b, 1)[:, t * NE:(t + 1) * NE], lambda i: colsN[:, i, b, tok],
                                  lambda j: router16[:, j])
                ins.then_inc(sig["logit_mm"], 1)
            def onehot_rows(b):
                pe.wait_ge(sig["onehot"], b + 1)
                for t in range(TILES):
                    ins = mm(bank(b, 0)[0:2 * NE, t * P:(t + 1) * P], onehot[:, b, t], id16[:, :], True, True)
                ins.then_inc(sig["ohT_mm"], 1)

            def onehot_columns(b):
                for half in range(2):
                    if half == 0:
                        pe.wait_ge(sig["ohT"], b + 1)
                        pe.wait_ge(sig["expsum"], b + 1)
                    else:
                        pe.wait_ge(sig["oh"], 2 * b + 1)
                    for e in range(4):
                        for t in range(TILES):
                            ins = mm(bank(b, e // 2)[:, (e % 2) * T + t * P:(e % 2) * T + (t + 1) * P],
                                     onehot[:, b, t, 4 * half + e:4 * half + e + 1].to_broadcast([P, P]),
                                     id16[:, :], True, True)
                    ins.then_inc(sig["oh_mm"], 1)

            def hidden(b):
                pe.wait_ge(sig["xm"], b + 1)
                for t in range(TILES):
                    mm(bank(b, 1)[:, t * D:(t + 1) * D], ohT[:, b, t * P:(t + 1) * P], mbias16[:, EH:EH + D], True, True)
                for k in range(EC):
                    dst = bank(b, 0)[:, k * T:(k + 1) * T]
                    for e in range(NE):
                        product(dst, lambda i: w("m1", i)[:, e * EH + k * P:e * EH + (k + 1) * P],
                                lambda j: xm[:, j, b % 2, e], start=e == 0, stop=False)
                    ins = mm(dst, mbias16[:, k * P:(k + 1) * P], ohT[:, b], False, True)
                ins.then_inc(sig["moe_h"], 1)

            def outputs(u):
                b, t = divmod(u, TILES)
                tok = slice(t * P, (t + 1) * P)
                pair_of = OUT_PAIRS[u]
                pe.wait_ge(sig["gelu_ready"], max(b, pair_of) + 1)
                pe.wait_ge(sig["y0"], max(b, pair_of) + 1)
                if pair_of in OUT_PAIRS[:u]:
                    pe.wait_ge(sig["picked"], u - OUT_PAIRS[:u][::-1].index(pair_of))
                for half in range(2):
                    for k in range(EC):
                        col = k * NE * D + half * 4 * D
                        ins = product(bank(pair_of, half), lambda i: gelu16[:, i, b, k, tok],
                                      lambda j: w("m2", j)[:, col:col + 4 * D], start=k == 0, stop=k == EC - 1)
                ins.then_inc(sig["moe_o"], 1)

            onehot_rows(0)
            onehot_rows(1)
            onehot_columns(0)
            onehot_rows(2)
            onehot_columns(1)
            onehot_rows(3)
            pe.wait_ge(sig["w_lo_pool"], 7)
            pe.wait_ge(sig["mbias_ready"], 1)
            hidden(0)
            onehot_columns(2)
            hidden(1)
            onehot_columns(3)
            pe.wait_ge(sig["w_lo_pool"], 8)
            outputs(0)
            hidden(2)
            outputs(1)
            hidden(3)
            for u in range(2, B * TILES):
                outputs(u)


def kernel(x, ctx_1024, mask_BxSxS2_ik1, L0_xattn_wq, L0_xattn_bq, L0_xattn_wk, L0_xattn_bk, L0_xattn_wv, L0_xattn_bv,
           L0_xattn_wo, L0_xattn_bo, L0_xattn_pos_bias, L0_xattn_gamma, L0_xattn_beta, L0_xattn_w1, L0_xattn_b1,
           L0_xattn_w2, L0_xattn_b2, L0_ffn_w_gate, L0_ffn_w_up, L0_ffn_w_down, L1_xattn_Wq, L1_xattn_bq, L1_xattn_Wk,
           L1_xattn_bk, L1_xattn_Wv, L1_xattn_bv, L1_xattn_Wo, L1_xattn_bo, L1_ffn_w_red, L1_ffn_wg, L1_ffn_W1,
           L1_ffn_b1, L1_ffn_W2, L1_ffn_b2):
    import concourse.bacc as bacc
    from concourse.bass_utils import run_bass_kernel_spmd

    def heads32(m):
        m = m.reshape(m.shape[0], QUADS, 4, 1, DK)
        wide = np.zeros((m.shape[0], QUADS, 4, 4, DK), np.float32)
        wide[:, :, :, 0:3] = m
        return wide.reshape(m.shape[0], QUADS * P)

    x_rows = np.ascontiguousarray(np.asarray(x).reshape(B, TILES, P, D).transpose(0, 2, 1, 3))
    ctx = np.asarray(ctx_1024)
    ctx_rows = np.ascontiguousarray(ctx.reshape(B, TILES, P, D).transpose(2, 0, 1, 3))
    ctx_cols = np.ascontiguousarray(ctx.transpose(2, 0, 1))
    mask = np.ascontiguousarray(np.asarray(mask_BxSxS2_ik1).reshape(B, TILES, P, T).transpose(2, 0, 1, 3))
    pos = np.ascontiguousarray(np.asarray(L0_xattn_pos_bias).reshape(TILES, P, T).transpose(1, 0, 2))

    consts = np.zeros((P, NC_), np.float32)
    row = np.arange(P)
    consts[:, CSEG["ident"][0]:CSEG["ident"][1]] = np.eye(P)
    consts[:, CSEG["iota"][0]:CSEG["iota"][1]] = np.tile(np.arange(NE), 2)
    consts[:, CSEG["lo_q"][0]] = np.where((row % 32) // DK == 2, -1.0, 0.0)
    consts[:, CSEG["lo_k"][0]] = np.where((row % 32) // DK == 1, -1.0, 0.0)
    consts[:, CSEG["lo_2"][0]] = np.where(row == 1, -1.0, 0.0)
    consts[:, CSEG["lo_16"][0]] = np.where((row >= NE) & (row < 2 * NE), -1.0, 0.0)
    consts[0, CSEG["sel"][0]:CSEG["sel"][1]] = (row % 32 >= 24) & (row % 32 < 28)
    i, j = np.arange(T).reshape(TILES, P).T[:, :, None], np.arange(T)[None, None, :]
    consts[:, CSEG["band"][0]:CSEG["band"][1]] = (np.abs(i - j) < WINDOW).reshape(P, TILES * T)
    consts[:, CSEG["cols"][0]:CSEG["cols"][1]] = np.stack([np.asarray(L0_xattn_bk), np.asarray(L0_xattn_gamma), np.asarray(L0_xattn_beta)], 1)
    consts[0:NG, CSEG["wredT"][0]:CSEG["wredT"][1]] = np.asarray(L1_ffn_w_red).T
    consts[0:NG, CSEG["wgT"][0]:CSEG["wgT"][1]] = np.asarray(L1_ffn_wg).T

    def mask_rows(m, rows, value):
        m = m.reshape(1, QUADS, 4, 32).copy()
        m[:, :, :, rows] = value
        return m.reshape(1, QUADS * P)

    bias = np.concatenate([
        np.asarray(L0_xattn_bq)[None], np.asarray(L0_xattn_bk)[None], np.asarray(L0_xattn_bv)[None],
        np.asarray(L0_xattn_bo)[None], np.asarray(L0_xattn_b1)[None], np.asarray(L0_xattn_b2)[None],
        mask_rows(heads32(np.asarray(L1_xattn_bq)[None]), slice(24, 28), -BIG),
        mask_rows(heads32(np.asarray(L1_xattn_bk)[None]), slice(28, 32), BIG),
        np.asarray(L1_xattn_bv)[None], np.asarray(L1_xattn_bo)[None]], 1)
    bias = np.ascontiguousarray(np.repeat(bias, 2, 0))
    mb = np.concatenate([np.asarray(L1_ffn_b1), np.asarray(L1_ffn_b2)], 1)
    mbias = np.ascontiguousarray(np.concatenate([mb, mb], 0))
    ffw = np.ascontiguousarray(np.stack([
        np.asarray(L0_ffn_w_gate).T, np.asarray(L0_ffn_w_up).T,
        np.asarray(L0_ffn_w_down).T.reshape(HC, P, D).transpose(1, 0, 2).reshape(P, HC * D)], 1))
    weights = np.ascontiguousarray(np.concatenate([
        np.asarray(L0_xattn_wq), np.asarray(L0_xattn_wk), np.asarray(L0_xattn_wv), np.asarray(L0_xattn_wo),
        np.asarray(L0_xattn_w1), np.asarray(L0_xattn_w2).reshape(HC, P, D).transpose(1, 0, 2).reshape(P, HC * D),
        heads32(np.asarray(L1_xattn_Wk)), np.asarray(L1_xattn_Wv), heads32(np.asarray(L1_xattn_Wq)), np.asarray(L1_xattn_Wo),
        np.asarray(L1_ffn_W1).transpose(1, 0, 2).reshape(P, NE * EH),
        np.asarray(L1_ffn_W2).reshape(NE, EC, P, D).transpose(2, 1, 0, 3).reshape(P, EC * NE * D)], 1))

    arrays = {"x": x_rows, "ctx_rows": ctx_rows, "ctx_cols": ctx_cols, "mask": mask, "consts": consts, "pos": pos,
              "gamma": np.ascontiguousarray(np.asarray(L0_xattn_gamma)),
              "beta": np.ascontiguousarray(np.asarray(L0_xattn_beta)),
              "bias": bias, "mbias": mbias, "ffw": ffw, "weights": weights}
    nc = bacc.Bacc("TRN2", target_bir_lowering=False, num_devices=1)
    args = [nc.dram_tensor(f"{n}_dram", a.shape, mybir.dt.from_np(a.dtype), kind="ExternalInput").ap()
            for n, a in arrays.items()]
    out = nc.dram_tensor("out_dram", (B, P, TILES, D), F32, kind="ExternalOutput").ap()
    build_program(nc, *args, out)
    r = run_bass_kernel_spmd(nc, [{f"{n}_dram": a for n, a in arrays.items()}], core_ids=[0])
    got = r.results[0]["out_dram"]
    return np.ascontiguousarray(got.transpose(0, 2, 1, 3).reshape(B, T, D))
```

```python
from contextlib import ExitStack

import concourse.bass as bass
import numpy as np
from concourse import mybir

F32, F16, BF16 = mybir.dt.float32, mybir.dt.float16, mybir.dt.bfloat16
I32, U32 = mybir.dt.int32, mybir.dt.uint32
ACT = mybir.ActivationFunctionType
ALU = mybir.AluOpType
AX = mybir.AxisListType

P = 128
B, T, D = 4, 256, 128
TILES = T // P
WINDOW = 32
HID = 512
HC = HID // P
NH, DK = 16, 8
PRING = 8
KRING = 4
QUADS = NH // 4
NE, EH, NG = 8, 256, 16
EC = EH // P
EPS = 1e-5
MAGIC = 12582912.0
BIG = 61440.0
GU_ORDER = [(pair + i, t) for pair in range(0, B, 2) for t in range(TILES) for i in range(2)]
ONEHOT_PAIRS = (0, 0, 2, 3)
ONEHOT_AT = {(QUADS * B - 2, 0): (0, 0), (QUADS * B - 2, 2): (0, 1), (QUADS * B - 1, 0): (1, 0), (QUADS * B - 1, 2): (1, 1)}
OUT_PAIRS = (0, 1, 0, 1, 2, 3, 0, 1)
PASSES = ((0, 0), (0, 1), (1, 0))

SEGS = [("qkv", 3 * D), ("wo", D), ("w1", HID), ("w2", HID), ("wk", QUADS * P), ("wv", D), ("wq", QUADS * P),
        ("wo1", D), ("m1", NE * EH), ("m2", EC * NE * D)]
SEG = {}
NW = 0
for _name, _n in SEGS:
    SEG[_name] = (NW, NW + _n)
    NW += _n
BSEGS = [("qkv", 3 * D), ("bo", D), ("b1", HID), ("b2", D), ("bq", QUADS * P), ("bk", QUADS * P), ("bv", D), ("bo1", D)]
BSEG = {}
NB = 0
for _name, _n in BSEGS:
    BSEG[_name] = (NB, NB + _n)
    NB += _n
BPARTS = (BSEG["qkv"], (BSEG["qkv"][1], NB))
CSEGS = [("ident", P), ("iota", 2 * NE), ("lo_q", 1), ("lo_k", 1), ("lo_2", 1), ("lo_16", 1), ("sel", P),
         ("band", 2 * T), ("cols", 3), ("wredT", P), ("wgT", NE)]
CSEG = {}
NC_ = 0
for _name, _n in CSEGS:
    CSEG[_name] = (NC_, NC_ + _n)
    NC_ += _n

LN_IN, LN_A, LN_OUT, LN_FFN, LN_ATT, LN_MOE = range(6)
NLN = 6
R_IN, R_A, R_ATT = range(3)
NMR_TURN = {LN_FFN: 0, LN_MOE: 1}
T_EMB, T_Y, T_A, T_QUANT, T_QUERY, T_TAIL = range(6)
C_EMB, C_Y, C_A, C_QUERY, C_TAIL = range(5)


def nth(stage, b):
    return stage * B + b + 1


def nth_norm(ln, b):
    if ln in (LN_OUT, LN_FFN):
        return nth(LN_OUT, 0) + 4 * (b // 2) + 2 * (ln - LN_OUT) + b % 2
    return nth(ln, b)


def nth_of_tail(stage, b, moe):
    return stage * B + 2 * b + (2 if moe else 1)


TAIL_START = 22
TAIL_STEPS = (0, 2, 4, 6, 10, 13, 15)
TAIL_ROWS = 9
POOL_ROOTS = (7, 11)


def tail_place(n, k):
    return divmod(4 * n + k - TAIL_START, 4 * QUADS)


def tail_at(n, k):
    b, place = tail_place(n, k)
    return (b, TAIL_STEPS.index(place)) if 0 <= b < B - 1 and place in TAIL_STEPS else None


SIGNALS = """
l_x0 l_x1 l_x2 l_x3 l_ctx l_cst l_pos l_gb l_bias l_mbias l_ctxT l_mask l_ffw l_out l_qkv l_wo l_w1 l_w2 l_wk
l_wv l_wq l_wo1 l_m1 l_m2 ones_ready id_ready bias_hi bias_ready bias_neg bias_rest mbias_hi mbias_ready zeros_ready w_hi w_lo
w_lo_pool absum means_ready meanc ffscale ffw_r ffw_c ffw_ready kscale pos_masked pos_max ew_done ewT_mm ewT_hi
ewT_ready wgsq router_ready mask_ind count_mm colmask resmask flagsum flag_ready ctxT_hi
ctxT_ready kproj ka_hi ka_ready vproj va_ready kz_zero kz_ready emb kT_mm kmax kmaxb kdiag kshift ek ekv eb_hi eb_lo numden 
ysig y attn_mm hid_mm hid_hi hid_ready ff_mm xb nb x1 amax amaxc ascale q1 q1T_ready gscale gu_mm
silu g q2 q2_act q2T_mm q2T_ready down_mm x2 q_mm qa_hi qa_ready s_mm smax spread shift_mm qb st_mm probs pv oT
oR_mm oden attn wo1_mm x3 logit_mm top8 topix onehot expsum score wsel ohT_mm ohT oh_mm oh xm_hi xm moe_h
gelu gelu_hi gelu_ready moe_o picked picksum y0 y_out turned cols_hi cols_ready ln_moments ln_vareps ln_rstd
ln_stats rows_ready rows_act ln_nmr router_step flagstep logits
""".split()


def build_program(nc, x, ctx_rows, ctx_cols, mask, consts, pos, gamma, beta, bias, mbias, ffw, weights, out):
    scope = ExitStack()
    with scope:
        def sb(name, shape, dt=F32):
            return scope.enter_context(nc.sbuf_tensor(name, shape, dt))

        sig = {n: scope.enter_context(nc.semaphore(n)) for n in SIGNALS}
        ps = scope.enter_context(nc.psum_tensor("ps", [P, 8, 512], F32))

        x_in = sb("x_in", [P, B, TILES, D])
        ctx_in = sb("ctx_in", [P, B, TILES, D])
        cst = sb("cst", [P, NC_])
        gamma_b = sb("gamma_b", [P, D])
        beta_b = sb("beta_b", [P, D])
        bias16 = sb("bias16", [2, NB], F16)
        mbias16 = sb("mbias16", [2 * NE, EH + D], F16)
        wf = sb("wf", [P, HID + SEG["m1"][0]])
        stage = sb("stage", [P, NE * EH])
        mask_in = wf[:, 0:B * TILES * T].bitcast(I32).rearrange("p (b t n) -> p b t n", b=B, t=TILES)
        w16 = sb("w16", [P, 2, NW], F16)
        ffw16 = sb("ffw16", [P, 3, HID], F16)
        ident = cst[:, CSEG["ident"][0]:CSEG["ident"][1]]
        id16 = sb("id16", [P, P], F16)
        idbig = sb("idbig", [P, P], BF16)
        sel16 = sb("sel16", [1, P], F16)
        ones32 = sb("ones32", [P, P])
        ones16 = sb("ones16", [P, T], F16)
        all_masked = sb("all_masked", [P, 2])
        mask_sums = sb("mask_sums", [P, 4])
        silu_junk = sb("silu_junk", [P, 1])
        halfs = sb("halfs", [P, 2 * NE])
        roots = sb("roots", [P, NE])
        minus_ones = sb("minus_ones", [P, NE])

        def c(name, rows=P):
            a, b_ = CSEG[name]
            return cst[0:rows, a:b_]

        def wf32(name):
            a, b_ = SEG[name]
            return stage[:, :] if name in ("m1", "m2") else wf[:, HID + a:HID + b_]

        def w(name, part):
            a, b_ = SEG[name]
            return w16[:, part, a:b_]

        def brow(name):
            a, b_ = BSEG[name]
            return bias16[:, a:b_]

        bk_col = c("cols")[:, 0:1]
        gamma_col = c("cols")[:, 1:2]
        beta_col = c("cols")[:, 2:3]

        gate_pt = sb("gate_pt", [P, 12 * TILES * T])
        hid_xm = sb("hid_xm", [P, 2 * B * HC * T], F16)
        eb_oT = sb("eb_oT", [P, B * QUADS * T])
        half_b = sb("half_b", [P, B * QUADS * T], F16)
        half_c = sb("half_c", [P, B * QUADS * T], F16)
        def taken(buf, start, n, rows=P):
            return buf[0:rows, start:start + n]

        at = 0
        bias_in = taken(gate_pt, 0, NB, 2)
        at += NB
        bias_h = taken(gate_pt, at, NB // 2, 2).bitcast(F16)
        at += NB // 2
        mbias_in = taken(gate_pt, at, EH + D, 2 * NE)
        at += EH + D
        mbias_h = taken(gate_pt, at, (EH + D) // 2, 2 * NE).bitcast(F16)
        at += (EH + D) // 2
        junk = taken(gate_pt, at, HID)
        at += HID
        ctxT_in = taken(gate_pt, at, B * T).rearrange("p (b n) -> p b n", b=B)
        at += B * T
        gelu32 = taken(gate_pt, 0, B * EC * T).rearrange("p (b c n) -> p b c n", b=B, c=EC)
        picked = taken(gate_pt, B * EC * T, 2 * NE * D).rearrange("p (k e n) -> p k e n", k=2, e=NE)

        absum = sb("absum", [P, 3])
        mean = sb("mean", [P, 3])
        wscale = sb("wscale", [P, 3])
        posmax = sb("posmax", [P, TILES])
        ewT = sb("ewT", [P, 2, TILES, T], F16)
        wgsq = sb("wgsq", [NG, NE])
        wnorm = sb("wnorm", [P, 5, NE])
        router = sb("router", [P, NE])
        logits = sb("logits", [P, B, TILES, NE])
        router16 = sb("router16", [P, 2, NE], F16)
        colrow = sb("colrow", [1, B, T], F16)
        flag_f = sb("flag_f", [1, 3])
        flag_i = sb("flag_i", [1, 1], I32)
        ka = sb("ka", [P, B, QUADS, T], F16)

        stats = sb("stats", [P, NLN, B, TILES, 6])
        moments = sb("moments", [P, NLN, B, TILES, 2])
        vareps = sb("vareps", [P, NLN, B, TILES])
        rstd = sb("rstd", [P, NLN, B, TILES])
        nmean = sb("nmean", [P, NLN, B, TILES])
        nmr = sb("nmr", [P, NLN, B, TILES])
        rows = sb("rows", [P, B, TILES, D])
        emb = sb("emb", [P, B, TILES, D])
        colsA = sb("colsA", [P, 2, B, T], F16)
        y_mem = sb("y_mem", [P, B * T])
        posw = y_mem[:, 0:TILES * T].rearrange("p (t n) -> p t n", t=TILES)
        ew = y_mem[:, TILES * T:2 * TILES * T].rearrange("p (t n) -> p t n", t=TILES)
        colsY = y_mem[:, :].bitcast(F16).rearrange("p (a b n) -> p a b n", a=2, b=B)
        ctxT = colsY
        n_mem = sb("n_mem", [P, 2 * B * T])
        colsN = n_mem[:, 0:B * T].bitcast(F16).rearrange("p (a b n) -> p a b n", a=2, b=B)
        a32_mem = n_mem[:, B * T:2 * B * T]
        a32 = a32_mem.rearrange("p (b n) -> p b n", b=B)
        kmx = sb("kmx", [P, B, 2])
        th = sb("th", [P, B, TILES, D])
        half = B * TILES * 2 * D
        eb = eb_oT[:, 0:half].rearrange("p (b t n) -> p b t n", b=B, t=TILES)
        oT = eb_oT[:, :].rearrange("p (b q n) -> p b q n", b=B, q=QUADS)
        ffw_in = eb_oT[:, half:half + 3 * HID].rearrange("p (k n) -> p k n", k=3)
        g = gate_pt[:, 0:B * TILES * HID].rearrange("p (b t n) -> p b t n", b=B, t=TILES)
        silu = gate_pt[:, B * TILES * HID:].rearrange("p (b n) -> p b n", b=B)
        pt = taken(gate_pt, 0, PRING * TILES * T).rearrange("p (k t n) -> p k t n", k=PRING, t=TILES)
        hid16 = hid_xm[:, :].rearrange("p (a b c n) -> p a b c n", a=2, b=B, c=HC)
        va = hid_xm[:, :].bitcast(F32).rearrange("p (b t h k) -> p b t h k", b=B, t=TILES, h=NH)
        eb16 = hid_xm[:, 0:2 * half].rearrange("p (a b t n) -> p a b t n", a=2, b=B, t=TILES)
        qh = eb_oT[:, 0:half].bitcast(F16).rearrange("p (b h n) -> p b h n", b=B, h=QUADS)
        resmask = wf[:, B * TILES * T:B * TILES * T + B * T].bitcast(BF16).rearrange("p (b t n) -> p b t n", b=B, t=TILES)
        gT = half_b[:, :].rearrange("p (b t c n) -> p b t c n", b=B, t=TILES, c=HC)
        kh = a32_mem[:, :].bitcast(F16).rearrange("p (b h n) -> p b h n", b=B, h=2)
        oh = half_b[:, :].rearrange("p (a e n) -> p a e n", a=2, e=NE)
        qa = half_c[:, :].rearrange("p (b h n) -> p b h n", b=B, h=QUADS)
        gelu16 = half_c[:, :].rearrange("p (a b c n) -> p a b c n", a=2, b=B, c=EC)
        xm_mem = (wf[:, 0:NE * T], stage[:, :])
        xm = [m.bitcast(F16).rearrange("p (a e n) -> p a e n", a=2, e=NE) for m in xm_mem]
        rden = sb("rden", [P, B, TILES, D])
        y = sb("y", [P, B, TILES, D])
        xb, x1, x2 = x_in, emb, y
        attn, y0, x3, nb, res = th, rden, xb, ctx_in, ctx_in
        ind = rden[:, :, :, :].rearrange("p b t n -> p (b t n)").bitcast(BF16).rearrange("p (b t n) -> p b t n", b=B, t=TILES)
        cnt = th[:, :, :, :].rearrange("p b t n -> p (b t n)")
        colmask = colsA[:, 0]
        colmask = colmask.rearrange("p b n -> p (b n)").bitcast(BF16).rearrange("p (b n) -> p b n", b=B)
        amax = sb("amax", [P, B, 4, TILES])
        fac = sb("fac", [P, B, 3, TILES])
        qd_mem = sb("qd_mem", [P, B * P])
        kdiag = qd_mem[:, :].rearrange("p (b n) -> p b n", b=B)
        qT = qd_mem[:, :].bitcast(F16).rearrange("p (b n) -> p b n", b=B)
        kz = taken(gate_pt, PRING * TILES * T, KRING * 4 * T // 2).bitcast(F16).rearrange(
            "p (r h n) -> p r h n", r=KRING, h=4)
        mx = sb("mx", [P, B, NH, TILES])
        spread = sb("spread", [P, 2, TILES, P], F16)
        qb = sb("qb", [P, 2, T], F16)
        oden = sb("oden", [P, B, TILES, NH])
        top8 = sb("top8", [P, B, TILES, 8])
        topix = sb("topix", [P, B, TILES, 8], U32)
        ntop = sb("ntop", [P, B, TILES])
        onehot = sb("onehot", [P, B, TILES, 2 * NE], F16)
        ejunk = sb("ejunk", [P, B, TILES, NE])
        esum = sb("esum", [P, B, TILES])
        score = sb("score", [P, B, TILES])
        wsel = sb("wsel", [P, B, TILES, NE])
        ohT = sb("ohT", [2 * NE, B, T], F16)
        picksum = sb("picksum", [P, 2, D])

        def bank(b, k):
            return ps[:, 2 * b + k, :]

        def score_bank(u):
            return ps[:, u % 2, :]

        def tail_bank(b):
            return ps[:, 7 if b < B - 1 else 6, :]

        def pair(b):
            return ps[:, 2 * b:2 * b + 2, :]

        block = scope.enter_context(nc.Block())

        @block.sync
        def _(sp):
            for b in range(B):
                sp.dma_start(x_in[:, b], x[b]).then_inc(sig[f"l_x{b}"], 16)
            sp.dma_start(cst[:, :], consts).then_inc(sig["l_cst"], 16)
            for name in ("qkv", "wo"):
                a, z = SEG[name]
                sp.dma_start(wf32(name), weights[:, a:z]).then_inc(sig["l_" + name], 16)
            sp.dma_start(posw[:, :, :], pos).then_inc(sig["l_pos"], 16)
            sp.dma_start(ffw_in[:, :, :], ffw).then_inc(sig["l_ffw"], 16)
            sp.dma_start(ctxT_in, ctx_cols).then_inc(sig["l_ctxT"], 16)
            for name in ("wk", "wv"):
                a, z = SEG[name]
                sp.dma_start(wf32(name), weights[:, a:z]).then_inc(sig["l_" + name], 16)
            for name in ("w1", "w2", "wq", "wo1", "m1"):
                a, z = SEG[name]
                sp.dma_start(wf32(name), weights[:, a:z]).then_inc(sig["l_" + name], 16)
            sp.wait_ge(sig["w_lo"], 2)
            sp.wait_ge(sig["w_lo_pool"], 2)
            sp.dma_start(mask_in, mask).then_inc(sig["l_mask"], 16)
            sp.wait_ge(sig["w_lo_pool"], 7)
            sp.dma_start(wf32("m2"), weights[:, SEG["m2"][0]:SEG["m2"][1]]).then_inc(sig["l_m2"], 16)
            for b in range(B):
                sp.wait_ge(sig["y_out"], TILES * (b + 1))
                sp.dma_start(out[b], res[:, b]).then_inc(sig["l_out"], 16)
            sp.wait_ge(sig["l_out"], 16 * B)

        @block.gpsimd
        def _(pool):
            nc.gpsimd.memset(ones32[:, :], 1.0)
            nc.gpsimd.memset(ones16[:, :], 1.0)
            nc.gpsimd.memset(halfs[:, :], -0.5)
            nc.gpsimd.memset(minus_ones[:, :], -1.0)
            nc.gpsimd.memset(all_masked[:, 0:1], -(T - 1) * BIG)
            nc.gpsimd.memset(all_masked[:, 1:2], -(T - 1) * 4 * BIG)
            nc.gpsimd.memset(roots[:, :], 0.5).then_inc(sig["ones_ready"], 1)
            pool.wait_ge(sig["ones_ready"], 1)

            def rstd_of(ln, b):
                pool.wait_ge(sig["ln_moments"], nth_norm(ln, b))
                if ln in NMR_TURN:
                    nc.gpsimd.tensor_scalar(nmean[:, ln, b, :], moments[:, ln, b, :, 0], -1.0, 0.0, ALU.mult, ALU.add)
                nc.gpsimd.tensor_scalar(vareps[:, ln, b, :], moments[:, ln, b, :, 1], EPS, 1.0, ALU.add,
                                        ALU.mult).then_inc(sig["ln_vareps"], 1)
                pool.wait_ge(sig["ln_vareps"], nth_norm(ln, b))
                nc.gpsimd.tensor_tensor(rstd[:, ln, b, :], vareps[:, ln, b, :], halfs[:, 0:TILES],
                                        ALU.pow).then_inc(sig["ln_rstd"], 1)

            def rows_shift(ln, b):
                pool.wait_ge(sig["ln_rstd"], nth_norm(ln, b))
                nc.gpsimd.tensor_tensor(nmr[:, ln, b, :], nmean[:, ln, b, :], rstd[:, ln, b, :], ALU.mult)\
                    .then_inc(sig["ln_nmr"], 1)

            def split_lo(name, n):
                a, z = SEG[name]
                pool.wait_ge(sig["w_hi"], n)
                nc.gpsimd.tensor_tensor(w16[:, 1, a:z], wf32(name), w16[:, 0, a:z], ALU.subtract)\
                    .then_inc(sig["w_lo_pool"], 1)

            for b in range(B):
                rstd_of(LN_IN, b)
            pool.wait_ge(sig["l_ctx"], 16)
            for b in range(B):
                pool.wait_ge(sig["rows_ready"], nth(R_IN, b))
                nc.gpsimd.tensor_tensor(emb[:, b], rows[:, b], ctx_in[:, b], ALU.add).then_inc(sig["emb"], 1)
            pool.wait_ge(sig["l_pos"], 16)
            pool.wait_ge(sig["l_cst"], 16)
            nc.gpsimd.tensor_tensor(posw[:, :, :], posw[:, :, :], c("band").rearrange("p (a n) -> p a n", a=TILES),
                                    ALU.mult).then_inc(sig["pos_masked"], 1)
            nc.gpsimd.tensor_tensor(wgsq[:, :], c("wgT", NG), c("wgT", NG), ALU.mult).then_inc(sig["wgsq"], 1)
            pool.wait_ge(sig["l_gb"], 32)
            pool.wait_ge(sig["rows_ready"], nth(R_IN, B - 1))
            for b in range(B):
                for t in range(TILES):
                    ins = nc.gpsimd.tensor_tensor(xb[:, b, t], x_in[:, b, t], beta_b[:, :], ALU.add)
                ins.then_inc(sig["xb"], 1)
            cols = slice(*BPARTS[1])
            pool.wait_ge(sig["bias_hi"], 2)
            nc.gpsimd.tensor_scalar(bias16[:, cols], bias_h[:, cols], c("lo_2", 2), 0.0, ALU.mult, ALU.add)\
                .then_inc(sig["bias_neg"], 1)
            pool.wait_ge(sig["bias_neg"], 1)
            nc.gpsimd.tensor_tensor(bias16[:, cols], bias16[:, cols], bias_in[:, cols], ALU.add).then_inc(sig["bias_rest"], 1)
            pool.wait_ge(sig["ffscale"], 1)
            for k in range(3):
                ins = nc.gpsimd.tensor_scalar(ffw_in[:, k], ffw_in[:, k], wscale[:, k:k + 1], MAGIC, ALU.mult, ALU.add)
            ins.then_inc(sig["ffw_r"], 1)
            pool.wait_ge(sig["meanc"], 1)
            nc.gpsimd.tensor_tensor(wnorm[:, 2], wnorm[:, 1], roots[:, :], ALU.pow).then_inc(sig["router_step"], 1)
            pool.wait_ge(sig["router_step"], 1)
            nc.gpsimd.tensor_scalar(wnorm[:, 3], wnorm[:, 2], 1e-4, 1.0, ALU.max, ALU.mult).then_inc(sig["router_step"], 1)
            pool.wait_ge(sig["router_step"], 2)
            nc.gpsimd.tensor_tensor(wnorm[:, 4], wnorm[:, 3], minus_ones[:, :], ALU.pow).then_inc(sig["router_step"], 1)
            pool.wait_ge(sig["router_step"], 3)
            nc.gpsimd.tensor_tensor(router[:, :], wnorm[:, 0], wnorm[:, 4], ALU.mult).then_inc(sig["router_step"], 1)
            pool.wait_ge(sig["router_step"], 4)
            nc.gpsimd.tensor_scalar(router16[:, 0], router[:, :], 1.0, 0.0, ALU.mult, ALU.add).then_inc(sig["router_step"], 1)
            pool.wait_ge(sig["router_step"], 5)
            nc.gpsimd.tensor_tensor(router16[:, 1], router[:, :], router16[:, 0], ALU.subtract)\
                .then_inc(sig["router_ready"], 1)
            split_lo("w1", 3)
            split_lo("w2", 4)
            split_lo("wk", 5)
            split_lo("wv", 6)
            split_lo("wq", 7)
            split_lo("wo1", 8)
            for b in range(B):
                pool.wait_ge(sig["ysig"], b + 1)
                nc.gpsimd.tensor_tensor(y[:, b], th[:, b], rden[:, b], ALU.mult).then_inc(sig["y"], 1)
            for b in range(B):
                rstd_of(LN_A, b)
            pool.wait_ge(sig["ffw_c"], 1)
            nc.gpsimd.tensor_scalar(ffw16[:, :, :].rearrange("p k n -> p (k n)"), ffw_in[:, :, :].rearrange("p k n -> p (k n)"),
                                    -MAGIC, 1.0, ALU.add, ALU.mult).then_inc(sig["ffw_ready"], 1)
            pool.wait_ge(sig["ctxT_hi"], 1)
            nc.gpsimd.tensor_tensor(ctxT[:, 1], ctxT_in, ctxT[:, 0], ALU.subtract).then_inc(sig["ctxT_ready"], 1)
            for first in range(0, B, 2):
                for b in (first, first + 1):
                    rstd_of(LN_OUT, b)
                for b in (first, first + 1):
                    rstd_of(LN_FFN, b)
                    rows_shift(LN_FFN, b)
            pool.wait_ge(sig["colmask"], 1)
            nc.gpsimd.tensor_scalar(resmask[:, :, :, :].rearrange("p a t n -> p (a t n)"),
                                    ind[:, :, :, :].rearrange("p a t n -> p (a t n)"), -4 * BIG, 0.0, ALU.mult, ALU.add)\
                .then_inc(sig["resmask"], 1)
            pool.wait_ge(sig["resmask"], 1)
            for b in range(B):
                ins = nc.gpsimd.tensor_tensor(resmask[:, b], resmask[:, b], colmask[:, b].unsqueeze(1).to_broadcast(
                    [P, TILES, T]), ALU.add)
            ins.then_inc(sig["resmask"], 1)
            nc.gpsimd.memset(spread[:, :, :, :], 0.0)
            pool.wait_ge(sig["ff_mm"], B)
            nc.gpsimd.memset(va[:, :, :, :, DK:32], 0.0).then_inc(sig["zeros_ready"], 1)
            pool.wait_ge(sig["zeros_ready"], 1)
            nc.gpsimd.memset(va[:, :, :, :, DK:DK + 1], 1.0).then_inc(sig["zeros_ready"], 1)
            split_lo("m1", 9)
            for b in range(B):
                pool.wait_ge(sig["ascale"], nth(1, b))
                nc.gpsimd.tensor_scalar(g[:, b, 0], g[:, b, 0], amax[:, b, 3, 0:1], MAGIC, ALU.mult, ALU.add)\
                    .then_inc(sig["q2"], 1)
            nc.gpsimd.memset(kz[:, :, :, :], 0.0).then_inc(sig["kz_zero"], 1)
            for b in range(B):
                rstd_of(LN_ATT, b)

            def shift_rows(n):
                b, quad = divmod(n, QUADS)
                pool.wait_ge(sig["smax"], 4 * n + 4)
                if n >= 2:
                    pool.wait_ge(sig["shift_mm"], n - 1)
                for t in range(TILES):
                    ins = nc.gpsimd.tensor_scalar(
                        spread[:, n % 2, t].rearrange("p (g r) -> p g r", g=4)[:, :, 28:32],
                        mx[:, b, 4 * quad:4 * quad + 4, t:t + 1].to_broadcast([P, 4, 4]),
                        -1.0 / (4 * BIG), 0.0, ALU.mult, ALU.add)
                ins.then_inc(sig["spread"], 1)

            def separated_keys(n):
                b, quad = divmod(n, QUADS)
                pool.wait_ge(sig["ka_ready"], B + b + 1)
                if n >= KRING:
                    pool.wait_ge(sig["st_mm"], 4 * (n - KRING + 1))
                for k in range(4):
                    part = slice(32 * k, 32 * k + 32)
                    ins = nc.gpsimd.tensor_scalar(kz[part, n % KRING, k], ka[part, b, quad], 1.0, 0.0, ALU.mult, ALU.add)
                ins.then_inc(sig["kz_ready"], 1)

            pool.wait_ge(sig["kz_zero"], 1)
            pool.wait_ge(sig["ln_rstd"], nth_norm(LN_ATT, B - 1))
            for n in range(KRING):
                separated_keys(n)
            pool.wait_ge(sig["kz_ready"], KRING)
            shift_rows(0)
            shift_rows(1)
            for n in range(B * QUADS):
                if n in POOL_ROOTS:
                    rstd_of(LN_MOE, POOL_ROOTS.index(n))
                    rows_shift(LN_MOE, POOL_ROOTS.index(n))
                if n + 2 < B * QUADS:
                    shift_rows(n + 2)
                if n + KRING < B * QUADS:
                    pool.wait_ge(sig["spread"], n + 3)
                    separated_keys(n + KRING)
                    pool.wait_ge(sig["kz_ready"], n + KRING + 1)
                if n == B * QUADS - KRING:
                    split_lo("m2", 10)
            for b in range(len(POOL_ROOTS), B):
                rstd_of(LN_MOE, b)
                rows_shift(LN_MOE, b)

        @block.scalar
        def _(act):
            nc_act = nc.scalar.activation
            act.dma_start(ctx_in[:, :, :, :], ctx_rows).then_inc(sig["l_ctx"], 16)
            act.dma_start(gamma_b[:, :], gamma.partition_broadcast(P)).then_inc(sig["l_gb"], 16)
            act.dma_start(beta_b[:, :], beta.partition_broadcast(P)).then_inc(sig["l_gb"], 16)
            act.dma_start(bias_in[:, :], bias).then_inc(sig["l_bias"], 16)
            act.dma_start(mbias_in[:, :], mbias).then_inc(sig["l_mbias"], 16)

            def split_hi(name):
                a, z = SEG[name]
                act.wait_ge(sig["l_" + name], 16)
                nc_act(w16[:, 0, a:z], wf32(name), ACT.Copy).then_inc(sig["w_hi"], 1)

            split_hi("qkv")
            act.wait_ge(sig["l_bias"], 16)

            def bias_hi(k):
                cols = slice(*BPARTS[k])
                nc_act(bias_h[:, cols], bias_in[:, cols], ACT.Copy).then_inc(sig["bias_hi"], 1)

            bias_hi(0)
            for b in range(B):
                act.wait_ge(sig["turned"], nth(T_EMB, b))
                nc_act(colsA[:, 0, b], bank(b, 0)[:, 0:T], ACT.Copy).then_inc(sig["cols_hi"], 1)
            act.wait_ge(sig["pos_max"], 1)
            for t in range(TILES):
                nc_act(ew[:, t], posw[:, t], ACT.Exp, bias=posmax[:, t:t + 1]).then_inc(sig["ew_done"], 1)
            bias_hi(1)
            act.wait_ge(sig["ewT_mm"], 1)
            nc_act(ewT[:, 0], bank(3, 1).rearrange("p (a n) -> p a n", a=TILES), ACT.Copy).then_inc(sig["ewT_hi"], 1)
            split_hi("wo")
            act.wait_ge(sig["l_ffw"], 16)
            for k in range(3):
                if k:
                    act.wait_ge(sig["absum"], k)
                nc_act(junk[:, :], ffw_in[:, k], ACT.Abs, accum_out=absum[:, k:k + 1]).then_inc(sig["absum"], 1)
            for b in range(B):
                act.wait_ge(sig["kshift"], b + 1)
                qk = bank(b, 0).rearrange("p (t n) -> p t n", t=TILES)
                nc_act(th[:, b], qk[:, :, 0:D], ACT.Tanh, scale=0.5)
                nc_act(eb[:, b, :, D:2 * D], qk[:, :, D:2 * D], ACT.Exp).then_inc(sig["ek"], 1)
            for b in range(B):
                act.wait_ge(sig["ekv"], b + 1)
                nc_act(eb16[:, 0, b], eb[:, b], ACT.Copy).then_inc(sig["eb_hi"], 1)
            act.wait_ge(sig["l_mbias"], 16)
            nc_act(mbias_h[:, :], mbias_in[:, :], ACT.Copy).then_inc(sig["mbias_hi"], 1)
            for name in ("w1", "w2", "wk", "wv", "wq", "wo1"):
                split_hi(name)
            for b in range(B):
                act.wait_ge(sig["turned"], nth(T_Y, b))
                nc_act(colsY[:, 0, b], bank(b, 1)[:, 0:T], ACT.Copy).then_inc(sig["cols_hi"], 1)

            def act_rows(ln, b, src):
                act.wait_ge(sig["ln_nmr"], NMR_TURN[ln] * B + b + 1)
                for t in range(TILES):
                    ins = nc_act(rows[:, b, t], src(t), ACT.Identity, scale=rstd[:, ln, b, t:t + 1],
                                 bias=nmr[:, ln, b, t:t + 1])
                ins.then_inc(sig["rows_act"], 1)

            for b in range(B):
                act.wait_ge(sig["turned"], nth(T_A, b))
                nc_act(a32[:, b], bank(b, 1)[:, 0:T], ACT.Identity, scale=gamma_col, bias=beta_col)
                nc_act(colsN[:, 0, b], bank(b, 1)[:, 0:T], ACT.Identity, scale=gamma_col, bias=beta_col)\
                    .then_inc(sig["cols_hi"], 1)
            act.wait_ge(sig["l_ctxT"], 16)
            nc_act(ctxT[:, 0], ctxT_in, ACT.Copy).then_inc(sig["ctxT_hi"], 1)
            for b in range(B):
                act.wait_ge(sig["hid_mm"], b + 1)
                nc_act(hid16[:, 0, b], pair(b), ACT.Relu).then_inc(sig["hid_hi"], 1)
            act.wait_ge(sig["count_mm"], 1)
            act.wait_ge(sig["ones_ready"], 1)
            for a in range(2):
                cols = slice(2 * a, 2 * a + 2)
                nc_act(colrow[:, cols].rearrange("p b n -> p (b n)"), bank(a, 1)[0:1], ACT.Relu, scale=BIG,
                       bias=all_masked[0:1, 0:1])
                nc_act(colmask[:, cols].rearrange("p b n -> p (b n)"), bank(a, 1), ACT.Relu, scale=4 * BIG,
                       bias=all_masked[:, 1:2], accum_out=mask_sums[:, 2 * a:2 * a + 1])
                ins = nc_act(cnt[:, a * 2 * T:(a + 1) * 2 * T], bank(a, 1), ACT.Copy, accum_out=mask_sums[:, 2 * a + 1:2 * a + 2])
            ins.then_inc(sig["colmask"], 1)
            split_hi("m1")
            nc_act(silu_junk[:, :], all_masked[:, 0:1], ACT.Silu)

            def key_hi(b, half_no):
                act.wait_ge(sig["kproj"], half_no * B + b + 1)
                nc_act(kh[:, b].rearrange("p h n -> p (h n)"), bank(b, 1), ACT.Copy).then_inc(sig["ka_hi"], 1)

            for b in range(B):
                act.wait_ge(sig["vproj"], b + 1)
                for t in range(TILES):
                    ins = nc_act(va[:, b, t, :, 0:DK],
                                 bank(b, 1)[:, t * D:(t + 1) * D].rearrange("p (h k) -> p h k", h=NH), ACT.Copy)
                ins.then_inc(sig["va_ready"], 1)

            def round_rows(b):
                act.wait_ge(sig["ascale"], nth(0, b))
                for t in range(TILES):
                    ins = nc_act(rows[:, b, t], rows[:, b, t], ACT.Copy, scale=amax[:, b, 1, t:t + 1], bias=MAGIC)
                ins.then_inc(sig["q1"], 1)

            for b in range(B):
                act_rows(LN_FFN, b, lambda t: x1[:, b, t])
                if b == B - 1:
                    round_rows(0)
                    round_rows(1)
                key_hi(b, 0)
            round_rows(2)
            round_rows(3)
            for b in range(B):
                act.wait_ge(sig["turned"], nth(T_QUANT, b))
                nc_act(qT[:, b], bank(b, 0)[:, 0:T], ACT.Copy, bias=-MAGIC).then_inc(sig["q1T_ready"], 1)

            def round_gated(b):
                act.wait_ge(sig["ascale"], nth(1, b))
                nc_act(g[:, b, 1], g[:, b, 1], ACT.Copy, scale=amax[:, b, 3, 1:2], bias=MAGIC).then_inc(sig["q2_act"], 1)

            for u, (b, t) in enumerate(GU_ORDER):
                act.wait_ge(sig["gu_mm"], u + 1)
                act.wait_ge(sig["gscale"], b + 1)
                if t:
                    act.wait_ge(sig["g"], u - 1)
                nc_act(silu[:, b], bank(b, 0), ACT.Silu, scale=fac[:, b, 0, t:t + 1]).then_inc(sig["silu"], 1)
                if (b, t) in ((2, 1), (3, 1)):
                    round_gated(b - 2)
            for b in range(2, B):
                round_gated(b)
            for b in range(B):
                act.wait_ge(sig["q2T_mm"], b + 1)
                nc_act(gT[:, b].rearrange("p t c n -> p (t c n)"), pair(b).rearrange("p a n -> p (a n)"), ACT.Copy,
                       bias=-MAGIC).then_inc(sig["q2T_ready"], 1)
            split_hi("m2")
            for b in range(B):
                key_hi(b, 1)
            act.wait_ge(sig["resmask"], 2)
            for b in range(B):
                act.wait_ge(sig["turned"], nth(T_QUERY, b))
                nc_act(colsA[:, 0, b], bank(b, 0)[:, 0:T], ACT.Copy).then_inc(sig["cols_hi"], 1)
            for b in range(B):
                act.wait_ge(sig["q_mm"], b + 1)
                nc_act(qh[:, b].rearrange("p h n -> p (h n)"), pair(b).rearrange("p a n -> p (a n)"), ACT.Copy)\
                    .then_inc(sig["qa_hi"], 1)
            def out_copy(m):
                act.wait_ge(sig["pv"], 2 * m + 2)
                b, half = divmod(m, 2)
                nc_act(oT[:, b, 2 * half:2 * half + 2].rearrange("p h n -> p (h n)"), ps[:, 4 + m % 2, :], ACT.Copy)\
                    .then_inc(sig["oT"], 1)

            def tail_rows(b):
                act_rows(LN_MOE, b, lambda t: x3[:, b, t])

            def tail_act(b, step):
                tb = tail_bank(b)
                if step == 2:
                    act.wait_ge(sig["turned"], nth_of_tail(T_TAIL, b, False))
                    nc_act(colsY[:, 0, b], tb[:, 0:T], ACT.Copy).then_inc(sig["cols_hi"], 1)
                if step == 4:
                    act.wait_ge(sig["turned"], nth_of_tail(T_TAIL, b, True))
                    nc_act(colsN[:, 0, b], tb[:, 0:T], ACT.Copy).then_inc(sig["cols_hi"], 1)
                if step == 6:
                    act.wait_ge(sig["topix"], b + 1)
                    for t in range(TILES):
                        ins = nc_act(ejunk[:, b, t], logits[:, b, t], ACT.Exp, bias=ntop[:, b, t:t + 1],
                                     accum_out=esum[:, b, t:t + 1])
                    ins.then_inc(sig["expsum"], 1)
                    act.wait_ge(sig["ohT_mm"], b + 1)
                    nc_act(ohT[:, b], tb[0:2 * NE, 0:T], ACT.Copy).then_inc(sig["ohT"], 1)

            def shifted_query(n):
                act.wait_ge(sig["shift_mm"], n + 1)
                if n >= 2:
                    act.wait_ge(sig["st_mm"], 4 * (n - 1))
                nc_act(qb[:, n % 2], ps[:, 6, 0:T], ACT.Copy).then_inc(sig["qb"], 1)

            shifted_query(0)
            def onehot_copy(b, half):
                act.wait_ge(sig["oh_mm"], 2 * b + half + 1)
                if b >= 2:
                    act.wait_ge(sig["xm"], b - 1)
                nc_act(oh[:, b % 2, 4 * half:4 * half + 4].rearrange("p e n -> p (e n)"),
                       pair(ONEHOT_PAIRS[b]).rearrange("p a n -> p (a n)"), ACT.Copy).then_inc(sig["oh"], 1)

            for n in range(B * QUADS):
                for k in range(4):
                    head = 4 * n + k
                    if k == 2 and n + 1 < B * QUADS:
                        shifted_query(n + 1)
                    act.wait_ge(sig["st_mm"], head + 1)
                    if head >= PRING:
                        act.wait_ge(sig["pv"], (head - PRING) // 4 + 1)
                    nc_act(pt[:, head % PRING].rearrange("p t n -> p (t n)"), ps[:, 2 + head % 2, :], ACT.Exp,
                           scale=DK ** -0.5).then_inc(sig["probs"], 1)
                    if tail_at(n, k):
                        tail_act(*tail_at(n, k))
                    if 0 <= tail_place(n, k)[0] < B - 1 and tail_place(n, k)[1] == TAIL_ROWS:
                        tail_rows(tail_place(n, k)[0])
                    if (n, k) in ONEHOT_AT:
                        onehot_copy(*ONEHOT_AT[n, k])
                if n >= 2 and n % 2 == 0:
                    out_copy(n // 2 - 1)
            out_copy(B * QUADS // 2 - 1)

            def gelu(b):
                act.wait_ge(sig["moe_h"], b + 1)
                nc_act(gelu32[:, b].rearrange("p c n -> p (c n)"), bank(b, 0), ACT.Gelu).then_inc(sig["gelu"], 1)
                act.wait_ge(sig["gelu"], b + 1)
                nc_act(gelu16[:, 0, b], gelu32[:, b], ACT.Copy).then_inc(sig["gelu_hi"], 1)

            tail_act(2, 4)
            tail_act(2, 6)
            tail_act(3, 2)
            onehot_copy(2, 0)
            gelu(0)
            tail_rows(3)
            onehot_copy(2, 1)
            gelu(1)
            tail_act(3, 4)
            tail_act(3, 6)
            onehot_copy(3, 0)
            onehot_copy(3, 1)
            gelu(2)
            gelu(3)

        @block.vector
        def _(dve):
            V = nc.vector

            def ln_stats(ln, b, src):
                for t in range(TILES):
                    ins = V.bn_stats(stats[:, ln, b, t], src(t))
                ins.then_inc(sig["ln_stats"], 1)

            def ln_moments(ln, b):
                dve.wait_ge(sig["ln_stats"], nth_norm(ln, b))
                for t in range(TILES):
                    ins = V.bn_aggr(moments[:, ln, b, t], stats[:, ln, b, t])
                ins.then_inc(sig["ln_moments"], 1)

            def ln_rows(ln, b, src):
                dve.wait_ge(sig["ln_rstd"], nth_norm(ln, b))
                for t in range(TILES):
                    ins = V.tensor_scalar(rows[:, b, t], src(t), moments[:, ln, b, t, 0:1], rstd[:, ln, b, t:t + 1],
                                          ALU.subtract, ALU.mult)
                ins.then_inc(sig["rows_ready"], 1)

            def lo_part(dst, src, hi, done):
                V.tensor_tensor(dst, src, hi, ALU.subtract).then_inc(sig[done], 1)

            def split_lo(name, n):
                a, z = SEG[name]
                dve.wait_ge(sig["w_hi"], n)
                lo_part(w16[:, 1, a:z], wf32(name), w16[:, 0, a:z], "w_lo")

            for b in range(B):
                dve.wait_ge(sig[f"l_x{b}"], 16)
                ln_stats(LN_IN, b, lambda t: x_in[:, b, t])
                ln_moments(LN_IN, b)
            dve.wait_ge(sig["l_cst"], 16)
            V.tensor_copy(id16[:, :], ident)
            V.tensor_scalar(idbig[:, :], ident, BIG, None, ALU.mult)
            V.tensor_copy(sel16[:, :], c("sel", 1)).then_inc(sig["id_ready"], 1)
            for b in range(B):
                ln_rows(LN_IN, b, lambda t: x_in[:, b, t])
            split_lo("qkv", 1)
            cols = slice(*BPARTS[0])
            dve.wait_ge(sig["bias_hi"], 1)
            V.scalar_tensor_tensor(bias16[:, cols], bias_h[:, cols], c("lo_2", 2), bias_in[:, cols], ALU.mult, ALU.add)\
                .then_inc(sig["bias_ready"], 1)
            for b in range(B):
                dve.wait_ge(sig["cols_hi"], nth(C_EMB, b))
                lo_part(colsA[:, 1, b], bank(b, 0)[:, 0:T], colsA[:, 0, b], "cols_ready")
            dve.wait_ge(sig["pos_masked"], 1)
            V.tensor_reduce(posmax[:, :], posw[:, :, :], AX.X, ALU.max, negate=True).then_inc(sig["pos_max"], 1)
            for b in range(B):
                if b == 2:
                    dve.wait_ge(sig["ewT_hi"], 1)
                    lo_part(ewT[:, 1], bank(3, 1).rearrange("p (a n) -> p a n", a=TILES), ewT[:, 0], "ewT_ready")
                dve.wait_ge(sig["kT_mm"], b + 1)
                V.tensor_reduce(kmx[:, b, 0:1], bank(b, 1)[:, T:2 * T], AX.X, ALU.max).then_inc(sig["kmax"], 1)
                dve.wait_ge(sig["kmax"], b + 1)
                V.tensor_scalar(kmx[:, b, 1:2], kmx[:, b, 0:1], bk_col, -1.0, ALU.add, ALU.mult)\
                    .then_inc(sig["kmaxb"], 1)
                dve.wait_ge(sig["kmaxb"], b + 1)
                V.tensor_scalar(kdiag[:, b], ident, kmx[:, b, 1:2], None, ALU.mult).then_inc(sig["kdiag"], 1)
            split_lo("wo", 2)
            dve.wait_ge(sig["means_ready"], 1)
            V.tensor_copy(wnorm[:, 0:2], bank(3, 1)[:, T + NE:T + 3 * NE].rearrange("p (a n) -> p a n", a=2))
            V.tensor_scalar(mean[:, :], bank(3, 1)[:, T:T + 3], 1.0 / (HID * D), 1e-5, ALU.mult, ALU.max)\
                .then_inc(sig["meanc"], 1)
            dve.wait_ge(sig["meanc"], 1)
            V.reciprocal(wscale[:, :], mean[:, :]).then_inc(sig["ffscale"], 1)
            for b in range(B):
                dve.wait_ge(sig["ek"], b + 1)
                V.scalar_tensor_tensor(eb[:, b, :, 0:D], eb[:, b, :, D:2 * D], 0.5,
                                       bank(b, 1)[:, 0:2 * D].rearrange("p (t n) -> p t n", t=TILES), ALU.mult, ALU.mult)\
                    .then_inc(sig["ekv"], 1)
            for b in range(B):
                dve.wait_ge(sig["eb_hi"], b + 1)
                lo_part(eb16[:, 1, b], eb[:, b], eb16[:, 0, b], "eb_lo")
            for b in range(B):
                nd = bank(b, 0).rearrange("p (t n) -> p t n", t=TILES)
                dve.wait_ge(sig["numden"], b + 1)
                V.reciprocal(rden[:, b], nd[:, :, D:2 * D])
                V.scalar_tensor_tensor(th[:, b], th[:, b], 1.0, nd[:, :, 0:D], ALU.add, ALU.mult)\
                    .then_inc(sig["ysig"], 1)
            for b in range(B):
                dve.wait_ge(sig["cols_hi"], nth(C_Y, b))
                lo_part(colsY[:, 1, b], bank(b, 1)[:, 0:T], colsY[:, 0, b], "cols_ready")
            for b in range(B):
                dve.wait_ge(sig["attn_mm"], b + 1)
                ln_stats(LN_A, b, lambda t: bank(b, 0)[:, t * D:(t + 1) * D])
                ln_moments(LN_A, b)
            for b in range(B):
                ln_rows(LN_A, b, lambda t: bank(b, 0)[:, t * D:(t + 1) * D])
            for b in range(B):
                dve.wait_ge(sig["cols_hi"], nth(C_A, b))
                lo_part(colsN[:, 1, b], a32[:, b], colsN[:, 0, b], "cols_ready")
            dve.wait_ge(sig["mbias_hi"], 1)
            V.scalar_tensor_tensor(mbias16[:, :], mbias_h[:, :], c("lo_16", 2 * NE), mbias_in[:, :], ALU.mult, ALU.add)\
                .then_inc(sig["mbias_ready"], 1)
            dve.wait_ge(sig["ffw_r"], 1)
            V.tensor_scalar(ffw_in[:, :, :].rearrange("p k n -> p (k n)"), ffw_in[:, :, :].rearrange("p k n -> p (k n)"),
                            MAGIC + 1.0, MAGIC - 1.0, ALU.min, ALU.max).then_inc(sig["ffw_c"], 1)
            dve.wait_ge(sig["y"], B)
            dve.wait_ge(sig["l_mask"], 16)
            V.tensor_scalar(ind[:, :, :, :].rearrange("p a t n -> p (a t n)"), mask_in.rearrange("p a t n -> p (a t n)"),
                            0.0, None, ALU.is_equal).then_inc(sig["mask_ind"], 1)
            for b in range(B):
                dve.wait_ge(sig["hid_hi"], b + 1)
                V.scalar_tensor_tensor(hid16[:, 1, b].rearrange("p c n -> p (c n)"), pair(b).rearrange("p a n -> p (a n)"),
                                       0.0, hid16[:, 0, b].rearrange("p c n -> p (c n)"), ALU.max, ALU.subtract)\
                    .then_inc(sig["hid_ready"], 1)
            for first in range(0, B, 2):
                two = (first, first + 1)
                for b in two:
                    dve.wait_ge(sig["ff_mm"], b + 1)
                    ln_stats(LN_OUT, b, lambda t: bank(b, 0)[:, t * D:(t + 1) * D])
                    ln_moments(LN_OUT, b)
                for b in two:
                    dve.wait_ge(sig["xb"], b + 1)
                    dve.wait_ge(sig["ln_moments"], nth_norm(LN_OUT, b))
                    for t in range(TILES):
                        ins = V.scalar_tensor_tensor(nb[:, b, t], bank(b, 0)[:, t * D:(t + 1) * D],
                                                     moments[:, LN_OUT, b, t, 0:1], gamma_b[:, :], ALU.subtract, ALU.mult)
                    ins.then_inc(sig["nb"], 1)
                for b in two:
                    dve.wait_ge(sig["nb"], b + 1)
                    dve.wait_ge(sig["ln_rstd"], nth_norm(LN_OUT, b))
                    for t in range(TILES):
                        ins = V.scalar_tensor_tensor(x1[:, b, t], nb[:, b, t], rstd[:, LN_OUT, b, t:t + 1], xb[:, b, t],
                                                     ALU.mult, ALU.add)
                    ins.then_inc(sig["x1"], 1)
                for b in two:
                    dve.wait_ge(sig["x1"], b + 1)
                    ln_stats(LN_FFN, b, lambda t: x1[:, b, t])
                for b in two:
                    ln_moments(LN_FFN, b)

            def key_lo(b, half_no):
                dve.wait_ge(sig["ka_hi"], half_no * B + b + 1)
                V.scalar_tensor_tensor(ka[:, b, 2 * half_no:2 * half_no + 2].rearrange("p h n -> p (h n)"),
                                       kh[:, b].rearrange("p h n -> p (h n)"), c("lo_k"), bank(b, 1), ALU.mult, ALU.add)\
                    .then_inc(sig["ka_ready"], 1)

            def quant_scale(b, row):
                dve.wait_ge(sig["amax"], B + 1 + GU_ORDER.index((b, 1)) if row else b + 1)
                V.tensor_scalar(amax[:, b, row, :], amax[:, b, row, :], 1e-5, 1.0 / 127.0, ALU.max, ALU.mult)\
                    .then_inc(sig["amaxc"], 1)
                dve.wait_ge(sig["amaxc"], nth(row // 2, b))
                V.reciprocal(amax[:, b, row + 1, :], amax[:, b, row, :]).then_inc(sig["ascale"], 1)

            for b in range(B):
                dve.wait_ge(sig["rows_act"], nth(NMR_TURN[LN_FFN], b))
                V.tensor_reduce(amax[:, b, 0, :], rows[:, b], AX.X, ALU.max, apply_absolute_value=True)\
                    .then_inc(sig["amax"], 1)
                if b == B - 1:
                    quant_scale(b, 0)
                key_lo(b, 0)
                if b < B - 1:
                    quant_scale(b, 0)
            for b in range(B):
                V.tensor_scalar(fac[:, b, 0, :], amax[:, b, 0, :], mean[:, 0:1], None, ALU.mult)
                V.tensor_scalar(fac[:, b, 1, :], amax[:, b, 0, :], mean[:, 1:2], None, ALU.mult).then_inc(sig["gscale"], 1)
            dve.wait_ge(sig["colmask"], 1)
            V.tensor_tensor(flag_f[:, 0:2], mask_sums[0:1, 0:2], mask_sums[0:1, 2:4], ALU.add).then_inc(sig["flagsum"], 1)
            dve.wait_ge(sig["flagsum"], 1)
            V.scalar_tensor_tensor(flag_f[:, 2:3], flag_f[:, 0:1], -T / (4 * BIG), flag_f[:, 1:2], ALU.mult, ALU.add)\
                .then_inc(sig["flagstep"], 1)
            dve.wait_ge(sig["flagstep"], 1)
            V.tensor_copy(flag_i[:, :], flag_f[:, 2:3]).then_inc(sig["flag_ready"], 1)
            def gate_max(u):
                b, t = GU_ORDER[u]
                dve.wait_ge(sig["g"], u + 1)
                V.tensor_reduce(amax[:, b, 2, t:t + 1], g[:, b, t], AX.X, ALU.max, apply_absolute_value=True)\
                    .then_inc(sig["amax"], 1)

            dve.wait_ge(sig["gscale"], B)
            for u, (b, t) in enumerate(GU_ORDER):
                dve.wait_ge(sig["silu"], u + 1)
                V.scalar_tensor_tensor(g[:, b, t], silu[:, b], fac[:, b, 1, t:t + 1], bank(b, 1), ALU.mult, ALU.mult)\
                    .then_inc(sig["g"], 1)
                if u:
                    gate_max(u - 1)
                if u == 4:
                    quant_scale(0, 2)
                if u == 5:
                    quant_scale(1, 2)
            gate_max(len(GU_ORDER) - 1)
            for b in range(2, B):
                quant_scale(b, 2)
            for b in range(B):
                V.tensor_scalar(fac[:, b, 2, :], amax[:, b, 2, :], mean[:, 2:3], None, ALU.mult).then_inc(sig["kscale"], 1)
            for b in range(B):
                dve.wait_ge(sig["down_mm"], b + 1)
                dve.wait_ge(sig["kscale"], b + 1)
                for t in range(TILES):
                    ins = V.scalar_tensor_tensor(x2[:, b, t], bank(b, 0)[:, t * D:(t + 1) * D], fac[:, b, 2, t:t + 1],
                                                 x1[:, b, t], ALU.mult, ALU.add)
                ins.then_inc(sig["x2"], 1)
                if b:
                    dve.wait_ge(sig["x2"], b)
                    ln_stats(LN_ATT, b - 1, lambda t: x2[:, b - 1, t])
                if b > 1:
                    ln_moments(LN_ATT, b - 2)
            dve.wait_ge(sig["x2"], B)
            ln_stats(LN_ATT, B - 1, lambda t: x2[:, B - 1, t])
            ln_moments(LN_ATT, B - 2)
            ln_moments(LN_ATT, B - 1)
            for b in range(B):
                ln_rows(LN_ATT, b, lambda t: x2[:, b, t])
                if b in (1, 2):
                    key_lo(b - 1, 1)
            for b in range(B):
                if b > 1:
                    key_lo(b, 1)
                dve.wait_ge(sig["cols_hi"], nth(C_QUERY, b))
                lo_part(colsA[:, 1, b], bank(b, 0)[:, 0:T], colsA[:, 0, b], "cols_ready")
            def query_lo(b):
                dve.wait_ge(sig["qa_hi"], b + 1)
                V.scalar_tensor_tensor(qa[:, b].rearrange("p h n -> p (h n)"), qh[:, b].rearrange("p h n -> p (h n)"),
                                       c("lo_q"), pair(b).rearrange("p a n -> p (a n)"), ALU.mult, ALU.add)\
                    .then_inc(sig["qa_ready"], 1)

            def head_max(n, i):
                b, quad = divmod(n, QUADS)
                t, pair_of = divmod(i, 2)
                head = 4 * quad + 2 * pair_of
                dve.wait_ge(sig["s_mm"], 4 * n + i + 1)
                V.tensor_reduce(mx[:, b, head:head + 2, t], score_bank(4 * n + i).rearrange("p (h n) -> p h n", h=2),
                                AX.X, ALU.max).then_inc(sig["smax"], 1)

            query_lo(0)
            query_lo(1)
            for k in range(4):
                head_max(0, k)
                if k == 1:
                    query_lo(2)
            query_lo(3)
            for k in range(4):
                head_max(1, k)

            def tail_dve(b, step):
                tb = tail_bank(b)
                if step < TILES:
                    heads = tb.rearrange("p (h r) -> p h r", h=NH)
                    dve.wait_ge(sig["oR_mm"], TILES * b + step + 1)
                    V.reciprocal(oden[:, b, step], heads[:, :, DK]).then_inc(sig["oden"], 1)
                    dve.wait_ge(sig["oden"], TILES * b + step + 1)
                    V.tensor_tensor(attn[:, b, step].rearrange("p (h k) -> p h k", h=NH), heads[:, :, 0:DK],
                                    oden[:, b, step].unsqueeze(2).to_broadcast([P, NH, DK]), ALU.mult)\
                        .then_inc(sig["attn"], 1)
                if step == 2:
                    dve.wait_ge(sig["cols_hi"], nth_of_tail(C_TAIL, b, False))
                    lo_part(colsY[:, 1, b], tb[:, 0:T], colsY[:, 0, b], "cols_ready")
                if step == 3:
                    dve.wait_ge(sig["wo1_mm"], b + 1)
                    V.tensor_tensor(x3[:, b].rearrange("p t n -> p (t n)"), tb[:, 0:T],
                                    x2[:, b].rearrange("p t n -> p (t n)"), ALU.add).then_inc(sig["x3"], 1)
                    dve.wait_ge(sig["x3"], b + 1)
                    ln_stats(LN_MOE, b, lambda t: x3[:, b, t])
                    ln_moments(LN_MOE, b)
                if step == 4:
                    dve.wait_ge(sig["cols_hi"], nth_of_tail(C_TAIL, b, True))
                    lo_part(colsN[:, 1, b], tb[:, 0:T], colsN[:, 0, b], "cols_ready")
                if step == 5:
                    dve.wait_ge(sig["logit_mm"], b + 1)
                    V.tensor_copy(logits[:, b], tb[:, 0:TILES * NE].rearrange("p (t e) -> p t e", t=TILES))\
                        .then_inc(sig["logits"], 1)
                    dve.wait_ge(sig["logits"], b + 1)
                    for t in range(TILES):
                        ins = V.max(top8[:, b, t], logits[:, b, t])
                    ins.then_inc(sig["top8"], 1)
                    dve.wait_ge(sig["top8"], b + 1)
                    V.tensor_scalar(ntop[:, b], top8[:, b, :, 0], -1.0, None, ALU.mult)
                    for t in range(TILES):
                        ins = V.max_index(topix[:, b, t], top8[:, b, t], logits[:, b, t])
                    ins.then_inc(sig["topix"], 1)
                    dve.wait_ge(sig["topix"], b + 1)
                    for t in range(TILES):
                        ins = V.tensor_scalar(onehot[:, b, t], c("iota"), topix[:, b, t, 0:1], None, ALU.is_equal)
                    ins.then_inc(sig["onehot"], 1)

            def masked_tokens(b):
                dve.wait_ge(sig["oh"], 2 * b + 2)
                if b >= 2:
                    dve.wait_ge(sig["moe_h"], b - 1)
                for part in range(2):
                    V.tensor_tensor(xm[b % 2][:, part], oh[:, b % 2],
                                    colsN[:, part, b].unsqueeze(1).to_broadcast([P, NE, T]), ALU.mult)\
                        .then_inc(sig["xm" if part else "xm_hi"], 1)

            for n in range(B * QUADS):
                for k in range(4):
                    if n + 2 < B * QUADS:
                        head_max(n + 2, k)
                    now, before = tail_at(n, k), tail_at(*divmod(4 * n + k - 1, 4))
                    if now and now[1] not in (2, 4):
                        tail_dve(*now)
                    if before and before[1] in (2, 4):
                        tail_dve(*before)
                    if (n, k) == (B * QUADS - 1, 0):
                        masked_tokens(0)

            def gates(b):
                dve.wait_ge(sig["expsum"], b + 1)
                V.reciprocal(score[:, b], esum[:, b]).then_inc(sig["score"], 1)
                dve.wait_ge(sig["onehot"], b + 1)
                dve.wait_ge(sig["score"], b + 1)
                for t in range(TILES):
                    ins = V.tensor_scalar(wsel[:, b, t], onehot[:, b, t, 0:NE], score[:, b, t:t + 1], None, ALU.mult)
                ins.then_inc(sig["wsel"], 1)

            def gelu_lo(b):
                dve.wait_ge(sig["gelu_hi"], b + 1)
                lo_part(gelu16[:, 1, b], gelu32[:, b], gelu16[:, 0, b], "gelu_ready")
                for t in range(TILES):
                    ins = V.scalar_tensor_tensor(y0[:, b, t], bank(b, 1)[:, t * D:(t + 1) * D], score[:, b, t:t + 1],
                                                 x3[:, b, t], ALU.mult, ALU.add)
                ins.then_inc(sig["y0"], 1)

            def pick(u):
                b, t = divmod(u, TILES)
                pair_of = OUT_PAIRS[u]
                dve.wait_ge(sig["moe_o"], u + 1)
                dve.wait_ge(sig["wsel"], b + 1)
                if u >= 2:
                    dve.wait_ge(sig["picksum"], u - 1)
                V.tensor_tensor(picked[:, u % 2], pair(pair_of).rearrange("p a (e n) -> p (a e) n", n=D),
                                wsel[:, b, t].unsqueeze(2).to_broadcast([P, NE, D]), ALU.mult)\
                    .then_inc(sig["picked"], 1)
                dve.wait_ge(sig["picked"], u + 1)
                if u >= 2:
                    dve.wait_ge(sig["y_out"], u - 1)
                V.tensor_reduce(picksum[:, u % 2], picked[:, u % 2].rearrange("p e n -> p n e"), AX.X, ALU.add)\
                    .then_inc(sig["picksum"], 1)
                dve.wait_ge(sig["picksum"], u + 1)
                dve.wait_ge(sig["y0"], b + 1)
                V.tensor_tensor(res[:, b, t], picksum[:, u % 2], y0[:, b, t], ALU.add).then_inc(sig["y_out"], 1)

            tail_dve(2, 4)
            masked_tokens(1)
            tail_dve(3, 0)
            tail_dve(2, 5)
            tail_dve(3, 1)
            gates(0)
            gates(1)
            tail_dve(3, 2)
            tail_dve(3, 3)
            gelu_lo(0)
            masked_tokens(2)
            gelu_lo(1)
            tail_dve(3, 4)
            tail_dve(3, 5)
            pick(0)
            gates(2)
            masked_tokens(3)
            gelu_lo(2)
            pick(1)
            gates(3)
            pick(2)
            gelu_lo(3)
            for u in range(3, B * TILES):
                pick(u)

        @block.tensor
        def _(pe):
            def mm(dst, lhsT, rhs, start, stop):
                return nc.tensor.matmul(dst, lhsT, rhs, start=start, stop=stop, skip_group_check=True)

            def product(dst, lhsT, rhs, start=True, stop=True):
                for n, (i, j) in enumerate(PASSES):
                    ins = mm(dst, lhsT(i), rhs(j), start and n == 0, stop and n == len(PASSES) - 1)
                return ins

            def transposed(dst, src):
                return nc.tensor.transpose(dst, src, ident)

            def row_bias(dst, name, stop=True):
                return mm(dst, ones16[0:2, 0:P], brow(name), False, stop)

            pe.wait_ge(sig["l_cst"], 16)
            for b in range(B):
                pe.wait_ge(sig["emb"], b + 1)
                for t in range(TILES):
                    ins = transposed(bank(b, 0)[:, t * P:(t + 1) * P], emb[:, b, t])
                ins.then_inc(sig["turned"], 1)
            pe.wait_ge(sig["w_lo"], 1)
            pe.wait_ge(sig["bias_ready"], 1)
            for b in range(B):
                if b == B - 2:
                    pe.wait_ge(sig["ew_done"], TILES)
                    for j in range(TILES):
                        for t in range(TILES):
                            ins = transposed(bank(3, 1)[:, j * T + t * P:j * T + (t + 1) * P], ew[:, t, j * P:(j + 1) * P])
                    ins.then_inc(sig["ewT_mm"], 1)
                if b == B - 1:
                    pe.wait_ge(sig["ewT_ready"], 1)
                pe.wait_ge(sig["cols_ready"], nth(C_EMB, b))
                product(bank(b, 1)[:, T:2 * T], lambda i: w("qkv", i)[:, D:2 * D], lambda j: colsA[:, j, b])
                for t in range(TILES):
                    tok = slice(t * P, (t + 1) * P)
                    dst = bank(b, 1)[:, t * D:(t + 1) * D]
                    product(dst, lambda i: colsA[:, i, b, tok], lambda j: w("qkv", j)[:, 2 * D:3 * D], stop=False)
                    ins = mm(dst, ones16[0:2, 0:P], brow("qkv")[:, 2 * D:3 * D], False, True)
                ins.then_inc(sig["kT_mm"], 1)
                for t in range(TILES):
                    tok = slice(t * P, (t + 1) * P)
                    dst = bank(b, 0)[:, t * 2 * D:(t + 1) * 2 * D]
                    product(dst, lambda i: colsA[:, i, b, tok], lambda j: w("qkv", j)[:, 0:2 * D], start=t == 0,
                            stop=False)
                    ins = mm(dst, ones16[0:2, 0:P], brow("qkv")[:, 0:2 * D], False, False)
            pe.wait_ge(sig["ones_ready"], 1)
            for b in range(B):
                pe.wait_ge(sig["kdiag"], b + 1)
                for t in range(TILES):
                    ins = mm(bank(b, 0)[:, t * 2 * D + D:(t + 1) * 2 * D], ones32[:, :], kdiag[:, b], False, True)
                ins.then_inc(sig["kshift"], 1)
            pe.wait_ge(sig["absum"], 3)
            pe.wait_ge(sig["wgsq"], 1)
            mm(bank(3, 1)[:, T + NE:T + 2 * NE], c("wredT", NG), c("wgT", NG), True, True)
            mm(bank(3, 1)[:, T + 2 * NE:T + 3 * NE], ones32[0:NG, :], wgsq[:, :], True, True)
            mm(bank(3, 1)[:, T:T + 3], ones32[:, :], absum[:, :], True, True).then_inc(sig["means_ready"], 1)
            pe.wait_ge(sig["ewT_ready"], 1)
            for b in range(B):
                pe.wait_ge(sig["eb_lo"], b + 1)
                for t in range(TILES):
                    tok = slice(t * P, (t + 1) * P)
                    for j in range(TILES):
                        ins = product(bank(b, 0)[:, t * 2 * D:(t + 1) * 2 * D], lambda i: ewT[:, i, j, tok],
                                      lambda k: eb16[:, k, b, j], start=j == 0, stop=j == TILES - 1)
                ins.then_inc(sig["numden"], 1)
            for b in range(B):
                pe.wait_ge(sig["y"], b + 1)
                for t in range(TILES):
                    ins = transposed(bank(b, 1)[:, t * P:(t + 1) * P], y[:, b, t])
                ins.then_inc(sig["turned"], 1)
            pe.wait_ge(sig["bias_rest"], 1)
            pe.wait_ge(sig["w_lo"], 2)
            pe.wait_ge(sig["id_ready"], 1)
            for b in range(B):
                pe.wait_ge(sig["cols_ready"], nth(C_Y, b))
                for t in range(TILES):
                    tok = slice(t * P, (t + 1) * P)
                    dst = bank(b, 0)[:, t * D:(t + 1) * D]
                    product(dst, lambda i: colsY[:, i, b, tok], lambda j: w("wo", j), stop=False)
                    mm(dst, colsA[:, 0, b, tok], id16[:, :], False, False)
                    mm(dst, colsA[:, 1, b, tok], id16[:, :], False, False)
                    ins = row_bias(dst, "bo")
                ins.then_inc(sig["attn_mm"], 1)
            for b in range(B):
                pe.wait_ge(sig["rows_ready"], nth(R_A, b))
                for t in range(TILES):
                    ins = transposed(bank(b, 1)[:, t * P:(t + 1) * P], rows[:, b, t])
                ins.then_inc(sig["turned"], 1)
            pe.wait_ge(sig["w_lo_pool"], 1)
            for b in range(B):
                pe.wait_ge(sig["cols_ready"], nth(C_A, b))
                for k in range(HC):
                    dst = bank(b, k // 2)[:, (k % 2) * T:(k % 2 + 1) * T]
                    product(dst, lambda i: w("w1", i)[:, k * P:(k + 1) * P], lambda j: colsN[:, j, b], stop=False)
                    ins = mm(dst, brow("b1")[:, k * P:(k + 1) * P], ones16[0:2, :], False, True)
                ins.then_inc(sig["hid_mm"], 1)
            pe.wait_ge(sig["w_lo_pool"], 2)
            for b in range(B):
                pe.wait_ge(sig["hid_ready"], b + 1)
                for t in range(TILES):
                    tok = slice(t * P, (t + 1) * P)
                    dst = bank(b, 0)[:, t * D:(t + 1) * D]
                    for k in range(HC):
                        product(dst, lambda i: hid16[:, i, b, k, tok], lambda j: w("w2", j)[:, k * D:(k + 1) * D],
                                start=k == 0, stop=False)
                    mm(dst, colsN[:, 0, b, tok], id16[:, :], False, False)
                    mm(dst, colsN[:, 1, b, tok], id16[:, :], False, False)
                    ins = row_bias(dst, "b2")
                ins.then_inc(sig["ff_mm"], 1)
                if b == 1:
                    pe.wait_ge(sig["mask_ind"], 1)
                    for a in range(B):
                        for t in range(TILES):
                            ins = mm(bank(a // 2, 1)[:, (a % 2) * T:(a % 2 + 1) * T], ones16[:, 0:P], ind[:, a, t], t == 0,
                                     t == TILES - 1)
                    ins.then_inc(sig["count_mm"], 1)

            def keys(b, half_no):
                for i in range(2):
                    k = 2 * half_no + i
                    dst = bank(b, 1)[:, i * T:(i + 1) * T]
                    product(dst, lambda i: w("wk", i)[:, k * P:(k + 1) * P], lambda j: ctxT[:, j, b], stop=False)
                    mm(dst, brow("bk")[:, k * P:(k + 1) * P], ones16[0:2, :], False, False)
                    ins = mm(dst, sel16[:, :], colrow[:, b], False, True)
                ins.then_inc(sig["kproj"], 1)

            pe.wait_ge(sig["ctxT_ready"], 1)
            pe.wait_ge(sig["w_lo_pool"], 4)
            pe.wait_ge(sig["colmask"], 1)
            for b in range(B):
                for t in range(TILES):
                    tok = slice(t * P, (t + 1) * P)
                    dst = bank(b, 1)[:, t * D:(t + 1) * D]
                    product(dst, lambda i: ctxT[:, i, b, tok], lambda j: w("wv", j), stop=False)
                    ins = row_bias(dst, "bv")
                ins.then_inc(sig["vproj"], 1)
            for b in range(B):
                pe.wait_ge(sig["va_ready"], b + 1)
                keys(b, 0)
            for b in range(B):
                pe.wait_ge(sig["q1"], b + 1)
                for t in range(TILES):
                    ins = transposed(bank(b, 0)[:, t * P:(t + 1) * P], rows[:, b, t])
                ins.then_inc(sig["turned"], 1)
            pe.wait_ge(sig["ffw_ready"], 1)
            for u, (b, t) in enumerate(GU_ORDER):
                tok = slice(t * P, (t + 1) * P)
                if t:
                    pe.wait_ge(sig["g"], u - 1)
                else:
                    pe.wait_ge(sig["q1T_ready"], b + 1)
                    pe.wait_ge(sig["ka_ready"], b + 1)
                mm(bank(b, 0), qT[:, b, tok], ffw16[:, 0], True, True)
                mm(bank(b, 1), qT[:, b, tok], ffw16[:, 1], True, True).then_inc(sig["gu_mm"], 1)
            for b in range(B):
                pe.wait_ge(sig["q2"], b + 1)
                pe.wait_ge(sig["q2_act"], b + 1)
                for t in range(TILES):
                    for k in range(HC):
                        ins = transposed(bank(b, t)[:, k * P:(k + 1) * P], g[:, b, t, k * P:(k + 1) * P])
                ins.then_inc(sig["q2T_mm"], 1)
            for b in range(B):
                pe.wait_ge(sig["q2T_ready"], b + 1)
                for t in range(TILES):
                    for k in range(HC):
                        ins = mm(bank(b, 0)[:, t * D:(t + 1) * D], gT[:, b, t, k], ffw16[:, 2, k * D:(k + 1) * D],
                                 k == 0, k == HC - 1)
                ins.then_inc(sig["down_mm"], 1)
            for b in range(B):
                keys(b, 1)
            for b in range(B):
                pe.wait_ge(sig["rows_ready"], nth(R_ATT, b))
                for t in range(TILES):
                    ins = transposed(bank(b, 0)[:, t * P:(t + 1) * P], rows[:, b, t])
                ins.then_inc(sig["turned"], 1)
            pe.wait_ge(sig["w_lo_pool"], 5)
            pe.wait_ge(sig["zeros_ready"], 2)

            def queries(b):
                pe.wait_ge(sig["cols_ready"], nth(C_QUERY, b))
                for k in range(QUADS):
                    dst = bank(b, k // 2)[:, (k % 2) * T:(k % 2 + 1) * T]
                    product(dst, lambda i: w("wq", i)[:, k * P:(k + 1) * P], lambda j: colsA[:, j, b], stop=False)
                    ins = mm(dst, brow("bq")[:, k * P:(k + 1) * P], ones16[0:2, :], False, True)
                ins.then_inc(sig["q_mm"], 1)

            def scores(n, i, masked):
                b, quad = divmod(n, QUADS)
                t, pair_of = divmod(i, 2)
                if n == 0 and i == 0:
                    pe.wait_ge(sig["qa_ready"], 1)
                if i == 0:
                    pe.wait_ge(sig["kz_ready"], n + 1)
                if 4 * n + i >= 2:
                    pe.wait_ge(sig["smax"], 4 * n + i - 1)
                dst = score_bank(4 * n + i)
                ins = mm(dst, qa[:, b, quad, t * P:(t + 1) * P],
                         kz[:, n % KRING, 2 * pair_of:2 * pair_of + 2].rearrange("p h n -> p (h n)"), True, not masked)
                if masked:
                    for h in range(2):
                        ins = mm(dst[:, h * T:(h + 1) * T], idbig[:, :], resmask[:, b, t], False, h == 1)
                ins.then_inc(sig["s_mm"], 1)

            def shift(n):
                pe.wait_ge(sig["spread"], n + 1)
                if n >= 1:
                    pe.wait_ge(sig["qb"], n)
                b, quad = divmod(n, QUADS)
                for t in range(TILES):
                    mm(ps[:, 6, t * P:(t + 1) * P], spread[:, n % 2, t], id16[:, :], t == 0, False)
                mm(ps[:, 6, 0:T], id16[:, :], qa[:, b, quad], False, True).then_inc(sig["shift_mm"], 1)

            def shifted_scores(n, k, masked):
                b, quad = divmod(n, QUADS)
                head = 4 * n + k
                if k == 0:
                    pe.wait_ge(sig["qb"], n + 1)
                if head >= 2:
                    pe.wait_ge(sig["probs"], head - 1)
                for t in range(TILES):
                    tok = slice(t * P, (t + 1) * P)
                    dst = ps[:, 2 + head % 2, t * T:(t + 1) * T]
                    ins = mm(dst, kz[:, n % KRING, k, tok], qb[:, n % 2], True, not masked)
                    if masked:
                        for q in range(TILES):
                            ins = mm(ps[:, 2 + head % 2, t * T + q * P:t * T + (q + 1) * P],
                                     resmask[:, b, q, tok], idbig[:, :], False, q == TILES - 1)
                ins.then_inc(sig["st_mm"], 1)

            def weighted_values(n, t):
                b, quad = divmod(n, QUADS)
                m = n // 2
                if t == 0:
                    pe.wait_ge(sig["probs"], 4 * n + 4)
                    if m >= 2 and n % 2 == 0:
                        pe.wait_ge(sig["oT"], m - 1)
                for k in range(4):
                    ins = mm(ps[32 * k:32 * k + 32, 4 + m % 2, (n % 2) * T:(n % 2 + 1) * T],
                             va[:, b, t, 4 * quad + k], pt[:, (4 * n + k) % PRING, t], t == 0, t == TILES - 1)
                if t == TILES - 1:
                    ins.then_inc(sig["pv"], 1)

            def tail_step(b, step):
                tb = tail_bank(b)
                if step < TILES:
                    pe.wait_ge(sig["oT"], 2 * b + 2)
                    if step == 0 and 1 <= b < B - 1:
                        pe.wait_ge(sig["ohT"], b)
                    if step == 0 and b == B - 1:
                        pe.wait_ge(sig["qb"], B * QUADS)
                    if step:
                        pe.wait_ge(sig["attn"], TILES * b + step)
                    for k in range(QUADS):
                        ins = transposed(tb[:, k * P:(k + 1) * P], oT[:, b, k, step * P:(step + 1) * P])
                    ins.then_inc(sig["oR_mm"], 1)
                if step == 2:
                    pe.wait_ge(sig["attn"], TILES * (b + 1))
                    for t in range(TILES):
                        ins = transposed(tb[:, t * P:(t + 1) * P], attn[:, b, t])
                    ins.then_inc(sig["turned"], 1)
                if step == 3:
                    pe.wait_ge(sig["w_lo_pool"], 6)
                    pe.wait_ge(sig["cols_ready"], nth_of_tail(C_TAIL, b, False))
                    for t in range(TILES):
                        tok = slice(t * P, (t + 1) * P)
                        dst = tb[:, t * D:(t + 1) * D]
                        product(dst, lambda i: colsY[:, i, b, tok], lambda j: w("wo1", j), stop=False)
                        ins = row_bias(dst, "bo1")
                    ins.then_inc(sig["wo1_mm"], 1)
                if step == 4:
                    pe.wait_ge(sig["rows_act"], nth(NMR_TURN[LN_MOE], b))
                    for t in range(TILES):
                        ins = transposed(tb[:, t * P:(t + 1) * P], rows[:, b, t])
                    ins.then_inc(sig["turned"], 1)
                if step == 5:
                    pe.wait_ge(sig["router_ready"], 1)
                    pe.wait_ge(sig["cols_ready"], nth_of_tail(C_TAIL, b, True))
                    for t in range(TILES):
                        tok = slice(t * P, (t + 1) * P)
                        ins = product(tb[:, t * NE:(t + 1) * NE], lambda i: colsN[:, i, b, tok], lambda j: router16[:, j])
                    ins.then_inc(sig["logit_mm"], 1)
                if step == 6:
                    pe.wait_ge(sig["onehot"], b + 1)
                    for t in range(TILES):
                        ins = mm(tb[0:2 * NE, t * P:(t + 1) * P], onehot[:, b, t], id16[:, :], True, True)
                    ins.then_inc(sig["ohT_mm"], 1)

            def onehot_columns(b, half):
                pair_of = ONEHOT_PAIRS[b]
                pe.wait_ge(sig["onehot"], b + 1)
                if half or b == 1:
                    pe.wait_ge(sig["oh"], 2 * b + half)
                elif b == 0:
                    pe.wait_ge(sig["smax"], 4 * B * QUADS)
                elif b == 2:
                    pe.wait_ge(sig["oT"], 2 * B)
                else:
                    pe.wait_ge(sig["ohT"], B)
                for e in range(4):
                    for t in range(TILES):
                        ins = mm(bank(pair_of, e // 2)[:, (e % 2) * T + t * P:(e % 2) * T + (t + 1) * P],
                                 onehot[:, b, t, 4 * half + e:4 * half + e + 1].to_broadcast([P, P]),
                                 id16[:, :], True, True)
                ins.then_inc(sig["oh_mm"], 1)

            def attention(masked):
                for b in range(2):
                    queries(b)
                for k in range(4):
                    scores(0, k, masked)
                    if k < 2:
                        queries(2 + k)
                for k in range(4):
                    scores(1, k, masked)
                    if k == 1:
                        pe.wait_ge(sig["qa_ready"], B)
                        shift(0)
                for n in range(B * QUADS):
                    for k in range(4):
                        shifted_scores(n, k, masked)
                        if n + 2 < B * QUADS:
                            scores(n + 2, k, masked)
                        if k == 1 and n + 1 < B * QUADS:
                            shift(n + 1)
                        if tail_at(n, k):
                            tail_step(*tail_at(n, k))
                        if (n, k) in ONEHOT_AT:
                            onehot_columns(*ONEHOT_AT[n, k])
                        if k < TILES and n >= 1:
                            weighted_values(n - 1, k)
                for t in range(TILES):
                    weighted_values(B * QUADS - 1, t)

            pe.wait_ge(sig["flag_ready"], 1)
            pe.wait_ge(sig["resmask"], 2)
            general = pe.value_load(flag_i[0:1, 0:1], min_val=0, max_val=B * T * T)
            with pe.If(general > 0):
                attention(True)
            with pe.Else():
                attention(False)

            def hidden(b, k):
                pe.wait_ge(sig["xm"], b + 1)
                if k == 0:
                    if b == 0:
                        pe.wait_ge(sig["oh"], 4)
                    if b == 1:
                        pe.wait_ge(sig["probs"], 4 * B * QUADS)
                    for t in range(TILES):
                        mm(bank(b, 1)[:, t * D:(t + 1) * D], ohT[:, b, t * P:(t + 1) * P], mbias16[:, EH:EH + D], True, True)
                dst = bank(b, 0)[:, k * T:(k + 1) * T]
                for e in range(NE):
                    product(dst, lambda i: w("m1", i)[:, e * EH + k * P:e * EH + (k + 1) * P],
                            lambda j: xm[b % 2][:, j, e], start=e == 0, stop=False)
                ins = mm(dst, mbias16[:, k * P:(k + 1) * P], ohT[:, b], False, True)
                if k == EC - 1:
                    ins.then_inc(sig["moe_h"], 1)

            def outputs(u):
                b, t = divmod(u, TILES)
                tok = slice(t * P, (t + 1) * P)
                pair_of = OUT_PAIRS[u]
                pe.wait_ge(sig["gelu_ready"], max(b, pair_of) + 1)
                pe.wait_ge(sig["y0"], max(b, pair_of) + 1)
                if pair_of in OUT_PAIRS[:u]:
                    pe.wait_ge(sig["picked"], u - OUT_PAIRS[:u][::-1].index(pair_of))
                for half in range(2):
                    for k in range(EC):
                        col = k * NE * D + half * 4 * D
                        ins = product(bank(pair_of, half), lambda i: gelu16[:, i, b, k, tok],
                                      lambda j: w("m2", j)[:, col:col + 4 * D], start=k == 0, stop=k == EC - 1)
                ins.then_inc(sig["moe_o"], 1)

            tail_step(2, 4)
            pe.wait_ge(sig["w_lo_pool"], 7)
            pe.wait_ge(sig["mbias_ready"], 1)
            pe.wait_ge(sig["ohT"], 1)
            tail_step(3, 0)
            hidden(0, 0)
            tail_step(2, 5)
            tail_step(3, 1)
            hidden(0, 1)
            tail_step(2, 6)
            tail_step(3, 2)
            onehot_columns(2, 0)
            hidden(1, 0)
            tail_step(3, 3)
            onehot_columns(2, 1)
            hidden(1, 1)
            pe.wait_ge(sig["w_lo_pool"], 8)
            tail_step(3, 4)
            outputs(0)
            tail_step(3, 5)
            hidden(2, 0)
            tail_step(3, 6)
            onehot_columns(3, 0)
            hidden(2, 1)
            onehot_columns(3, 1)
            outputs(1)
            outputs(2)
            hidden(3, 0)
            hidden(3, 1)
            for u in range(3, B * TILES):
                outputs(u)


def kernel(x, ctx_1024, mask_BxSxS2_ik1, L0_xattn_wq, L0_xattn_bq, L0_xattn_wk, L0_xattn_bk, L0_xattn_wv, L0_xattn_bv,
           L0_xattn_wo, L0_xattn_bo, L0_xattn_pos_bias, L0_xattn_gamma, L0_xattn_beta, L0_xattn_w1, L0_xattn_b1,
           L0_xattn_w2, L0_xattn_b2, L0_ffn_w_gate, L0_ffn_w_up, L0_ffn_w_down, L1_xattn_Wq, L1_xattn_bq, L1_xattn_Wk,
           L1_xattn_bk, L1_xattn_Wv, L1_xattn_bv, L1_xattn_Wo, L1_xattn_bo, L1_ffn_w_red, L1_ffn_wg, L1_ffn_W1,
           L1_ffn_b1, L1_ffn_W2, L1_ffn_b2):
    import concourse.bacc as bacc
    from concourse.bass_utils import run_bass_kernel_spmd

    def heads32(m):
        m = m.reshape(m.shape[0], QUADS, 4, 1, DK)
        wide = np.zeros((m.shape[0], QUADS, 4, 4, DK), np.float32)
        wide[:, :, :, 0:3] = m
        return wide.reshape(m.shape[0], QUADS * P)

    x_rows = np.ascontiguousarray(np.asarray(x).reshape(B, TILES, P, D).transpose(0, 2, 1, 3))
    ctx = np.asarray(ctx_1024)
    ctx_rows = np.ascontiguousarray(ctx.reshape(B, TILES, P, D).transpose(2, 0, 1, 3))
    ctx_cols = np.ascontiguousarray(ctx.transpose(2, 0, 1))
    mask = np.ascontiguousarray(np.asarray(mask_BxSxS2_ik1).reshape(B, TILES, P, T).transpose(2, 0, 1, 3))
    pos = np.ascontiguousarray(np.asarray(L0_xattn_pos_bias).reshape(TILES, P, T).transpose(1, 0, 2))

    consts = np.zeros((P, NC_), np.float32)
    row = np.arange(P)
    consts[:, CSEG["ident"][0]:CSEG["ident"][1]] = np.eye(P)
    consts[:, CSEG["iota"][0]:CSEG["iota"][1]] = np.tile(np.arange(NE), 2)
    consts[:, CSEG["lo_q"][0]] = np.where((row % 32) // DK == 2, -1.0, 0.0)
    consts[:, CSEG["lo_k"][0]] = np.where((row % 32) // DK == 1, -1.0, 0.0)
    consts[:, CSEG["lo_2"][0]] = np.where(row == 1, -1.0, 0.0)
    consts[:, CSEG["lo_16"][0]] = np.where((row >= NE) & (row < 2 * NE), -1.0, 0.0)
    consts[0, CSEG["sel"][0]:CSEG["sel"][1]] = (row % 32 >= 24) & (row % 32 < 28)
    i, j = np.arange(T).reshape(TILES, P).T[:, :, None], np.arange(T)[None, None, :]
    consts[:, CSEG["band"][0]:CSEG["band"][1]] = (np.abs(i - j) < WINDOW).reshape(P, TILES * T)
    consts[:, CSEG["cols"][0]:CSEG["cols"][1]] = np.stack([np.asarray(L0_xattn_bk), np.asarray(L0_xattn_gamma), np.asarray(L0_xattn_beta)], 1)
    consts[0:NG, CSEG["wredT"][0]:CSEG["wredT"][1]] = np.asarray(L1_ffn_w_red).T
    consts[0:NG, CSEG["wgT"][0]:CSEG["wgT"][1]] = np.asarray(L1_ffn_wg).T

    def mask_rows(m, rows, value):
        m = m.reshape(1, QUADS, 4, 32).copy()
        m[:, :, :, rows] = value
        return m.reshape(1, QUADS * P)

    bias = np.concatenate([
        np.asarray(L0_xattn_bq)[None], np.asarray(L0_xattn_bk)[None], np.asarray(L0_xattn_bv)[None],
        np.asarray(L0_xattn_bo)[None], np.asarray(L0_xattn_b1)[None], np.asarray(L0_xattn_b2)[None],
        mask_rows(heads32(np.asarray(L1_xattn_bq)[None]), slice(24, 28), -BIG),
        mask_rows(heads32(np.asarray(L1_xattn_bk)[None]), slice(28, 32), BIG),
        np.asarray(L1_xattn_bv)[None], np.asarray(L1_xattn_bo)[None]], 1)
    bias = np.ascontiguousarray(np.repeat(bias, 2, 0))
    mb = np.concatenate([np.asarray(L1_ffn_b1), np.asarray(L1_ffn_b2)], 1)
    mbias = np.ascontiguousarray(np.concatenate([mb, mb], 0))
    ffw = np.ascontiguousarray(np.stack([
        np.asarray(L0_ffn_w_gate).T, np.asarray(L0_ffn_w_up).T,
        np.asarray(L0_ffn_w_down).T.reshape(HC, P, D).transpose(1, 0, 2).reshape(P, HC * D)], 1))
    weights = np.ascontiguousarray(np.concatenate([
        np.asarray(L0_xattn_wq), np.asarray(L0_xattn_wk), np.asarray(L0_xattn_wv), np.asarray(L0_xattn_wo),
        np.asarray(L0_xattn_w1), np.asarray(L0_xattn_w2).reshape(HC, P, D).transpose(1, 0, 2).reshape(P, HC * D),
        heads32(np.asarray(L1_xattn_Wk)), np.asarray(L1_xattn_Wv), heads32(np.asarray(L1_xattn_Wq)), np.asarray(L1_xattn_Wo),
        np.asarray(L1_ffn_W1).transpose(1, 0, 2).reshape(P, NE * EH),
        np.asarray(L1_ffn_W2).reshape(NE, EC, P, D).transpose(2, 1, 0, 3).reshape(P, EC * NE * D)], 1))

    arrays = {"x": x_rows, "ctx_rows": ctx_rows, "ctx_cols": ctx_cols, "mask": mask, "consts": consts, "pos": pos,
              "gamma": np.ascontiguousarray(np.asarray(L0_xattn_gamma)),
              "beta": np.ascontiguousarray(np.asarray(L0_xattn_beta)),
              "bias": bias, "mbias": mbias, "ffw": ffw, "weights": weights}
    nc = bacc.Bacc("TRN2", target_bir_lowering=False, num_devices=1)
    args = [nc.dram_tensor(f"{n}_dram", a.shape, mybir.dt.from_np(a.dtype), kind="ExternalInput").ap()
            for n, a in arrays.items()]
    out = nc.dram_tensor("out_dram", (B, P, TILES, D), F32, kind="ExternalOutput").ap()
    build_program(nc, *args, out)
    r = run_bass_kernel_spmd(nc, [{f"{n}_dram": a for n, a in arrays.items()}], core_ids=[0])
    got = r.results[0]["out_dram"]
    return np.ascontiguousarray(got.transpose(0, 2, 1, 3).reshape(B, T, D))
```
